# Optimizing a Trainium2 kernel written in Bass

```python
import numpy as np
import jax
import jax.numpy as jnp

def _softmax(x, axis=-1):
    return jax.nn.softmax(x, axis=axis)

def _gelu(x):
    return jax.nn.gelu(x, approximate=True)

def _silu(x):
    return jax.nn.silu(x)

def _sigmoid(x):
    return jax.nn.sigmoid(x)

def _layernorm(x, axis=-1, eps=1e-05):
    m = jnp.mean(x, axis=axis, keepdims=True)
    v = jnp.var(x, axis=axis, keepdims=True)
    return (x - m) / jnp.sqrt(v + eps)

def _scatter_add(tgt, idx, src, axis=0):
    return tgt.at[idx].add(src)

def _segment_sum(src, seg, n):
    return jax.ops.segment_sum(src, seg, n)
kernel_name = 'mk_gps_d1_gnn_r8_4e9f4b'

def setup_inputs(seed: int=0):
    np.random.seed(seed)
    _w = jnp.asarray

    def _rec_inputs():
        import jax
        import jax.numpy as jnp
        _gk = jax.random.key(seed)
        x = -0.0003713 + 1 * jax.random.normal(jax.random.fold_in(_gk, 1), (6250, 256), jnp.float32)
        src = jax.random.randint(jax.random.fold_in(_gk, 2), (100000,), 0, 6250, jnp.int32)
        dst = jnp.minimum((6250 * jax.random.uniform(jax.random.fold_in(_gk, 3), (100000,)) ** 2.0).astype(jnp.int32), 49999)
        _o = jnp.argsort(dst, stable=True)
        src = src[_o]
        dst = dst[_o]
        edge_attr_64 = -9.77346e-05 + 0.999888 * jax.random.normal(jax.random.fold_in(_gk, 12), (100000, 64), jnp.float32)
        return (x, src, dst, edge_attr_64)
    x, src, dst, edge_attr_64 = _rec_inputs()

    def _L0_gnn_setup():
        import jax, jax.numpy as jnp
        import numpy as np
        ALPHA = 0.2
        key = jax.random.key(seed)
        ks = jax.random.split(key, 6)
        N, E, F_IN, F_OUT, E_DIM = (6250, 100000, 256, 256, 64)
        h = jax.random.normal(ks[0], (N, F_IN), dtype=jnp.float32)
        e_feat = jax.random.normal(ks[1], (E, E_DIM), dtype=jnp.float32)
        W = jax.random.normal(ks[2], (F_OUT, F_IN), dtype=jnp.float32) * (1.0 / np.sqrt(F_IN))
        A = jax.random.normal(ks[3], (1, 2 * F_OUT + E_DIM), dtype=jnp.float32) * 0.05
        src = jax.random.randint(ks[4], (E,), 0, N, dtype=jnp.int32)
        dst = jax.random.randint(ks[5], (E,), 0, N, dtype=jnp.int32)
        return {'h': h, 'e_feat': e_feat, 'W': W, 'A': A, 'src': src, 'dst': dst}
    _L0_gnn_all = _L0_gnn_setup()
    _L0_gnn_in = {k: v for k, v in _L0_gnn_all.items() if k in ('W', 'A')}
    del _L0_gnn_all

    def _L0_mix_setup():
        import jax, jax.numpy as jnp
        import numpy as np
        HEADS = 8
        EPS = 1e-05

        def _ln(t, w, b, headc):
            m = jnp.mean(t, axis=-1, keepdims=True)
            d = t - m
            std = jnp.sqrt(jnp.sum(d * d, axis=-1, keepdims=True) / (headc - 1))
            return w * (d / (std + EPS)) + b
        key = jax.random.key(seed)
        B, N, C = (32, 512, 256)
        headc = C // HEADS
        x = jax.random.normal(key, (B, N, C), dtype=jnp.float32)
        return {'x': x, 'kln_weight': jnp.ones((HEADS, 1, headc), dtype=jnp.float32), 'kln_bias': jnp.zeros((HEADS, 1, headc), dtype=jnp.float32), 'vln_weight': jnp.ones((HEADS, 1, headc), dtype=jnp.float32), 'vln_bias': jnp.zeros((HEADS, 1, headc), dtype=jnp.float32)}
    _L0_mix_all = _L0_mix_setup()
    _L0_mix_in = {k: v for k, v in _L0_mix_all.items() if k in ('kln_weight', 'kln_bias', 'vln_weight', 'vln_bias')}
    del _L0_mix_all

    def _L0_ffn_setup():
        import jax, jax.numpy as jnp
        import numpy as np
        B, S, H, F, E, K = (8, 512, 256, 512, 16, 2)
        EPS = 1e-05
        key = jax.random.key(seed)
        ks = jax.random.split(key, 9)
        sc = 0.02
        return {'x': jax.random.normal(ks[0], (B, S, H), dtype=jnp.float32), 'gate_w': jax.random.normal(ks[1], (H, E), dtype=jnp.float32) * sc, 'gate_b': jnp.zeros((E,), dtype=jnp.float32), 'w1': jax.random.normal(ks[2], (E, H, F), dtype=jnp.float32) * sc, 'b1': jnp.zeros((E, F), dtype=jnp.float32), 'w2': jax.random.normal(ks[3], (E, F, H), dtype=jnp.float32) * sc, 'b2': jnp.zeros((E, H), dtype=jnp.float32), 'gamma': jnp.ones((H,), dtype=jnp.float32), 'beta': jnp.zeros((H,), dtype=jnp.float32)}
    _L0_ffn_all = _L0_ffn_setup()
    _L0_ffn_in = {k: v for k, v in _L0_ffn_all.items() if k in ('gate_w', 'gate_b', 'w1', 'b1', 'w2', 'b2', 'gamma', 'beta')}
    del _L0_ffn_all
    return {'x': x, 'src': src, 'dst': dst, 'edge_attr_64': edge_attr_64, 'L0_gnn_W': _L0_gnn_in['W'], 'L0_gnn_A': _L0_gnn_in['A'], 'L0_mix_kln_weight': _L0_mix_in['kln_weight'], 'L0_mix_kln_bias': _L0_mix_in['kln_bias'], 'L0_mix_vln_weight': _L0_mix_in['vln_weight'], 'L0_mix_vln_bias': _L0_mix_in['vln_bias'], 'L0_ffn_gate_w': _L0_ffn_in['gate_w'], 'L0_ffn_gate_b': _L0_ffn_in['gate_b'], 'L0_ffn_w1': _L0_ffn_in['w1'], 'L0_ffn_b1': _L0_ffn_in['b1'], 'L0_ffn_w2': _L0_ffn_in['w2'], 'L0_ffn_b2': _L0_ffn_in['b2'], 'L0_ffn_gamma': _L0_ffn_in['gamma'], 'L0_ffn_beta': _L0_ffn_in['beta']}

def reference(x, src, dst, edge_attr_64, L0_gnn_W, L0_gnn_A, L0_mix_kln_weight, L0_mix_kln_bias, L0_mix_vln_weight, L0_mix_vln_bias, L0_ffn_gate_w, L0_ffn_gate_b, L0_ffn_w1, L0_ffn_b1, L0_ffn_w2, L0_ffn_b2, L0_ffn_gamma, L0_ffn_beta):
    import jax
    import jax.numpy as jnp

    def _L0_gnn_ref(h, e_feat, W, A, src, dst):
        import jax, jax.numpy as jnp
        import numpy as np
        ALPHA = 0.2
        N = h.shape[0]
        F_OUT = W.shape[0]
        z = h @ W.T
        z_src = z[src]
        z_dst = z[dst]
        a_src, a_dst, a_e = (A[0, :F_OUT], A[0, F_OUT:2 * F_OUT], A[0, 2 * F_OUT:])
        logits = z_src @ a_src + z_dst @ a_dst + e_feat @ a_e
        e = jax.nn.leaky_relu(logits, ALPHA)
        m = jax.ops.segment_max(e, dst, num_segments=N)
        ex = jnp.exp(e - m[dst])
        denom = jax.ops.segment_sum(ex, dst, num_segments=N)
        alpha = ex / denom[dst]
        h_out = jax.ops.segment_sum(alpha[:, None] * z_src, dst, num_segments=N)
        return h_out

    def _L0_mix_ref(x, kln_weight, kln_bias, vln_weight, vln_bias):
        import jax, jax.numpy as jnp
        import numpy as np
        HEADS = 8
        EPS = 1e-05

        def _ln(t, w, b, headc):
            m = jnp.mean(t, axis=-1, keepdims=True)
            d = t - m
            std = jnp.sqrt(jnp.sum(d * d, axis=-1, keepdims=True) / (headc - 1))
            return w * (d / (std + EPS)) + b
        B, N, C = x.shape
        headc = C // HEADS
        qkv = x.reshape(B, N, HEADS, headc).transpose(0, 2, 1, 3)
        k = _ln(qkv, kln_weight, kln_bias, headc)
        v = _ln(qkv, vln_weight, vln_bias, headc)
        kv = jnp.einsum('bhnd,bhne->bhde', k, v) / N
        out = jnp.einsum('bhnd,bhde->bhne', qkv, kv)
        out = out.transpose(0, 2, 1, 3).reshape(B, N, C)
        return out + x

    def _L0_ffn_ref(x, gate_w, gate_b, w1, b1, w2, b2, gamma, beta):
        import jax, jax.numpy as jnp
        import numpy as np
        B, S, H, F, E, K = (8, 512, 256, 512, 16, 2)
        EPS = 1e-05
        gate_logits = x @ gate_w + gate_b
        topk_vals, topk_idx = jax.lax.top_k(gate_logits, K)
        topk_w = jax.nn.softmax(topk_vals, axis=-1)
        h = jax.nn.relu(jnp.einsum('bsh,ehf->bsef', x, w1) + b1)
        expert_out = jnp.einsum('bsef,efh->bseh', h, w2) + b2
        sel = jnp.take_along_axis(expert_out, topk_idx[:, :, :, None], axis=2)
        moe = jnp.sum(topk_w[..., None] * sel, axis=2)
        y = x + moe
        mu = jnp.mean(y, axis=-1, keepdims=True)
        var = jnp.var(y, axis=-1, keepdims=True)
        return (y - mu) / jnp.sqrt(var + EPS) * gamma + beta
    xn = _layernorm(x, axis=-1)
    x = x + _L0_gnn_ref(xn, edge_attr_64, L0_gnn_W, L0_gnn_A, src, dst) + _L0_mix_ref(xn[None], L0_mix_kln_weight, L0_mix_kln_bias, L0_mix_vln_weight, L0_mix_vln_bias)[0]
    x = x + _L0_ffn_ref(_layernorm(x, axis=-1)[None], L0_ffn_gate_w, L0_ffn_gate_b, L0_ffn_w1, L0_ffn_b1, L0_ffn_w2, L0_ffn_b2, L0_ffn_gamma, L0_ffn_beta)[0]
    return x

_drawn_inputs = setup_inputs


def setup_inputs(seed=0):
    import zlib

    import numpy as np

    out = dict(_drawn_inputs(seed))
    spreads = {'L0_mix_kln_weight': (1.0, 0.2),
     'L0_mix_kln_bias': (0.0, 0.465),
     'L0_mix_vln_weight': (1.0, 0.2),
     'L0_mix_vln_bias': (0.0, 0.464),
     'L0_ffn_gate_b': (0.0, 0.458),
     'L0_ffn_b1': (0.0, 0.8),
     'L0_ffn_b2': (0.0, 0.436),
     'L0_ffn_gamma': (1.0, 0.2),
     'L0_ffn_beta': (0.0, 0.325)}
    factors = {'L0_ffn_w1': 3.664, 'L0_ffn_w2': 2.925}
    for name, (base, spread) in spreads.items():
        noise = np.random.default_rng([zlib.crc32(name.encode()), seed]).standard_normal(out[name].shape)
        drawn = base * np.exp(spread * noise) if base else spread * noise
        out[name] = jnp.asarray(drawn.astype(out[name].dtype))
    for name, factor in factors.items():
        out[name] = (out[name] * factor).astype(out[name].dtype)
    return out
```

```python
from contextlib import ExitStack

import concourse.bass as bass
from concourse import mybir

F32 = mybir.dt.float32
BF16 = mybir.dt.bfloat16
I32 = mybir.dt.int32
ALU = mybir.AluOpType
ACT = mybir.ActivationFunctionType
AX_X = mybir.AxisListType.X
DVE = mybir.EngineType.DVE
ds = bass.ds

P = 128
N, D, E, ED = 6250, 256, 100000, 64
HEADS, HC = 8, 32
NX, FF = 16, 512
DC, FC = D // P, FF // P
NT = 50
NP = NT * P
ET = 784
EP = ET * P
RG = 7
RP = ET // RG
TC = 8
GU = 16
XB = 256
N_TURNS = (2 * N + NX * (XB - 1)) // XB + 1
ZERO_DMAS = 13
LN_EPS = 1e-5
HEAD_EPS = 1e-5
SLOPE = 0.2
BIG = 1e30


class Link:

    def __init__(self, engine, semaphore, start=0):
        self.engine, self.semaphore, self.start = engine, semaphore, start
        self.count, self.turn, self.per = 0, None, 0

    def loop(self, turn, per):
        self.start += self.count
        self.turn, self.per, self.count = turn, per, 0

    def end_loop(self, turns):
        assert self.count == self.per, (self.count, self.per)
        self.start += turns * self.per
        self.turn, self.count = None, 0

    def __call__(self, ins):
        self.count += 1
        ins.then_inc(self.semaphore, 1)
        at = self.start + self.count
        if self.turn is not None:
            at = self.turn * self.per + at
        self.engine.wait_ge(self.semaphore, at)


def prime(engine, s, semaphore):
    cell = s.prime[0:1, s.primed:s.primed + 1]
    s.primed += 1
    engine.dma_start(cell, s.gate_b[0:1].rearrange("(a b) -> a b", a=1)).then_inc(semaphore, 16)


def tiled(ap):
    return ap.rearrange("(t p) d -> t p d", p=P)


class Store:
    pass


def build(nc, x, src, dst, edge_attr, W, A, kw, kb, vw, vb, gate_w, gate_b, w1, b1, w2, b2, gamma, beta, out):
    s = Store()
    s.nc = nc
    s.x, s.src, s.dst, s.edge_attr, s.W, s.A = x, src, dst, edge_attr, W, A
    s.kw, s.kb, s.vw, s.vb = kw, kb, vw, vb
    s.gate_w, s.gate_b, s.w1, s.b1, s.w2, s.b2, s.gamma, s.beta, s.out = gate_w, gate_b, w1, b1, w2, b2, gamma, beta, out
    s.xn = nc.dram_tensor("xn_rows", (NP, D), F32, kind="Internal").ap()
    s.x1 = nc.dram_tensor("x1_rows", (NP, D), F32, kind="Internal").ap()
    s.lows = nc.dram_tensor("low_digits", (1, 2, EP), BF16, kind="Internal").ap()
    s.ea = nc.dram_tensor("edge_logits", (EP,), F32, kind="Internal").ap()
    s.h = nc.dram_tensor("h_rows", (NP, D), F32, kind="Internal").ap()
    s.lists = nc.dram_tensor("lists", (NX * NP + 2 * NP, 1), I32, kind="Internal").ap()
    s.results = nc.dram_tensor("results", (N_TURNS * XB, D), F32, kind="Internal").ap()
    s.bounce = nc.dram_tensor("row_ends", (8, ET, 2), F32, kind="Internal").ap()
    with ExitStack() as ctx:
        sb = lambda name, shape, dt: ctx.enter_context(nc.sbuf_tensor(name, shape, dt))
        s.semaphores = []
        s.prime, s.primed = sb("prime", [1, 16], F32), 0
        s.ident = sb("ident", [P, P], F32)
        s.iota_f = sb("iota_f", [P, P], F32)
        s.iota_p = sb("iota_p", [P, 1], F32)
        s.WT = sb("WT", [P, DC, D], F32)
        s.wsd = sb("wsd", [P, DC, 2], F32)
        s.KV = sb("KV", [P, DC, P], F32)
        s.blockmask = sb("blockmask", [P, P], F32)
        s.agg = sb("agg", [P, DC, NP], F32)
        with ExitStack() as edge_ctx:
            eb = lambda name, shape, dt: edge_ctx.enter_context(nc.sbuf_tensor(name, shape, dt))
            s.score_bits = eb("score_bits", [P, 2, 3, NT], BF16)
            s.high = eb("high", [P, 2, ET], BF16)
            s.edge_score = eb("edge_score", [P, 2, ET], F32)
            s.srcT = eb("srcT", [P, ET], I32)
            s.relT = eb("relT", [P, ET], F32)
            s.alphaT = eb("alphaT", [P, ET], F32)
            s.base = eb("base", [1, ET], I32)
            s.windows = eb("windows", [1, 1], I32)
            s.dst_f = eb("dst_f", [RP, RG, P], F32)
            constants(s)
            node_scores(s)
            edge_digits(s)
            table_lookup(s)
            edge_softmax(s)
            aggregate(s)
        nc.clear_and_free_semaphores(s.semaphores)
        nc.all_engine_barrier()
        s.semaphores = []
        s.best = sb("best", [P, NT, 2], F32)
        s.which = sb("which", [P, NT, 2], mybir.dt.uint32)
        s.weight = sb("weight", [P, NT, 2], F32)
        s.slot = sb("slot", [P, 2, NT], I32)
        s.result_row = sb("result_row", [P, 2, NT], I32)
        s.list = sb("list", [P, NX, NT], I32)
        s.turns = sb("turns", [1, NX], I32)
        s.before = sb("before", [1, NX], I32)
        s.total = sb("total", [1, 1], I32)
        node_update(s)
        route(s)
        experts(s)
        final_norm(s)
        nc.clear_and_free_semaphores(s.semaphores)


def scope(s):
    ctx = ExitStack()
    sb = lambda name, shape, dt: ctx.enter_context(s.nc.sbuf_tensor(name, shape, dt))
    ps = lambda name, shape, dt=F32: ctx.enter_context(s.nc.psum_tensor(name, shape, dt))

    def sem(name):
        s.semaphores.append(s.nc.alloc_semaphore(name))
        return s.semaphores[-1]
    return ctx, sb, ps, sem


def constants(s):
    nc = s.nc
    ctx, sb, ps, sem = scope(s)
    with ctx:
        w_sb = sb("w_sb", [P, DC, D], F32)
        a_sb = sb("a_sb", [P, DC, 2], F32)
        fi = sb("fi", [P, P], I32)
        pi = sb("pi", [P, 1], I32)
        fb = sb("fb", [P, P], I32)
        pb = sb("pb", [P, 1], I32)
        fbf = sb("fbf", [P, P], F32)
        pbf = sb("pbf", [P, 1], F32)
        pT = [ps(f"pT{c}", [P, DC, P]) for c in range(DC)]
        pw = ps("pw", [P, DC, 2])
        w_loaded, ramps, const_link, ident_ready, wT_ready, wsd_ready = map(
            sem, ["c_w_loaded", "c_ramps", "c_link", "c_ident", "c_wT", "c_wsd"])
        block = ctx.enter_context(nc.Block())

        @block.sync
        def _(sp):
            sp.dma_start(w_sb[:, :, :], s.W.rearrange("(c p) i -> p c i", p=P)).then_inc(w_loaded, 16)
            for k in range(2):
                for c in range(DC):
                    sp.dma_start(a_sb[:, c, k:k + 1], s.A[0, k * D + c * P:k * D + (c + 1) * P].rearrange("(p a) -> p a", a=1),
                                 allow_slow_non_contiguous=True).then_inc(w_loaded, 16)

        @block.gpsimd
        def _(pool):
            pool.iota(fi[:, :], [[1, P]], base=0, channel_multiplier=0).then_inc(ramps, 1)
            pool.iota(pi[:, :], [[0, 1]], base=0, channel_multiplier=1).then_inc(ramps, 1)

        @block.vector
        def _(dve):
            link = Link(dve, const_link)
            dve.wait_ge(ramps, 2)
            dve.tensor_copy(s.iota_f[:, :], fi[:, :])
            link(dve.tensor_copy(s.iota_p[:, :], pi[:, :]))
            dve.tensor_scalar(s.ident[:, :], s.iota_f[:, :], s.iota_p[:, 0:1], None, ALU.is_equal).then_inc(ident_ready, 1)
            shift = HC.bit_length() - 1
            link(dve.tensor_scalar(fb[:, :], fi[:, :], shift, None, ALU.logical_shift_right))
            link(dve.tensor_scalar(pb[:, :], pi[:, :], shift, None, ALU.logical_shift_right))
            link(dve.tensor_copy(fbf[:, :], fb[:, :]))
            link(dve.tensor_copy(pbf[:, :], pb[:, :]))
            link(dve.tensor_scalar(s.blockmask[:, :], fbf[:, :], pbf[:, 0:1], None, ALU.is_equal))
            dve.wait_ge(wT_ready, 2 * DC)
            for c in range(DC):
                dve.tensor_copy(s.WT[:, c, :].rearrange("p (o q) -> p o q", o=DC), pT[c][:, :, :])
            dve.wait_ge(wsd_ready, 1)
            dve.tensor_copy(s.wsd[:, :, :], pw[:, :, :])

        @block.tensor
        def _(pe):
            pe.wait_ge(w_loaded, 16 * (1 + 2 * DC))
            pe.wait_ge(ident_ready, 1)
            for c in range(DC):
                for o in range(DC):
                    pe.transpose(pT[c][:, o, :], w_sb[:, o, c * P:(c + 1) * P], s.ident[:, :]).then_inc(wT_ready, 1)
            for c in range(DC):
                for o in range(DC):
                    last = pe.matmul(pw[:, c, :], w_sb[:, o, c * P:(c + 1) * P], a_sb[:, o, :], start=(o == 0), stop=(o == DC - 1))
            last.then_inc(wsd_ready, 1)


def node_scores(s):
    nc = s.nc
    ctx, sb, ps, sem = scope(s)
    with ctx:
        xt = sb("xt", [P, 2, D], F32)
        stats = sb("stats", [P, 2, 6], F32)
        mv = sb("mv", [P, 2, 2], F32)
        rstd = sb("rstd", [P, 2, 1], F32)
        xn = sb("xn", [P, 2, D], F32)
        xnT = sb("xnT", [P, 2, DC, P], F32)
        hsum = sb("hsum", [P, 2, HEADS], F32)
        dev = sb("dev", [P, 2, D], F32)
        sq = sb("sq", [P, 2, D], F32)
        hvar = sb("hvar", [P, 2, HEADS], F32)
        hstd = sb("hstd", [P, 2, HEADS], F32)
        hinv = sb("hinv", [P, 2, HEADS], F32)
        spare = sb("a_spare", [P, 1], F32)
        std = sb("a_std", [P, 2, 1], F32)
        eps = sb("a_eps", [P, 1], F32)
        nh = sb("nh", [P, 2, DC, P + 1], F32)
        zrow = sb("zrow", [1, P + 1], F32)
        score = sb("score", [P, 2, NT], F32)
        rest = sb("rest", [P, 2, NT], F32)
        piece = sb("piece", [P, 2, NT], F32)
        gram = sb("gram", [P, DC, P + 1], F32)
        ones = sb("ones", [P, P], F32)
        diag = sb("diag", [P, DC, P], F32)
        cols = sb("cols", [P, 2, DC], F32)
        rows = sb("rows", [P, 2, D], F32)
        kx = sb("kx", [P, DC, P], F32)
        kcol = sb("kcol", [P, DC, 1], F32)
        pT = [ps(f"a_pT{j}", [P, DC, P]) for j in range(2)]
        pS = ps("a_pS", [P, NT, 2])
        pG = [ps(f"a_pG{c}", [P, 512]) for c in range(DC)]
        pB = ps("a_pB", [P, DC, P])
        x_in = [sem(f"a_x_in{j}") for j in range(2)]
        xn_out = [sem(f"a_xn_out{j}") for j in range(2)]
        x_used, xn_ready, dev_ready, sq_ready, nh_ready = map(sem, ["a_x_used", "a_xn_ready", "a_dev_ready", "a_sq_ready", "a_nh_ready"])
        xnT_done, xnT_copied, score_done, gram_used, zeroed, gram_all = map(
            sem, ["a_xnT_done", "a_xnT_copied", "a_score_done", "a_gram_used", "a_zeroed", "a_gram_all"])
        mv_ready, std_ready, hvar_ready, hstd_ready, eps_set = map(sem, ["a_mv", "a_std", "a_hvar", "a_hstd", "a_eps_set"])
        dlink, mix_in, diag_ready, bc_done, ones_set = map(sem, ["a_dlink", "a_mix_in", "a_diag", "a_bc", "a_ones_set"])
        x_t, xn_t = tiled(s.x), tiled(s.xn)
        block = ctx.enter_context(nc.Block())

        @block.sync
        def _(sp):
            flat = lambda w: w.rearrange("h a c -> (h a c)")
            for k, w in enumerate((s.kw, s.kb)):
                for c in range(DC):
                    sp.dma_start(cols[:, k, c:c + 1], flat(w)[c * P:(c + 1) * P].rearrange("(p a) -> p a", a=1),
                                 allow_slow_non_contiguous=True).then_inc(mix_in, 16)
            for k, w in enumerate((s.vw, s.vb)):
                sp.dma_start(rows[:, k, :], w.rearrange("h a c -> a (h c)").broadcast_to([P, D])).then_inc(mix_in, 16)
            with sp.Fori(0, NT // 2) as i:
                for j in range(2):
                    sp.wait_ge(x_used, 2 * i + j + 1)
                    sp.dma_start(xt[:, j, :], x_t[ds(2 * i + j, 1), :, :].rearrange("a p d -> p (a d)")).then_inc(x_in[j], 16)

        @block.vector
        def _(dve):
            link = Link(dve, dlink)
            dve.sem_inc(x_used, 2)
            dve.memset(zrow[:, :], 0.0).then_inc(zeroed, 1)
            dve.memset(ones[:, :], 1.0).then_inc(ones_set, 1)
            dve.memset(eps[:, :], LN_EPS).then_inc(eps_set, 1)
            for j in range(2):
                for c in range(DC):
                    link(dve.memset(nh[:, j, c, P:P + 1], 1.0))
            with dve.Fori(0, NT // 2) as i:
                link.loop(i, 2 * 5)
                for j in range(2):
                    k = 2 * i + j
                    dve.wait_ge(x_in[j], 16 * i + 16)
                    link(dve.bn_stats(stats[:, j, :], xt[:, j, :]))
                    dve.memset(spare[:, :], 0.0)
                    dve.bn_aggr(mv[:, j, :], stats[:, j, :]).then_inc(mv_ready, 1)
                    dve.wait_ge(std_ready, k + 1)
                    link(dve.reciprocal(rstd[:, j, :], std[:, j, :]))
                    dve.wait_ge(xn_out[j], 16 * i + 16)
                    dve.wait_ge(xnT_done, k + 1)
                    dve.tensor_scalar(xn[:, j, :], xt[:, j, :], mv[:, j, 0:1], rstd[:, j, 0:1], ALU.subtract, ALU.mult).then_inc(x_used, 1)
                    dve.wait_ge(x_used, k + 3)
                    dve.tensor_reduce(hsum[:, j, :], xn[:, j, :].rearrange("p (h c) -> p h c", h=HEADS), AX_X, ALU.add).then_inc(xn_ready, 1)
                    dve.wait_ge(xn_ready, k + 1)
                    heads = lambda t: t[:, j, :].rearrange("p (h c) -> p h c", h=HEADS)
                    wide = lambda t: t[:, j, :].rearrange("p (h a) -> p h a", a=1).broadcast_to([P, HEADS, HC])
                    dve.scalar_tensor_tensor(heads(dev), wide(hsum), -1.0 / HC, heads(xn), ALU.mult, ALU.add).then_inc(dev_ready, 1)
                    dve.wait_ge(dev_ready, k + 1)
                    dve.wait_ge(sq_ready, k + 1)
                    dve.tensor_reduce(hvar[:, j, :], heads(sq), AX_X, ALU.add).then_inc(hvar_ready, 1)
                    dve.wait_ge(hstd_ready, k + 1)
                    link(dve.tensor_scalar(hstd[:, j, :], hstd[:, j, :], HEAD_EPS, None, ALU.add))
                    link(dve.reciprocal(hinv[:, j, :], hstd[:, j, :]))
                    dve.wait_ge(gram_used, k + 1)
                    for c in range(DC):
                        hh = HEADS // DC
                        last = dve.tensor_tensor(
                            nh[:, j, c, 0:P].rearrange("p (h c) -> p h c", h=hh),
                            dev[:, j, c * P:(c + 1) * P].rearrange("p (h c) -> p h c", h=hh),
                            hinv[:, j, c * hh:(c + 1) * hh].rearrange("p (h a) -> p h a", a=1).broadcast_to([P, hh, HC]), ALU.mult)
                        if c == 0:
                            link(last)
                    last.then_inc(nh_ready, 1)
            link.end_loop(NT // 2)
            dve.wait_ge(score_done, NT)
            link(dve.tensor_copy(score[:, :, :], pS[:, :, :].rearrange("p t k -> p k t")))
            for m in range(3):
                frm = score if m == 0 else rest
                link(dve.tensor_copy(s.score_bits[:, :, m, :], frm[:, :, :]))
                link(dve.tensor_copy(piece[:, :, :], s.score_bits[:, :, m, :]))
                link(dve.tensor_tensor(rest[:, :, :], frm[:, :, :], piece[:, :, :], ALU.subtract))
            dve.wait_ge(gram_all, 1)
            for c in range(DC):
                link(dve.tensor_copy(gram[:, c, :], pG[c][:, 0:P + 1]))
            for c in range(DC):
                dve.tensor_scalar(diag[:, c, :], s.ident[:, :], gram[:, c, P:P + 1], None, ALU.mult).then_inc(diag_ready, 1)
            dve.wait_ge(bc_done, 1)
            dve.wait_ge(mix_in, 16 * (2 * DC + 2))
            for c in range(DC):
                vcols = slice(c * P, (c + 1) * P)
                link(dve.tensor_scalar(kx[:, c, :], gram[:, c, 0:P], cols[:, 0, c:c + 1], None, ALU.mult))
                link(dve.scalar_tensor_tensor(kx[:, c, :], pB[:, c, :], cols[:, 1, c:c + 1], kx[:, c, :], ALU.mult, ALU.add))
                link(dve.tensor_tensor(kx[:, c, :], kx[:, c, :], rows[:, 0, vcols], ALU.mult))
                link(dve.tensor_scalar(kcol[:, c, :], gram[:, c, P:P + 1], cols[:, 0, c:c + 1], None, ALU.mult))
                link(dve.scalar_tensor_tensor(kcol[:, c, :], cols[:, 1, c:c + 1], float(N), kcol[:, c, :], ALU.mult, ALU.add))
                link(dve.scalar_tensor_tensor(kx[:, c, :], rows[:, 1, vcols], kcol[:, c, 0:1], kx[:, c, :], ALU.mult, ALU.add))
                link(dve.scalar_tensor_tensor(s.KV[:, c, :], kx[:, c, :], 1.0 / N, s.blockmask[:, :], ALU.mult, ALU.mult))

        @block.scalar
        def _(act):
            act.wait_ge(eps_set, 1)
            for j in range(2):
                prime(act, s, xn_out[j])
            with act.Fori(0, NT // 2) as i:
                for j in range(2):
                    k = 2 * i + j
                    act.wait_ge(mv_ready, k + 1)
                    act.activation(std[:, j, :], mv[:, j, 1:2], ACT.Sqrt, bias=eps[:, 0:1]).then_inc(std_ready, 1)
                    act.wait_ge(xn_ready, k + 1)
                    act.dma_start(xn_t[ds(k, 1), :, :].rearrange("a p d -> p (a d)"), xn[:, j, :]).then_inc(xn_out[j], 16)
                    act.wait_ge(dev_ready, k + 1)
                    act.activation(sq[:, j, :], dev[:, j, :], ACT.Square).then_inc(sq_ready, 1)
                    act.wait_ge(hvar_ready, k + 1)
                    act.activation(hstd[:, j, :], hvar[:, j, :], ACT.Sqrt, scale=1.0 / (HC - 1)).then_inc(hstd_ready, 1)
                    act.wait_ge(xnT_done, k + 3)
                    act.activation(xnT[:, j, :, :], pT[j][:, :, :], ACT.Identity).then_inc(xnT_copied, 1)
            for j in range(2):
                act.wait_ge(xn_out[j], 16 * (NT // 2 + 1))

        @block.tensor
        def _(pe):
            pe.sem_inc(xnT_done, 2)
            pe.sem_inc(gram_used, 2)
            pe.wait_ge(zeroed, 1)
            for c in range(DC):
                pe.matmul(pG[c][:, 0:P + 1], zrow[:, 0:P], zrow[:, :], start=True, stop=False)
            with pe.Fori(0, NT // 2) as i:
                for j in range(2):
                    k = 2 * i + j
                    pe.wait_ge(xn_ready, k + 1)
                    for c in range(DC):
                        last = pe.transpose(pT[j][:, c, :], xn[:, j, c * P:(c + 1) * P], s.ident[:, :])
                    last.then_inc(xnT_done, 1)
                    pe.wait_ge(xnT_copied, k + 1)
                    for c in range(DC):
                        last = pe.matmul(pS[:, ds(k, 1), :].rearrange("p a k -> p (a k)"), xnT[:, j, c, :], s.wsd[:, c, :], start=(c == 0), stop=(c == DC - 1))
                    last.then_inc(score_done, 1)
                    pe.wait_ge(nh_ready, k + 1)
                    for c in range(DC):
                        last = pe.matmul(pG[c][:, 0:P + 1], nh[:, j, c, 0:P], nh[:, j, c, :], start=False, stop=False)
                    last.then_inc(gram_used, 1)
            for c in range(DC):
                last = pe.matmul(pG[c][:, 0:P + 1], zrow[:, 0:P], zrow[:, :], start=False, stop=True)
            last.then_inc(gram_all, 1)
            pe.wait_ge(ones_set, 1)
            pe.wait_ge(diag_ready, DC)
            for c in range(DC):
                last = pe.matmul(pB[:, c, :], ones[:, :], diag[:, c, :], start=True, stop=True)
            last.then_inc(bc_done, 1)


def edge_digits(s):
    nc = s.nc
    ctx, sb, ps, sem = scope(s)
    with ctx:
        rows = sb("d_rows", [RP, 2, RG, P], I32)
        digit = sb("d_digit", [RP, 2, 2, RG, P], I32)
        high_f = sb("d_high_f", [RP, 2, RG, P], F32)
        low_b = sb("d_low_b", [RP, 2, RG, P], BF16)
        src_f = sb("d_src_f", [RP, RG, P], F32)
        HALF = 4
        pT = [[ps(f"d_pT{k}{h}", [P, HALF, RP]) for h in range(2)] for k in range(3)]
        rows_in, link_sem, low_ready, low_out, f_ready, T_done, base_in = map(
            sem, ["d_rows_in", "d_link", "d_low", "d_low_out", "d_f_ready", "d_T", "d_base_in"])
        block = ctx.enter_context(nc.Block())
        by_row = lambda a: a.rearrange("(g p e) -> p g e", p=RP, e=P)

        @block.sync
        def _(sp):
            sp.dma_start(rows[:, 0, :, :], by_row(s.src)).then_inc(rows_in, 16)
            sp.dma_start(rows[:, 1, :, :], by_row(s.dst)).then_inc(rows_in, 16)
            sp.dma_start(s.base[:, :], s.dst.rearrange("(a t e) -> a t e", a=1, e=P)[:, :, 0], allow_slow_non_contiguous=True).then_inc(base_in, 16)
            sp.wait_ge(low_ready, 1)
            for k in range(2):
                sp.dma_start(by_row(s.lows[0, k, :]), low_b[:, k, :, :]).then_inc(low_out, 16)
            sp.wait_ge(low_out, 32)
            sp.wait_ge(base_in, 16)

        @block.vector
        def _(dve):
            link = Link(dve, link_sem)
            dve.wait_ge(rows_in, 32)
            link(dve.tensor_scalar(digit[:, 0], rows[:, :], 7, None, ALU.logical_shift_right))
            link(dve.tensor_scalar(digit[:, 1], rows[:, :], P - 1, None, ALU.bitwise_and))
            dve.tensor_copy(low_b[:, :], digit[:, 1]).then_inc(low_ready, 1)
            dve.tensor_copy(high_f[:, :], digit[:, 0]).then_inc(f_ready, 1)
            dve.tensor_copy(src_f[:, :], rows[:, 0]).then_inc(f_ready, 1)
            dve.tensor_copy(s.dst_f[:, :], rows[:, 1]).then_inc(f_ready, 1)
            dve.wait_ge(T_done, 1)
            for k in range(3):
                for h in range(2):
                    n = min(HALF, RG - HALF * h)
                    to = (s.high[:, k, :] if k < 2 else s.srcT[:, :])[:, HALF * h * RP:(HALF * h + n) * RP]
                    dve.tensor_copy(to.rearrange("p (g r) -> p g r", g=n), pT[k][h][:, 0:n, :])

        @block.tensor
        def _(pe):
            pe.wait_ge(f_ready, 3)
            for k in range(3):
                for g in range(RG):
                    of = high_f[:, k, g, :] if k < 2 else src_f[:, g, :]
                    last = pe.transpose(pT[k][g // HALF][:, g % HALF, :], of, s.ident[0:RP, 0:RP])
            last.then_inc(T_done, 1)


def table_lookup(s):
    nc = s.nc
    ctx, sb, ps, sem = scope(s)
    with ctx:
        low = sb("t_low", [P, 2, 2, TC * P], BF16)
        onehot = sb("t_onehot", [P, 2, 2, TC * P], BF16)
        ramp = sb("t_ramp", [P, NT], BF16)
        off = sb("t_off", [P, 2, 2, TC, NT], BF16)
        picked = sb("t_picked", [P, 2, 2, TC, NT], F32)
        attr = sb("t_attr", [P, 2, TC, ED], F32)
        prod = sb("t_prod", [P, 2, TC, ED], F32)
        a_e = sb("t_a_e", [P, ED], F32)
        ea = sb("t_ea", [P, ET], F32)
        pR = [[ps(f"t_pR{j}{k}", [P, TC, NT]) for k in range(2)] for j in range(2)]
        low_in = [sem(f"t_low_in{j}") for j in range(2)]
        attr_in = [sem(f"t_attr_in{j}") for j in range(2)]
        a_in, low_used, rows_done = map(sem, ["t_a_in", "t_low_used", "t_rows"])
        off_ready, prod_ready, picked_ready, scores_done, link_sem, ramp_ready, ea_out, ea_ready = map(
            sem, ["t_off", "t_prod", "t_picked", "t_scores", "t_link", "t_ramp_s", "t_ea_out", "t_ea_ready"])
        block = ctx.enter_context(nc.Block())
        attr_c = s.edge_attr.rearrange("(p c) d -> p c d", p=P)
        TURNS = ET // TC // 2

        @block.sync
        def _(sp):
            sp.dma_start(a_e[:, :], s.A[:, 2 * D:2 * D + ED].broadcast_to([P, ED])).then_inc(a_in, 16)
            with sp.Fori(0, TURNS) as i:
                for j in range(2):
                    k = 2 * i + j
                    sp.wait_ge(low_used, k + 1)
                    sp.dma_start(low[:, j, :, :], s.lows[:, :, ds(k * (TC * P), TC * P)].broadcast_to([P, 2, TC * P])).then_inc(low_in[j], 16)
                    sp.wait_ge(prod_ready, k + 1)
                    sp.dma_start(attr[:, j, :, :], attr_c[:, ds(k * TC, TC), :]).then_inc(attr_in[j], 16)
            sp.wait_ge(ea_ready, 2 * TURNS + 2)
            sp.dma_start(s.ea.rearrange("(p c) -> p c", p=P), ea[:, :]).then_inc(ea_out, 16)
            sp.wait_ge(ea_out, 16)

        @block.gpsimd
        def _(pool):
            pool.sem_inc(prod_ready, 2)
            pool.wait_ge(a_in, 16)
            pool.tensor_copy(ramp[:, :], s.iota_f[:, 0:NT]).then_inc(ramp_ready, 1)
            pool.wait_ge(ramp_ready, 1)
            with pool.Fori(0, TURNS) as i:
                for j in range(2):
                    k = 2 * i + j
                    pool.wait_ge(picked_ready, 2 * k + 2)
                    for q in range(2):
                        pool.tensor_tensor(
                            off[:, j, q], ramp[:, :].rearrange("p (a n) -> p a n", a=1).broadcast_to([P, TC, NT]),
                            s.high[:, q, ds(k * TC, TC)].rearrange("p (t a) -> p t a", a=1).broadcast_to([P, TC, NT]),
                            ALU.subtract).then_inc(off_ready, 1)
                    pool.wait_ge(attr_in[j], 16 * i + 16)
                    pool.wait_ge(ea_ready, k + 1)
                    pool.tensor_tensor(prod[:, j], attr[:, j], a_e[:, :].rearrange("p (a n) -> p a n", a=1).broadcast_to([P, TC, ED]),
                                       ALU.mult).then_inc(prod_ready, 1)

        @block.vector
        def _(dve):
            dve.sem_inc(low_used, 2)
            dve.sem_inc(picked_ready, 4)
            dve.sem_inc(ea_ready, 2)
            def build(k, turn, j):
                dve.wait_ge(low_in[j], 16 * turn + 16)
                dve.wait_ge(rows_done, k + 1)
                dve.tensor_scalar(onehot[:, j], low[:, j], s.iota_p[:, 0:1], None, ALU.is_equal).then_inc(low_used, 1)
            with dve.Fori(0, TURNS) as i:
                for j in range(2):
                    build(2 * i + j, i, j)
                for j in range(2):
                    k = 2 * i + j
                    dve.wait_ge(rows_done, k + 3)
                    for q in range(2):
                        dve.wait_ge(off_ready, 2 * k + q + 1)
                        dve.scalar_tensor_tensor(picked[:, j, q], off[:, j, q], 0.0, pR[j][q][:, :, :], ALU.is_equal, ALU.mult).then_inc(picked_ready, 1)
                    dve.wait_ge(prod_ready, k + 3)
                    dve.tensor_reduce(ea[:, ds(k * TC, TC)], prod[:, j], AX_X, ALU.add).then_inc(ea_ready, 1)
                    dve.wait_ge(picked_ready, 2 * k + 6)
                    dve.tensor_reduce(s.edge_score[:, :, ds(k * TC, TC)], picked[:, j], AX_X, ALU.add)

        @block.tensor
        def _(pe):
            pe.sem_inc(rows_done, 2)
            with pe.Fori(0, TURNS) as i:
                for j in range(2):
                    k = 2 * i + j
                    pe.wait_ge(low_used, k + 3)
                    pe.wait_ge(picked_ready, 2 * k + 2)
                    for q in range(2):
                        for t in range(TC):
                            for m in range(3):
                                last = pe.matmul(pR[j][q][:, t, :], onehot[:, j, q, t * P:(t + 1) * P], s.score_bits[:, q, m, :],
                                                 start=(m == 0), stop=(m == 2))
                    last.then_inc(rows_done, 1)


def edge_softmax(s):
    nc = s.nc
    ctx, sb, ps, sem = scope(s)
    with ctx:
        row = lambda name: sb("s_" + name, [RP, RG, P], F32)
        g, sd, first, last, keep, fwd, top, total, e, em, ex = map(
            row, ["g", "sd", "first", "last", "keep", "fwd", "top", "total", "e", "em", "ex"])
        notfirst, tmp, in_first, in_last, rel, ea = map(row, ["notfirst", "tmp", "in_first", "in_last", "rel", "ea"])
        ends = sb("s_ends", [RP, RG, 2], F32)
        keys = sb("s_keys", [RP, RG, 2], F32)
        wide = sb("s_wide", [RP, RG, 2], F32)
        K2 = 2 * ET
        one = lambda name: sb("s1_" + name, [1, K2], F32)
        key1, val1, first1, last1, keep1, fwd1, tot1, reset1 = map(one, ["key", "val", "first", "last", "keep", "fwd", "tot", "reset"])
        span = sb("s_span", [1, ET], F32)
        span1 = sb("s_span1", [1, 1], F32)
        span_i = sb("s_span_i", [1, 1], I32)
        HALF = 4
        pT = [[ps(f"s_pT{k}{h}", [RP, HALF, P]) for h in range(2)] for k in range(2)]
        pB = [[ps(f"s_pB{k}{h}", [P, HALF, RP]) for h in range(2)] for k in range(2)]
        link_sem, ea_in, T_done, B_done, keys_ready, ends_ready, back_ready, exp_in, exp_done, out_ready, zeroed = map(
            sem, ["s_link", "s_ea_in", "s_T", "s_B", "s_keys_ready", "s_ends_ready", "s_back_ready", "s_exp_in", "s_exp", "s_out", "s_zeroed"])
        stored = [sem(f"s_stored{n}") for n in range(5)]
        line_in = [sem(f"s_line_in{n}") for n in range(3)]
        wide_in = [sem(f"s_wide_in{n}") for n in range(2)]
        block = ctx.enter_context(nc.Block())
        flat = lambda t: t[:, :, :].rearrange("p g e -> p (g e)")
        to_rows = lambda n: s.bounce[n].rearrange("(g p) k -> p g k", p=RP)
        to_line = lambda n: s.bounce[n].rearrange("(a t) k -> a (t k)", a=1)

        @block.gpsimd
        def _(pool):
            pool.memset(s.agg[:, :, :], 0.0)

        @block.sync
        def _(sp):
            sp.dma_start(ea[:, :, :], s.ea.rearrange("(g p e) -> p g e", p=RP, e=P)).then_inc(ea_in, 16)
            sp.wait_ge(keys_ready, 1)
            sp.dma_start(to_rows(0), keys[:, :, :]).then_inc(stored[0], 16)
            sp.wait_ge(stored[0], 16)
            sp.dma_start(key1[:, :], to_line(0)).then_inc(line_in[0], 16)
            for n in range(2):
                sp.wait_ge(ends_ready, n + 1)
                sp.dma_start(to_rows(1 + n), ends[:, :, :]).then_inc(stored[1 + n], 16)
                sp.wait_ge(stored[1 + n], 16)
                sp.dma_start(val1[:, :], to_line(1 + n)).then_inc(line_in[1 + n], 16)
                sp.wait_ge(back_ready, n + 1)
                sp.dma_start(to_line(3 + n), tot1[:, :]).then_inc(stored[3 + n], 16)
                sp.wait_ge(stored[3 + n], 16)
                sp.dma_start(wide[:, :, :], to_rows(3 + n)).then_inc(wide_in[n], 16)

        @block.vector
        def _(dve):
            link = Link(dve, link_sem)
            dst = s.dst_f
            bc = lambda col: col.broadcast_to([RP, RG, P])
            link(dve.tensor_copy(keys[:, :, 0:1], dst[:, :, 0:1]))
            dve.tensor_copy(keys[:, :, 1:2], dst[:, :, P - 1:P]).then_inc(keys_ready, 1)
            link(dve.memset(first[:, :, 0:1], 1.0))
            link(dve.memset(last[:, :, P - 1:P], 1.0))
            link(dve.tensor_tensor(first[:, :, 1:P], dst[:, :, 1:P], dst[:, :, 0:P - 1], ALU.not_equal))
            link(dve.tensor_copy(last[:, :, 0:P - 1], first[:, :, 1:P]))
            link(dve.tensor_scalar(keep[:, :, :], last[:, :, :], -1.0, 1.0, ALU.mult, ALU.add))
            link(dve.tensor_scalar(notfirst[:, :, :], first[:, :, :], -1.0, 1.0, ALU.mult, ALU.add))
            link(dve.tensor_scalar(first[:, :, :], first[:, :, :], -BIG, None, ALU.mult))
            link(dve.tensor_tensor(in_first[:, :, :], dst[:, :, :], bc(dst[:, :, 0:1]), ALU.is_equal))
            link(dve.tensor_tensor(in_last[:, :, :], dst[:, :, :], bc(dst[:, :, P - 1:P]), ALU.is_equal))
            link(dve.tensor_tensor(rel[:, :, :], dst[:, :, :], bc(dst[:, :, 0:1]), ALU.subtract))
            dve.wait_ge(T_done, 1)
            dve.wait_ge(ea_in, 16)
            for h in range(2):
                n = min(HALF, RG - HALF * h)
                gs = slice(HALF * h, HALF * h + n)
                link(dve.tensor_tensor(g[:, gs, :], pT[0][h][:, 0:n, :], ea[:, gs, :], ALU.add))
                link(dve.tensor_copy(sd[:, gs, :], pT[1][h][:, 0:n, :]))

            def runs(data, in_place_of_zero, op_reset, op, to):
                link(dve.tensor_tensor_scan(flat(fwd), in_place_of_zero, flat(data), 0.0, op_reset, op))
                link(dve.tensor_tensor(fwd[:, :, :], fwd[:, :, :], last[:, :, :], ALU.mult))
                link(dve.tensor_tensor_scan(flat(to)[:, ::-1], flat(keep)[:, ::-1], flat(fwd)[:, ::-1], 0.0, ALU.mult, ALU.add))
                link(dve.tensor_copy(ends[:, :, 0:1], to[:, :, 0:1]))
                dve.tensor_copy(ends[:, :, 1:2], to[:, :, P - 1:P]).then_inc(ends_ready, 1)

            def runs_over_rows(reset, op_reset, op):
                link(dve.tensor_tensor_scan(fwd1[:, :], reset, val1[:, :], 0.0, op_reset, op))
                link(dve.tensor_tensor(fwd1[:, :], fwd1[:, :], last1[:, :], ALU.mult))
                dve.tensor_tensor_scan(tot1[:, ::-1], keep1[:, ::-1], fwd1[:, ::-1], 0.0, ALU.mult, ALU.add).then_inc(back_ready, 1)

            runs(g, flat(first), ALU.add, ALU.max, top)
            dve.wait_ge(line_in[0], 16)
            link(dve.memset(first1[:, 0:1], 1.0))
            link(dve.memset(last1[:, K2 - 1:K2], 1.0))
            link(dve.tensor_tensor(first1[:, 1:K2], key1[:, 1:K2], key1[:, 0:K2 - 1], ALU.not_equal))
            link(dve.tensor_copy(last1[:, 0:K2 - 1], first1[:, 1:K2]))
            link(dve.tensor_scalar(keep1[:, :], last1[:, :], -1.0, 1.0, ALU.mult, ALU.add))
            link(dve.tensor_scalar(reset1[:, :], first1[:, :], -BIG, None, ALU.mult))
            pairs = lambda t: t[:, :].rearrange("a (t k) -> a t k", k=2)
            link(dve.tensor_tensor(span[:, :], pairs(key1)[:, :, 1], pairs(key1)[:, :, 0], ALU.subtract))
            link(dve.tensor_reduce(span1[:, :], span[:, :], AX_X, ALU.max))
            link(dve.tensor_copy(span_i[:, :], span1[:, :]))
            link(dve.tensor_scalar(span_i[:, :], span_i[:, :], 7, None, ALU.logical_shift_right))
            link(dve.tensor_scalar(s.windows[:, :], span_i[:, :], 1, None, ALU.add))
            dve.wait_ge(line_in[1], 16)
            runs_over_rows(reset1[:, :], ALU.add, ALU.max)
            dve.wait_ge(wide_in[0], 16)
            for k, part in enumerate((in_first, in_last)):
                link(dve.tensor_scalar(tmp[:, :, :], part[:, :, :], 1.0, BIG, ALU.subtract, ALU.mult))
                link(dve.tensor_tensor(tmp[:, :, :], tmp[:, :, :], bc(wide[:, :, k:k + 1]), ALU.add))
                link(dve.tensor_tensor(top[:, :, :], top[:, :, :], tmp[:, :, :], ALU.max))
            for value, to in ((g, e), (top, em)):
                link(dve.tensor_tensor(value[:, :, :], value[:, :, :], sd[:, :, :], ALU.add))
                link(dve.scalar_tensor_tensor(flat(to), flat(value), SLOPE, flat(value), ALU.mult, ALU.max))
            dve.tensor_tensor(e[:, :, :], e[:, :, :], em[:, :, :], ALU.subtract).then_inc(exp_in, 1)
            dve.wait_ge(exp_done, 1)
            runs(ex, flat(notfirst), ALU.mult, ALU.add, total)
            dve.wait_ge(line_in[2], 16)
            link(dve.tensor_tensor(pairs(val1)[:, :, 1], pairs(val1)[:, :, 1], pairs(first1)[:, :, 1], ALU.mult))
            link(dve.tensor_scalar(first1[:, :], first1[:, :], -1.0, 1.0, ALU.mult, ALU.add))
            runs_over_rows(first1[:, :], ALU.mult, ALU.add)
            dve.wait_ge(wide_in[1], 16)
            for k, part in enumerate((in_first, in_last)):
                link(dve.tensor_tensor(tmp[:, :, :], part[:, :, :], bc(wide[:, :, k:k + 1]), ALU.mult))
                link(dve.tensor_tensor(total[:, :, :], total[:, :, :], tmp[:, :, :], ALU.max))
            link(dve.reciprocal(tmp[:, :, :], total[:, :, :]))
            dve.tensor_tensor(ex[:, :, :], ex[:, :, :], tmp[:, :, :], ALU.mult).then_inc(out_ready, 1)
            dve.wait_ge(B_done, 1)
            for k, to in enumerate((s.alphaT, s.relT)):
                for h in range(2):
                    n = min(HALF, RG - HALF * h)
                    dve.tensor_copy(to[:, HALF * h * RP:(HALF * h + n) * RP].rearrange("p (g r) -> p g r", g=n), pB[k][h][:, 0:n, :])

        @block.scalar
        def _(act):
            act.wait_ge(exp_in, 1)
            act.activation(flat(ex), flat(e), ACT.Exp).then_inc(exp_done, 1)

        @block.tensor
        def _(pe):
            for k in range(2):
                for gg in range(RG):
                    done = pe.transpose(pT[k][gg // HALF][:, gg % HALF, :], s.edge_score[:, k, gg * RP:(gg + 1) * RP], s.ident[:, :])
            done.then_inc(T_done, 1)
            pe.wait_ge(out_ready, 1)
            for k, of in enumerate((ex, rel)):
                for gg in range(RG):
                    done = pe.transpose(pB[k][gg // HALF][:, gg % HALF, :], of[:, gg, :], s.ident[0:RP, 0:RP])
            done.then_inc(B_done, 1)


def aggregate(s):
    nc = s.nc
    ctx, sb, ps, sem = scope(s)
    with ctx:
        BANKS = 8
        SLOTS = 8
        index = sb("g_index", [P, GU], I32)
        spare = sb("g_spare", [P, 3], F32)
        rows = sb("g_rows", [P, GU, D], F32)
        place = sb("g_place", [P, GU, P], F32)
        ramp = sb("g_ramp", [P, P], F32)
        base = sb("g_base", [1, ET], I32)
        pA = [ps(f"g_pA{b}", [P, DC, P]) for b in range(BANKS)]
        row_in = [sem(f"g_row_in{q}") for q in range(GU)]
        index_ready, placed, summed, added, link_sem, setup, taken = map(sem, ["g_index_ready", "g_placed", "g_summed", "g_added", "g_link", "g_setup", "g_taken"])
        ZR = N_TURNS * XB // P // ZERO_DMAS
        zero = sb("g_zero", [P, ZR * D], F32)
        zero_set, zero_out = sem("g_zero_set"), sem("g_zero_out")
        block = ctx.enter_context(nc.Block())
        TURNS = ET // GU

        @block.sync
        def _(sp):
            sp.wait_ge(zero_set, 1)
            to = s.results.rearrange("(z p r) d -> z p (r d)", z=ZERO_DMAS, p=P)
            for z in range(ZERO_DMAS):
                sp.dma_start(to[z], zero[:, :]).then_inc(zero_out, 16)
            sp.wait_ge(zero_out, 16 * ZERO_DMAS)

        @block.scalar
        def _(act):
            windows = act.value_load(s.windows[0:1, 0:1], min_val=1, max_val=NT)
            with act.Fori(0, windows) as w:
                with act.Fori(0, TURNS) as i:
                    turn = w * TURNS + i
                    for h in range(GU // SLOTS):
                        act.wait_ge(summed, turn * GU + SLOTS * (h + 1))
                        act.wait_ge(taken, turn * 2 + h + 1)
                        act.activation(index[:, h * SLOTS:(h + 1) * SLOTS], s.srcT[:, ds(i * GU + h * SLOTS, SLOTS)], ACT.Copy).then_inc(index_ready, 1)

        @block.gpsimd
        def _(pool):
            pool.sem_inc(taken, 2)
            pool.memset(spare[:, :], 0.0).then_inc(setup, 1)
            pool.wait_ge(setup, 1)
            windows = pool.value_load(s.windows[0:1, 0:1], min_val=1, max_val=NT)
            with pool.Fori(0, windows) as w:
                with pool.Fori(0, TURNS) as i:
                    turn = w * TURNS + i
                    for q in range(GU):
                        if q % SLOTS == 0:
                            pool.wait_ge(index_ready, turn * (GU // SLOTS) + q // SLOTS + 1)
                            pool.tensor_tensor(spare[:, 1 + q // SLOTS:2 + q // SLOTS], spare[:, 0:1], spare[:, 0:1], ALU.mult).then_inc(taken, 1)
                        pool.indirect_dma_start(rows[:, q, :], None, s.xn, bass.IndirectOffsetOnAxis(ap=index[:, q:q + 1], axis=0)).then_inc(row_in[q], 16)

        @block.vector
        def _(dve):
            link = Link(dve, link_sem)
            dve.sem_inc(added, BANKS)
            windows = dve.value_load(s.windows[0:1, 0:1], min_val=1, max_val=NT)
            dve.memset(zero[:, :], 0.0).then_inc(zero_set, 1)
            link(dve.tensor_copy(ramp[:, :], s.iota_f[:, :]))
            link(dve.tensor_copy(base[:, :], s.base[:, :]))
            with dve.Fori(0, windows) as w:
                link.loop(w, 2)
                with dve.Fori(0, TURNS) as i:
                    turn = w * TURNS + i
                    _, starts = nc.values_load_multi_w_load_instructions(
                        base[0:1, ds(i * GU, GU)], engines=[DVE], min_val=0, max_val=NP - P,
                        skip_runtime_bounds_check_because="destinations are nodes, and later windows are held below NP - 128")
                    for q in range(GU):
                        col = i * GU + q
                        dve.tensor_scalar(place[:, q, :], ramp[:, :], s.relT[:, ds(col, 1)], s.alphaT[:, ds(col, 1)],
                                          ALU.is_equal, ALU.mult).then_inc(placed, 1)
                    for q in range(GU):
                        dve.wait_ge(summed, turn * GU + q + 1 + GU)
                        dve.wait_ge(added, turn * GU + q + BANKS)
                        window = s.agg[:, :, ds(starts[q], P)]
                        dve.tensor_tensor(window, window, pA[q % BANKS][:, :, :], ALU.add).then_inc(added, 1)
                dve.wait_ge(added, (w + 1) * ET + BANKS)
                link(dve.tensor_scalar(ramp[:, :], ramp[:, :], float(P), None, ALU.add))
                link(dve.tensor_scalar(base[:, :], base[:, :], float(P), float(NP - P), ALU.add, ALU.min))

        @block.tensor
        def _(pe):
            pe.sem_inc(summed, GU)
            windows = pe.value_load(s.windows[0:1, 0:1], min_val=1, max_val=NT)
            with pe.Fori(0, windows) as w:
                with pe.Fori(0, TURNS) as i:
                    turn = w * TURNS + i
                    for q in range(GU):
                        pe.wait_ge(row_in[q], 16 * turn + 16)
                        pe.wait_ge(placed, turn * GU + q + 1)
                        pe.wait_ge(added, turn * GU + q + 1)
                        for c in range(DC):
                            last = pe.matmul(pA[q % BANKS][:, c, :], rows[:, q, c * P:(c + 1) * P], place[:, q, :], start=True, stop=True)
                        last.then_inc(summed, 1)


def node_update(s):
    nc = s.nc
    ctx, sb, ps, sem = scope(s)
    with ctx:
        xt = sb("u_xt", [P, 2, D], F32)
        xn = sb("u_xn", [P, 2, D], F32)
        aggs = sb("u_aggs", [P, 2, DC, P], F32)
        xnT = sb("u_xnT", [P, 2, DC, P], F32)
        x1 = sb("u_x1", [P, 2, D], F32)
        h = sb("u_h", [P, 2, D], F32)
        hT = sb("u_hT", [P, 2, DC, P], F32)
        stats = sb("u_stats", [P, 2, 6], F32)
        mv = sb("u_mv", [P, 2, 2], F32)
        std = sb("u_std", [P, 2, 1], F32)
        rstd = sb("u_rstd", [P, 2, 1], F32)
        eps = sb("u_eps", [P, 1], F32)
        spare = sb("u_spare", [P, 1], F32)
        gate = sb("u_gate", [P, DC, NX], F32)
        gate_b = sb("u_gate_b", [P, NX], F32)
        logit = sb("u_logit", [P, 2, NX], F32)
        best = sb("u_best", [P, 2, 8], F32)
        which = sb("u_which", [P, 2, 8], mybir.dt.uint32)
        pT = [ps(f"u_pT{j}", [P, DC, P]) for j in range(2)]
        pX = [ps(f"u_pX{j}", [P, D]) for j in range(2)]
        pH = [ps(f"u_pH{j}", [P, DC, P]) for j in range(2)]
        pL = [ps(f"u_pL{j}", [P, NX]) for j in range(2)]
        in_x = [sem(f"u_in_x{j}") for j in range(2)]
        in_xn = [sem(f"u_in_xn{j}") for j in range(2)]
        x1_out = [sem(f"u_x1_out{j}") for j in range(2)]
        h_out = [sem(f"u_h_out{j}") for j in range(2)]
        eps_set, gate_in, x1_ready, xnT_done, xnT_copied, aggs_ready, x_done, mv_ready, std_ready, h_ready = map(
            sem, ["u_eps_set", "u_gate_in", "u_x1_ready", "u_xnT_done", "u_xnT_copied", "u_aggs_ready", "u_x_done", "u_mv_ready", "u_std_ready", "u_h_ready"])
        hT_done, hT_copied, logit_done, link_sem, top_ready = map(sem, ["u_hT_done", "u_hT_copied", "u_logit_done", "u_link", "u_top"])
        x_t, xn_t, x1_t, h_t = tiled(s.x), tiled(s.xn), tiled(s.x1), tiled(s.h)
        block = ctx.enter_context(nc.Block())
        tile = lambda a, k: a[ds(k, 1), :, :].rearrange("a p d -> p (a d)")

        @block.sync
        def _(sp):
            sp.dma_start(gate[:, :, :], s.gate_w.rearrange("(c p) e -> p c e", p=P)).then_inc(gate_in, 16)
            sp.dma_start(gate_b[:, :], s.gate_b.rearrange("(a e) -> a e", a=1).broadcast_to([P, NX])).then_inc(gate_in, 16)
            with sp.Fori(0, NT // 2) as i:
                for j in range(2):
                    k = 2 * i + j
                    sp.wait_ge(x1_ready, k + 1)
                    sp.wait_ge(xnT_done, k + 1)
                    sp.dma_start(xt[:, j, :], tile(x_t, k)).then_inc(in_x[j], 16)
                    sp.dma_start(xn[:, j, :], tile(xn_t, k)).then_inc(in_xn[j], 16)

        @block.vector
        def _(dve):
            link = Link(dve, link_sem)
            dve.sem_inc(x1_ready, 2)
            dve.memset(eps[:, :], LN_EPS).then_inc(eps_set, 1)
            dve.wait_ge(gate_in, 32)
            with dve.Fori(0, NT // 2) as i:
                link.loop(i, 2 * 5)
                for j in range(2):
                    k = 2 * i + j
                    dve.wait_ge(in_x[j], 16 * i + 16)
                    dve.wait_ge(in_xn[j], 16 * i + 16)
                    dve.wait_ge(x_done, k + 1)
                    dve.wait_ge(x1_out[j], 16 * i + 16)
                    link(dve.tensor_tensor(x1[:, j, :], pX[j][:, :], xt[:, j, :], ALU.add))
                    dve.tensor_tensor(x1[:, j, :], x1[:, j, :], xn[:, j, :], ALU.add).then_inc(x1_ready, 1)
                    dve.wait_ge(x1_ready, k + 3)
                    link(dve.bn_stats(stats[:, j, :], x1[:, j, :]))
                    dve.memset(spare[:, :], 0.0)
                    dve.bn_aggr(mv[:, j, :], stats[:, j, :]).then_inc(mv_ready, 1)
                    dve.wait_ge(std_ready, k + 1)
                    link(dve.reciprocal(rstd[:, j, :], std[:, j, :]))
                    dve.wait_ge(h_out[j], 16 * i + 16)
                    dve.wait_ge(hT_done, k + 1)
                    dve.tensor_scalar(h[:, j, :], x1[:, j, :], mv[:, j, 0:1], rstd[:, j, 0:1], ALU.subtract, ALU.mult).then_inc(h_ready, 1)
                    dve.wait_ge(logit_done, k + 1)
                    link(dve.tensor_tensor(logit[:, j, :], pL[j][:, :], gate_b[:, :], ALU.add))
                    dve.memset(spare[:, :], 0.0)
                    link(dve.max(best[:, j, :], logit[:, j, :]))
                    dve.memset(spare[:, :], 0.0)
                    dve.max_index(which[:, j, :], best[:, j, :], logit[:, j, :]).then_inc(top_ready, 1)
                    dve.wait_ge(top_ready, k + 1)
                    row = lambda a: a[:, ds(k, 1), :].rearrange("p a e -> p (a e)")
                    dve.tensor_copy(row(s.best), best[:, j, 0:2])
                    dve.tensor_copy(row(s.which), which[:, j, 0:2])

        @block.scalar
        def _(act):
            act.wait_ge(eps_set, 1)
            act.sem_inc(aggs_ready, 2)
            for j in range(2):
                prime(act, s, x1_out[j])
                prime(act, s, h_out[j])
            with act.Fori(0, NT // 2) as i:
                for j in range(2):
                    k = 2 * i + j
                    act.wait_ge(hT_done, k + 1)
                    act.activation(aggs[:, j, :, :], s.agg[:, :, ds(k * P, P)], ACT.Identity).then_inc(aggs_ready, 1)
                    act.wait_ge(xnT_done, k + 3)
                    act.activation(xnT[:, j, :, :], pT[j][:, :, :], ACT.Identity).then_inc(xnT_copied, 1)
                    act.wait_ge(mv_ready, k + 1)
                    act.activation(std[:, j, :], mv[:, j, 1:2], ACT.Sqrt, bias=eps[:, 0:1]).then_inc(std_ready, 1)
                    act.wait_ge(x1_ready, k + 3)
                    act.dma_start(tile(x1_t, k), x1[:, j, :]).then_inc(x1_out[j], 16)
                    act.wait_ge(h_ready, k + 1)
                    act.dma_start(tile(h_t, k), h[:, j, :]).then_inc(h_out[j], 16)
                    act.wait_ge(hT_done, k + 3)
                    act.activation(hT[:, j, :, :], pH[j][:, :, :], ACT.Identity).then_inc(hT_copied, 1)
            for j in range(2):
                act.wait_ge(x1_out[j], 16 * (NT // 2 + 1))
                act.wait_ge(h_out[j], 16 * (NT // 2 + 1))

        @block.tensor
        def _(pe):
            pe.sem_inc(xnT_done, 2)
            pe.sem_inc(hT_done, 2)
            pe.wait_ge(gate_in, 32)
            with pe.Fori(0, NT // 2) as i:
                for j in range(2):
                    k = 2 * i + j
                    pe.wait_ge(in_xn[j], 16 * i + 16)
                    for c in range(DC):
                        last = pe.transpose(pT[j][:, c, :], xn[:, j, c * P:(c + 1) * P], s.ident[:, :])
                    last.then_inc(xnT_done, 1)
                    pe.wait_ge(x1_ready, k + 1)
                    pe.wait_ge(aggs_ready, k + 3)
                    for c in range(DC):
                        pe.matmul(pX[j][:, :], aggs[:, j, c, :], s.WT[:, c, :], start=(c == 0), stop=False)
                    pe.wait_ge(xnT_copied, k + 1)
                    for c in range(DC):
                        last = pe.matmul(pX[j][:, c * P:(c + 1) * P], xnT[:, j, c, :], s.KV[:, c, :], start=False, stop=(c == DC - 1))
                    last.then_inc(x_done, 1)
                    pe.wait_ge(h_ready, k + 1)
                    for c in range(DC):
                        last = pe.transpose(pH[j][:, c, :], h[:, j, c * P:(c + 1) * P], s.ident[:, :])
                    last.then_inc(hT_done, 1)
                    pe.wait_ge(hT_copied, k + 1)
                    for c in range(DC):
                        last = pe.matmul(pL[j][:, :], hT[:, j, c, :], gate[:, c, :], start=(c == 0), stop=(c == DC - 1))
                    last.then_inc(logit_done, 1)


def route(s):
    nc = s.nc
    ctx, sb, ps, sem = scope(s)
    with ctx:
        mat = lambda name: sb("r_" + name, [P, NX, NT], F32)
        hot = [mat(f"hot{k}") for k in range(2)]
        both, keep, incl, place, picked = map(mat, ["both", "keep", "incl", "place", "picked"])
        which_f = sb("r_which_f", [P, NT, 2], F32)
        delta = sb("r_delta", [P, NT], F32)
        ex = sb("r_ex", [P, NT], F32)
        den = sb("r_den", [P, NT], F32)
        node_i = sb("r_node_i", [P, NT], I32)
        node_f = sb("r_node_f", [P, NT], F32)
        valid = sb("r_valid", [P, NT], F32)
        exp_i = sb("r_exp_i", [P, NX], I32)
        exp_f = sb("r_exp_f", [P, NX], F32)
        before = sb("r_before", [P, P], F32)
        ones = sb("r_ones", [P, P], F32)
        slot_f = sb("r_slot_f", [P, 2, NT], F32)
        away = sb("r_away", [P, 2, NT], F32)
        begin = sb("r_begin", [P, 2, NT], F32)
        rank = sb("r_rank", [P, 2, NT], F32)
        rank_i = sb("r_rank_i", [P, 2, NT], I32)
        digit_i = sb("r_digit_i", [P, 2, 2, NT], I32)
        digit = sb("r_digit", [P, 2, 2, NT], F32)
        turns_i = sb("r_turns_i", [P, NX], I32)
        turns_f = sb("r_turns_f", [P, NX], F32)
        keep1 = sb("r_keep1", [P, NX], F32)
        ends = sb("r_ends", [P, NX], F32)
        zero = sb("r_zero", [P, NX * NP // P], I32)
        H = NX // 2
        pR = [ps(f"r_pR{h}", [P, H, NT]) for h in range(2)]
        pC = [ps(f"r_pC{h}", [P, H, NT]) for h in range(2)]
        ramps, zero_set, zero_out, link_sem, both_ready, counted, delta_ready, exp_ready, slots_ready = map(
            sem, ["r_ramps", "r_zero_set", "r_zero_out", "r_link", "r_both", "r_counted", "r_delta_s", "r_exp", "r_slots"])
        list_in = sem("r_list_in")
        listed = [sem(f"r_listed{k}") for k in range(2)]
        block = ctx.enter_context(nc.Block())

        @block.sync
        def _(sp):
            sp.wait_ge(zero_set, 1)
            sp.dma_start(s.lists[0:NX * NP, :].rearrange("(p c) a -> p (c a)", p=P), zero[:, :]).then_inc(zero_out, 16)

        @block.gpsimd
        def _(pool):
            pool.iota(node_i[:, :], [[P, NT]], base=0, channel_multiplier=1).then_inc(ramps, 1)
            pool.iota(exp_i[:, :], [[1, NX]], base=0, channel_multiplier=0).then_inc(ramps, 1)
            pool.memset(zero[:, :], 0).then_inc(zero_set, 1)
            pool.wait_ge(zero_out, 16)
            pool.wait_ge(slots_ready, 1)
            for t in range(NT):
                for k in range(2):
                    if t:
                        pool.wait_ge(listed[k], 16 * t)
                    pool.indirect_dma_start(s.lists, bass.IndirectOffsetOnAxis(ap=s.slot[:, k, t:t + 1], axis=0), node_i[:, t:t + 1], None).then_inc(listed[k], 16)
            for k in range(2):
                pool.wait_ge(listed[k], 16 * NT)
            pool.dma_start(s.list[:, :, :], s.lists[0:NX * NP, :].rearrange("(e p c) a -> p e (c a)", e=NX, p=P)).then_inc(list_in, 16)
            pool.wait_ge(list_in, 16)

        @block.vector
        def _(dve):
            link = Link(dve, link_sem)
            tt = lambda o, a, b, op: link(dve.tensor_tensor(o, a, b, op))
            over_e = lambda a: a.rearrange("p (a t) -> p a t", a=1).broadcast_to([P, NX, NT])
            dve.tensor_tensor(delta[:, :], s.best[:, :, 1], s.best[:, :, 0], ALU.subtract).then_inc(delta_ready, 1)
            dve.wait_ge(exp_ready, 1)
            link(dve.tensor_scalar(den[:, :], ex[:, :], 1.0, None, ALU.add))
            link(dve.reciprocal(s.weight[:, :, 0], den[:, :]))
            tt(s.weight[:, :, 1], s.weight[:, :, 0], ex[:, :], ALU.mult)
            link(dve.tensor_copy(which_f[:, :, :], s.which[:, :, 0:2]))
            dve.wait_ge(ramps, 2)
            link(dve.tensor_copy(node_f[:, :], node_i[:, :]))
            link(dve.tensor_copy(exp_f[:, :], exp_i[:, :]))
            link(dve.tensor_scalar(valid[:, :], node_f[:, :], float(N), None, ALU.is_lt))
            for k in range(2):
                tt(hot[k][:, :, :], exp_f[:, :].rearrange("p (e a) -> p e a", a=1).broadcast_to([P, NX, NT]), over_e(which_f[:, :, k]), ALU.is_equal)
                tt(hot[k][:, :, :], hot[k][:, :, :], over_e(valid[:, :]), ALU.mult)
            link(dve.tensor_scalar(before[:, :], s.iota_f[:, :], s.iota_p[:, 0:1], None, ALU.is_gt))
            link(dve.memset(ones[:, :], 1.0))
            dve.tensor_tensor(both[:, :, :], hot[0][:, :, :], hot[1][:, :, :], ALU.add).then_inc(both_ready, 1)
            link(dve.memset(keep[:, :, :], 1.0))
            link(dve.memset(keep[:, :, 0:1], 0.0))
            dve.wait_ge(counted, 1)
            for h in range(2):
                e = slice(h * H, (h + 1) * H)
                link(dve.tensor_copy(picked[:, e, :], pC[h][:, :, :]))
            flat = lambda t: t[:, :, :].rearrange("p e t -> p (e t)")
            link(dve.tensor_tensor_scan(flat(incl), flat(keep), flat(picked), 0.0, ALU.mult, ALU.add))
            link(dve.tensor_scalar(turns_f[:, :], incl[:, :, NT - 1], float(XB - 1), float(XB), ALU.add, ALU.max))
            link(dve.tensor_copy(turns_i[:, :], turns_f[:, :]))
            link(dve.tensor_scalar(turns_i[:, :], turns_i[:, :], XB.bit_length() - 1, None, ALU.logical_shift_right))
            link(dve.tensor_copy(s.turns[:, :], turns_i[0:1, :]))
            link(dve.tensor_copy(turns_f[:, :], turns_i[:, :]))
            link(dve.memset(keep1[:, :], 1.0))
            link(dve.tensor_tensor_scan(ends[:, :], keep1[:, :], turns_f[:, :], 0.0, ALU.mult, ALU.add))
            link(dve.tensor_copy(s.total[:, :], ends[0:1, NX - 1:NX]))
            tt(ends[:, :], ends[:, :], turns_f[:, :], ALU.subtract)
            link(dve.tensor_copy(s.before[:, :], ends[0:1, :]))
            link(dve.tensor_scalar(ends[:, :], ends[:, :], float(XB), None, ALU.mult))
            tt(place[:, :, :], incl[:, :, :], picked[:, :, :], ALU.subtract)
            for h in range(2):
                e = slice(h * H, (h + 1) * H)
                tt(place[:, e, :], place[:, e, :], pR[h][:, :, :], ALU.add)
            for k in range(2):
                tt(picked[:, :, :], place[:, :, :], hot[k][:, :, :], ALU.mult)
                link(dve.tensor_reduce(rank[:, k, :], picked[:, :, :].rearrange("p e t -> p t e"), AX_X, ALU.add))
                tt(picked[:, :, :], hot[k][:, :, :], ends[:, :].rearrange("p (e a) -> p e a", a=1).broadcast_to([P, NX, NT]), ALU.mult)
                link(dve.tensor_reduce(begin[:, k, :], picked[:, :, :].rearrange("p e t -> p t e"), AX_X, ALU.add))
            link(dve.tensor_copy(rank_i[:, :, :], rank[:, :, :]))
            link(dve.tensor_scalar(digit_i[:, 0], rank_i[:, :, :], 7, None, ALU.logical_shift_right))
            link(dve.tensor_scalar(digit_i[:, 1], rank_i[:, :, :], P - 1, None, ALU.bitwise_and))
            link(dve.tensor_copy(digit[:, :], digit_i[:, :]))
            for k in range(2):
                link(dve.scalar_tensor_tensor(slot_f[:, k, :], digit[:, 1, k, :], float(NP // P), digit[:, 0, k, :], ALU.mult, ALU.add))
                link(dve.scalar_tensor_tensor(slot_f[:, k, :], which_f[:, :, k], float(NP), slot_f[:, k, :], ALU.mult, ALU.add))
                link(dve.tensor_scalar(away[:, k, :], node_f[:, :], float(NX * NP + k * NP), None, ALU.add))
                tt(slot_f[:, k, :], slot_f[:, k, :], away[:, k, :], ALU.subtract)
                tt(slot_f[:, k, :], slot_f[:, k, :], valid[:, :], ALU.mult)
                tt(slot_f[:, k, :], slot_f[:, k, :], away[:, k, :], ALU.add)
                tt(rank[:, k, :], rank[:, k, :], begin[:, k, :], ALU.add)
            link(dve.tensor_copy(s.result_row[:, :, :], rank[:, :, :]))
            dve.tensor_copy(s.slot[:, :, :], slot_f[:, :, :]).then_inc(slots_ready, 1)
        @block.scalar
        def _(act):
            act.wait_ge(delta_ready, 1)
            act.activation(ex[:, :], delta[:, :], ACT.Exp).then_inc(exp_ready, 1)

        @block.tensor
        def _(pe):
            pe.wait_ge(both_ready, 1)
            for h in range(2):
                of = both[:, h * H:(h + 1) * H, :].rearrange("p e t -> p (e t)")
                pe.matmul(pR[h][:, :, :].rearrange("p e t -> p (e t)"), before[:, :], of, start=True, stop=True)
                last = pe.matmul(pC[h][:, :, :].rearrange("p e t -> p (e t)"), ones[:, :], of, start=True, stop=True)
            last.then_inc(counted, 1)


def experts(s):
    nc = s.nc
    ctx, sb, ps, sem = scope(s)
    with ctx:
        B = XB // P
        w1 = sb("x_w1", [P, 2, DC, FF], F32)
        w2 = sb("x_w2", [P, 2, FC, D], F32)
        b1 = sb("x_b1", [P, 2, FC], F32)
        b2 = sb("x_b2", [P, 2, D], F32)
        index = sb("x_index", [P, B], I32)
        rows = sb("x_rows", [P, B, D], F32)
        xT = sb("x_xT", [P, DC, XB], F32)
        hid = sb("x_hid", [P, FC, XB], F32)
        res = sb("x_res", [P, B, D], F32)
        spare = sb("x_spare", [P, 2 * B + 1], F32)
        done = sb("x_done", [1, 1], F32)
        end = sb("x_end", [1, 1], F32)
        pT = [ps(f"x_pT{b}", [P, DC, P]) for b in range(B)]
        pH = [ps(f"x_pH{f}", [P, XB]) for f in range(FC)]
        pY = [ps(f"x_pY{b}", [P, D]) for b in range(B)]
        w_in = [sem(f"x_w_in{r}") for r in range(2)]
        row_in = [sem(f"x_row_in{b}") for b in range(B)]
        res_out = [sem(f"x_res_out{b}") for b in range(B)]
        w_used, rows_T, xT_ready, hid_done, hid_ready, y_done, res_ready, setup, taken = map(
            sem, ["x_w_used", "x_rows_T", "x_xT_ready", "x_hid_done", "x_hid_ready", "x_y_done", "x_res_ready", "x_setup", "x_taken"])
        copied = sem("x_copied")
        results = tiled(s.results)
        block = ctx.enter_context(nc.Block())

        def turns(engine, body, first=None, after=None, peeled=0):
            def two(pair):
                for r in range(2):
                    e = 2 * pair + r
                    if first is not None:
                        first(pair, r, e)
                    count = engine.value_load(s.turns[0:1, ds(e, 1)], min_val=1, max_val=NP // XB)
                    start = engine.value_load(s.before[0:1, ds(e, 1)], min_val=0, max_val=N_TURNS - 1)
                    with engine.Fori(0, count) as b:
                        turn = nc.s_assert_within(start + b, 0, N_TURNS - 1, skip_runtime_bounds_check_because="all experts' turns are at most N_TURNS")
                        body(e, r, b, turn)
                    if after is not None:
                        after(r, e, start + count)

            with engine.Fori(0, NX // 2 - peeled) as pair:
                two(pair)
            for pair in range(NX // 2 - peeled, NX // 2):
                two(pair)

        @block.sync
        def _(sp):
            def load(r, e):
                sp.dma_start(w1[:, r], s.w1[ds(e, 1), :, :].rearrange("a (c p) f -> p (a c) f", p=P)).then_inc(w_in[r], 16)
                sp.dma_start(w2[:, r], s.w2[ds(e, 1), :, :].rearrange("a (c p) f -> p (a c) f", p=P)).then_inc(w_in[r], 16)
                sp.dma_start(b1[:, r], s.b1[ds(e, 1), :].rearrange("a (c p) -> p (a c)", p=P), allow_slow_non_contiguous=True).then_inc(w_in[r], 16)
                sp.dma_start(b2[:, r], s.b2[ds(e, 1), :].broadcast_to([P, D])).then_inc(w_in[r], 16)

            def load_next(pair, r, e):
                if isinstance(e, int) and e + 1 == NX:
                    return
                sp.wait_ge(w_used, e + 1)
                load(1 - r, e + 1)

            def body(e, r, b, n):
                for q in range(B):
                    sp.wait_ge(res_ready, n * B + q + 1 + B)
                    sp.dma_start(results[ds(n * B + q, 1), :, :].rearrange("a p d -> p (a d)"), res[:, q, :]).then_inc(res_out[q], 16)
            load(0, 0)
            for q in range(B):
                prime(sp, s, res_out[q])
            turns(sp, body, load_next, peeled=1)

        @block.scalar
        def _(act):
            def first(pair, r, e):
                act.wait_ge(w_in[r], 64 * pair + 64)

            def body(e, r, b, n):
                for q in range(B):
                    act.wait_ge(rows_T, n * B + q + 1 + B)
                    act.activation(xT[:, :, q * P:(q + 1) * P], pT[q][:, :, :], ACT.Identity).then_inc(xT_ready, 1)
                for f in range(FC):
                    act.wait_ge(hid_done, n * FC + f + 1)
                    act.activation(hid[:, f, :], pH[f][:, :], ACT.Relu, bias=b1[:, r, f:f + 1]).then_inc(hid_ready, 1)
            turns(act, body, first)

        @block.gpsimd
        def _(pool):
            pool.memset(spare[:, :], 0.0).then_inc(setup, 1)
            pool.wait_ge(setup, 1)

            def body(e, r, b, n):
                for q in range(B):
                    pool.wait_ge(rows_T, n * B + q + 1)
                    pool.tensor_tensor(spare[:, 1 + q:2 + q], spare[:, 0:1], spare[:, 0:1], ALU.mult).then_inc(taken, 1)
                    pool.tensor_copy(index[:, q:q + 1], s.list[:, ds(e, 1), ds(b * B + q, 1)].rearrange("p a c -> p (a c)")).then_inc(copied, 1)
                    pool.wait_ge(copied, n * B + q + 1)
                    pool.wait_ge(taken, (n * B + q) * 2 + 1)
                    pool.tensor_tensor(spare[:, 1 + B + q:2 + B + q], spare[:, 0:1], spare[:, 0:1], ALU.mult).then_inc(taken, 1)
                    pool.indirect_dma_start(rows[:, q, :], None, s.h, bass.IndirectOffsetOnAxis(ap=index[:, q:q + 1], axis=0)).then_inc(row_in[q], 16)
            turns(pool, body)

        @block.tensor
        def _(pe):
            pe.sem_inc(rows_T, B)

            def first(pair, r, e):
                pe.wait_ge(w_in[r], 64 * pair + 64)

            def body(e, r, b, n):
                for q in range(B):
                    pe.wait_ge(row_in[q], 16 * n + 16)
                    for c in range(DC):
                        last = pe.transpose(pT[q][:, c, :], rows[:, q, c * P:(c + 1) * P], s.ident[:, :])
                    last.then_inc(rows_T, 1)
                pe.wait_ge(xT_ready, n * B + B)
                for f in range(FC):
                    for c in range(DC):
                        last = pe.matmul(pH[f][:, :], w1[:, r, c, f * P:(f + 1) * P], xT[:, c, :], start=(c == 0), stop=(c == DC - 1))
                    last.then_inc(hid_done, 1)
                for q in range(B):
                    pe.wait_ge(res_ready, n * B + q + 1)
                    for f in range(FC):
                        if q == 0:
                            pe.wait_ge(hid_ready, n * FC + f + 1)
                        last = pe.matmul(pY[q][:, :], hid[:, f, q * P:(q + 1) * P], w2[:, r, f, :], start=(f == 0), stop=(f == FC - 1))
                    last.then_inc(y_done, 1)
            turns(pe, body, first)

        @block.vector
        def _(dve):
            dve.sem_inc(res_ready, B)
            dve.sem_inc(w_used, 1)

            def first(pair, r, e):
                dve.wait_ge(w_in[r], 64 * pair + 64)

            def body(e, r, b, n):
                for q in range(B):
                    dve.wait_ge(y_done, n * B + q + 1)
                    dve.wait_ge(res_out[q], 16 * n + 16)
                    dve.tensor_tensor(res[:, q, :], pY[q][:, :], b2[:, r, :], ALU.add).then_inc(res_ready, 1)
            def after(r, e, n):
                dve.wait_ge(res_ready, n * B + B)
                dve.wait_ge(w_used, e + 1)
                dve.memset(done[:, :], 0.0).then_inc(w_used, 1)
            turns(dve, body, first, after)
            total = dve.value_load(s.total[0:1, 0:1], min_val=NX, max_val=N_TURNS)
            for q in range(B):
                dve.wait_ge(res_out[q], total * 16 + 16)
            dve.memset(end[:, :], 0.0)


def final_norm(s):
    nc = s.nc
    ctx, sb, ps, sem = scope(s)
    with ctx:
        x1 = sb("f_x1", [P, 2, D], F32)
        h = sb("f_h", [P, 2, D], F32)
        res = sb("f_res", [P, 2, 2, D], F32)
        index = sb("f_index", [P, 2, 2], I32)
        y = sb("f_y", [P, 2, D], F32)
        o = sb("f_o", [P, 2, D], F32)
        scale = sb("f_gamma", [P, D], F32)
        shift = sb("f_beta", [P, D], F32)
        stats = sb("f_stats", [P, 2, 6], F32)
        mv = sb("f_mv", [P, 2, 2], F32)
        std = sb("f_std", [P, 2, 1], F32)
        rstd = sb("f_rstd", [P, 2, 1], F32)
        eps = sb("f_eps", [P, 1], F32)
        spare = sb("f_spare", [P, 3], F32)
        spare2 = sb("f_spare2", [P, 1], F32)
        row_in = [[sem(f"f_row_in{j}{k}") for k in range(2)] for j in range(2)]
        x1_in = [sem(f"f_x1_in{j}") for j in range(2)]
        h_in = [sem(f"f_h_in{j}") for j in range(2)]
        out_out = [sem(f"f_out{j}") for j in range(2)]
        gb_in, eps_set, index_ready, y_ready, mv_ready, std_ready, o_ready, link_sem, taken, setup = map(
            sem, ["f_gb_in", "f_eps_set", "f_index_ready", "f_y", "f_mv", "f_std_s", "f_o_ready", "f_link", "f_taken", "f_setup"])
        x1_t, h_t, out_t = tiled(s.x1), tiled(s.h), tiled(s.out)
        tile = lambda a, k: a[ds(k, 1), :, :].rearrange("a p d -> p (a d)")
        block = ctx.enter_context(nc.Block())

        @block.sync
        def _(sp):
            sp.dma_start(scale[:, :], s.gamma.rearrange("(a d) -> a d", a=1).broadcast_to([P, D])).then_inc(gb_in, 16)
            sp.dma_start(shift[:, :], s.beta.rearrange("(a d) -> a d", a=1).broadcast_to([P, D])).then_inc(gb_in, 16)
            with sp.Fori(0, NT // 2) as i:
                for j in range(2):
                    k = 2 * i + j
                    sp.wait_ge(y_ready, k + 1)
                    sp.dma_start(h[:, j, :], tile(h_t, k)).then_inc(h_in[j], 16)
                    sp.wait_ge(o_ready, k + 1)
                    sp.dma_start(x1[:, j, :], tile(x1_t, k)).then_inc(x1_in[j], 16)

        @block.scalar
        def _(act):
            act.wait_ge(eps_set, 1)
            for j in range(2):
                prime(act, s, out_out[j])

            def index_of(k, j):
                act.wait_ge(y_ready, k + 1)
                act.wait_ge(taken, k + 1)
                act.activation(index[:, j, :], s.result_row[:, :, ds(k, 1)].rearrange("p e a -> p (e a)"), ACT.Copy).then_inc(index_ready, 1)
            with act.Fori(0, NT // 2) as i:
                for j in range(2):
                    k = 2 * i + j
                    index_of(k, j)
                for j in range(2):
                    k = 2 * i + j
                    act.wait_ge(mv_ready, k + 1)
                    act.activation(std[:, j, :], mv[:, j, 1:2], ACT.Sqrt, bias=eps[:, 0:1]).then_inc(std_ready, 1)
                    act.wait_ge(o_ready, k + 3)
                    act.dma_start(tile(out_t, k), o[:, j, :]).then_inc(out_out[j], 16)
            for j in range(2):
                act.wait_ge(out_out[j], 16 * (NT // 2 + 1))

        @block.gpsimd
        def _(pool):
            pool.sem_inc(taken, 2)
            pool.memset(spare[:, :], 0.0).then_inc(setup, 1)
            pool.wait_ge(setup, 1)
            with pool.Fori(0, NT // 2) as i:
                for j in range(2):
                    k = 2 * i + j
                    pool.wait_ge(index_ready, k + 1)
                    pool.tensor_tensor(spare[:, 1 + j:2 + j], spare[:, 0:1], spare[:, 0:1], ALU.mult).then_inc(taken, 1)
                    for e in range(2):
                        pool.indirect_dma_start(res[:, j, e, :], None, s.results, bass.IndirectOffsetOnAxis(ap=index[:, j, e:e + 1], axis=0)).then_inc(row_in[j][e], 16)

        @block.vector
        def _(dve):
            link = Link(dve, link_sem)
            dve.sem_inc(y_ready, 2)
            dve.sem_inc(o_ready, 2)
            dve.memset(eps[:, :], LN_EPS).then_inc(eps_set, 1)
            dve.wait_ge(gb_in, 32)
            with dve.Fori(0, NT // 2) as i:
                link.loop(i, 2 * 6)
                for j in range(2):
                    k = 2 * i + j
                    dve.wait_ge(h_in[j], 16 * i + 16)
                    for e in range(2):
                        dve.wait_ge(row_in[j][e], 16 * i + 16)
                    w = lambda e: s.weight[:, ds(k, 1), e:e + 1].rearrange("p a e -> p (a e)")
                    link(dve.scalar_tensor_tensor(y[:, j, :], res[:, j, 0, :], w(0), h[:, j, :], ALU.mult, ALU.add))
                    dve.scalar_tensor_tensor(y[:, j, :], res[:, j, 1, :], w(1), y[:, j, :], ALU.mult, ALU.add).then_inc(y_ready, 1)
                    dve.wait_ge(y_ready, k + 3)
                    link(dve.bn_stats(stats[:, j, :], y[:, j, :]))
                    dve.memset(spare2[:, :], 0.0)
                    dve.bn_aggr(mv[:, j, :], stats[:, j, :]).then_inc(mv_ready, 1)
                    dve.wait_ge(std_ready, k + 1)
                    link(dve.reciprocal(rstd[:, j, :], std[:, j, :]))
                    dve.wait_ge(out_out[j], 16 * i + 16)
                    link(dve.tensor_scalar(o[:, j, :], y[:, j, :], mv[:, j, 0:1], rstd[:, j, 0:1], ALU.subtract, ALU.mult))
                    link(dve.tensor_tensor(o[:, j, :], o[:, j, :], scale[:, :], ALU.mult))
                    link(dve.tensor_tensor(o[:, j, :], o[:, j, :], shift[:, :], ALU.add))
                    dve.wait_ge(x1_in[j], 16 * i + 16)
                    dve.tensor_tensor(o[:, j, :], o[:, j, :], x1[:, j, :], ALU.add).then_inc(o_ready, 1)


def laid_out(x, src, dst, edge_attr_64, L0_gnn_W, L0_gnn_A, L0_mix_kln_weight, L0_mix_kln_bias, L0_mix_vln_weight,
             L0_mix_vln_bias, L0_ffn_gate_w, L0_ffn_gate_b, L0_ffn_w1, L0_ffn_b1, L0_ffn_w2, L0_ffn_b2, L0_ffn_gamma, L0_ffn_beta):
    import numpy as np

    def padded(a, rows, fill=0):
        a = np.asarray(a)
        return np.concatenate([a, np.full((rows - a.shape[0],) + a.shape[1:], fill, a.dtype)])

    named = dict(
        x=padded(x, NP), src=padded(src, EP), dst=padded(dst, EP, N), edge_attr=padded(edge_attr_64, EP), W=L0_gnn_W, A=L0_gnn_A,
        kw=L0_mix_kln_weight, kb=L0_mix_kln_bias, vw=L0_mix_vln_weight, vb=L0_mix_vln_bias,
        gate_w=L0_ffn_gate_w, gate_b=L0_ffn_gate_b, w1=L0_ffn_w1, b1=L0_ffn_b1, w2=L0_ffn_w2, b2=L0_ffn_b2,
        gamma=L0_ffn_gamma, beta=L0_ffn_beta)
    return {f"in_{k}": np.ascontiguousarray(v) for k, v in named.items()}


def kernel(**inputs):
    import numpy as np
    import concourse.bacc as bacc
    from concourse.bass_utils import run_bass_kernel_spmd

    nc = bacc.Bacc("TRN2", target_bir_lowering=False, num_devices=1)
    arrays = laid_out(**inputs)
    args = [nc.dram_tensor(name, a.shape, mybir.dt.from_np(a.dtype), kind="ExternalInput").ap() for name, a in arrays.items()]
    args.append(nc.dram_tensor("out_rows", (NP, D), F32, kind="ExternalOutput").ap())
    build(nc, *args)
    r = run_bass_kernel_spmd(nc, [arrays], core_ids=[0])
    return np.asarray(r.results[0]["out_rows"])[:N]
```

```python
from contextlib import ExitStack

import concourse.bass as bass
from concourse import mybir

F32 = mybir.dt.float32
BF16 = mybir.dt.bfloat16
I32 = mybir.dt.int32
ALU = mybir.AluOpType
ACT = mybir.ActivationFunctionType
AX_X = mybir.AxisListType.X
DVE = mybir.EngineType.DVE
ds = bass.ds

P = 128
N, D, E, ED = 6250, 256, 100000, 64
HEADS, HC = 8, 32
NX, FF = 16, 512
DC, FC = D // P, FF // P
NT = 49
NP = NT * P
G = 7
ET = 784
EP = ET * P
RG = 7
RP = ET // RG
TC = 8
GU = 16
XB = 256
N_TURNS = (2 * N + NX * (XB - 1)) // XB + 1
ZERO_DMAS = 13
XL = -(-(N + XB) // P) * P
AWAY = NX * XL
LN_EPS = 1e-5
HEAD_EPS = 1e-5
SLOPE = 0.2
BIG = 1e30


class Link:

    def __init__(self, engine, semaphore, start=0):
        self.engine, self.semaphore, self.start = engine, semaphore, start
        self.count, self.turn, self.per = 0, None, 0

    def loop(self, turn, per):
        self.start += self.count
        self.turn, self.per, self.count = turn, per, 0

    def end_loop(self, turns):
        assert self.count == self.per, (self.count, self.per)
        self.start += turns * self.per
        self.turn, self.count = None, 0

    def __call__(self, ins):
        self.count += 1
        ins.then_inc(self.semaphore, 1)
        at = self.start + self.count
        if self.turn is not None:
            at = self.turn * self.per + at
        self.engine.wait_ge(self.semaphore, at)


def before(q, slots, per=G):
    if q >= slots:
        return slots
    return per - max(u for u in range(per) if u % slots == q % slots) + q


def prime(engine, s, semaphore):
    cell = s.prime[0:1, s.primed:s.primed + 1]
    s.primed += 1
    engine.dma_start(cell, s.gate_b[0:1].rearrange("(a b) -> a b", a=1)).then_inc(semaphore, 16)


def tiled(ap):
    return ap.rearrange("(t p) d -> t p d", p=P)


class Store:
    pass


def build(nc, x, src, dst, edge_attr, W, A, kw, kb, vw, vb, gate_w, gate_b, w1, b1, w2, b2, gamma, beta, out):
    s = Store()
    s.nc = nc
    s.x, s.src, s.dst, s.edge_attr, s.W, s.A = x, src, dst, edge_attr, W, A
    s.kw, s.kb, s.vw, s.vb = kw, kb, vw, vb
    s.gate_w, s.gate_b, s.w1, s.b1, s.w2, s.b2, s.gamma, s.beta, s.out = gate_w, gate_b, w1, b1, w2, b2, gamma, beta, out
    s.xn = nc.dram_tensor("xn_rows", (NP, D), F32, kind="Internal").ap()
    s.x1 = nc.dram_tensor("x1_rows", (NP, D), F32, kind="Internal").ap()
    s.lows = nc.dram_tensor("low_digits", (1, 2, EP), BF16, kind="Internal").ap()
    s.ea = nc.dram_tensor("edge_logits", (EP,), F32, kind="Internal").ap()
    s.h = nc.dram_tensor("h_rows", (NP, D), F32, kind="Internal").ap()
    s.sorted = nc.dram_tensor("rows_by_expert", (AWAY + 2 * P, D), F32, kind="Internal").ap()
    s.results = nc.dram_tensor("results", (N_TURNS * XB, D), F32, kind="Internal").ap()
    s.bounce = nc.dram_tensor("row_ends", (8, ET, 2), F32, kind="Internal").ap()
    with ExitStack() as ctx:
        sb = lambda name, shape, dt: ctx.enter_context(nc.sbuf_tensor(name, shape, dt))
        s.semaphores = []
        s.prime, s.primed = sb("prime", [1, 16], F32), 0
        s.ident = sb("ident", [P, P], F32)
        s.iota_f = sb("iota_f", [P, P], F32)
        s.iota_p = sb("iota_p", [P, 1], F32)
        s.WT = sb("WT", [P, DC, D], F32)
        s.wsd = sb("wsd", [P, DC, 2], F32)
        s.KV = sb("KV", [P, DC, P], F32)
        s.blockmask = sb("blockmask", [P, P], F32)
        s.agg = sb("agg", [P, DC, NP + P], F32)
        with ExitStack() as edge_ctx:
            eb = lambda name, shape, dt: edge_ctx.enter_context(nc.sbuf_tensor(name, shape, dt))
            s.score_bits = eb("score_bits", [P, 2, 3, NT], BF16)
            s.high = eb("high", [P, 2, ET], BF16)
            s.edge_score = eb("edge_score", [P, 2, ET], F32)
            s.srcT = eb("srcT", [P, ET], I32)
            s.relT = eb("relT", [P, ET], F32)
            s.alphaT = eb("alphaT", [P, ET], F32)
            s.base = eb("base", [1, ET], I32)
            s.windows = eb("windows", [1, 1], I32)
            s.dst_f = eb("dst_f", [RP, RG, P], F32)
            constants(s)
            node_scores(s)
            edge_digits(s)
            table_lookup(s)
            edge_softmax(s)
            aggregate(s)
        nc.clear_and_free_semaphores(s.semaphores)
        nc.all_engine_barrier()
        s.semaphores = []
        s.best = sb("best", [P, NT, 2], F32)
        s.weight = sb("weight", [P, NT, 2], F32)
        s.result_row = sb("result_row", [P, 2, NT], I32)
        s.count = sb("count", [1, NX], I32)
        s.turns = sb("turns", [1, NX], I32)
        s.before = sb("before", [1, NX], I32)
        s.total = sb("total", [1, 1], I32)
        node_update(s)
        experts(s)
        final_norm(s)
        nc.clear_and_free_semaphores(s.semaphores)


def scope(s):
    ctx = ExitStack()
    sb = lambda name, shape, dt: ctx.enter_context(s.nc.sbuf_tensor(name, shape, dt))
    ps = lambda name, shape, dt=F32: ctx.enter_context(s.nc.psum_tensor(name, shape, dt))

    def sem(name):
        s.semaphores.append(s.nc.alloc_semaphore(name))
        return s.semaphores[-1]
    return ctx, sb, ps, sem


def constants(s):
    nc = s.nc
    ctx, sb, ps, sem = scope(s)
    with ctx:
        w_sb = sb("w_sb", [P, DC, D], F32)
        a_sb = sb("a_sb", [P, DC, 2], F32)
        fi = sb("fi", [P, P], I32)
        pi = sb("pi", [P, 1], I32)
        fb = sb("fb", [P, P], I32)
        pb = sb("pb", [P, 1], I32)
        fbf = sb("fbf", [P, P], F32)
        pbf = sb("pbf", [P, 1], F32)
        pT = [ps(f"pT{c}", [P, DC, P]) for c in range(DC)]
        pw = ps("pw", [P, DC, 2])
        w_loaded, ramps, const_link, ident_ready, wT_ready, wsd_ready = map(
            sem, ["c_w_loaded", "c_ramps", "c_link", "c_ident", "c_wT", "c_wsd"])
        block = ctx.enter_context(nc.Block())

        @block.sync
        def _(sp):
            sp.dma_start(w_sb[:, :, :], s.W.rearrange("(c p) i -> p c i", p=P)).then_inc(w_loaded, 16)
            for k in range(2):
                for c in range(DC):
                    sp.dma_start(a_sb[:, c, k:k + 1], s.A[0, k * D + c * P:k * D + (c + 1) * P].rearrange("(p a) -> p a", a=1),
                                 allow_slow_non_contiguous=True).then_inc(w_loaded, 16)

        @block.gpsimd
        def _(pool):
            pool.iota(fi[:, :], [[1, P]], base=0, channel_multiplier=0).then_inc(ramps, 1)
            pool.iota(pi[:, :], [[0, 1]], base=0, channel_multiplier=1).then_inc(ramps, 1)

        @block.vector
        def _(dve):
            link = Link(dve, const_link)
            dve.wait_ge(ramps, 2)
            dve.tensor_copy(s.iota_f[:, :], fi[:, :])
            link(dve.tensor_copy(s.iota_p[:, :], pi[:, :]))
            dve.tensor_scalar(s.ident[:, :], s.iota_f[:, :], s.iota_p[:, 0:1], None, ALU.is_equal).then_inc(ident_ready, 1)
            shift = HC.bit_length() - 1
            link(dve.tensor_scalar(fb[:, :], fi[:, :], shift, None, ALU.logical_shift_right))
            link(dve.tensor_scalar(pb[:, :], pi[:, :], shift, None, ALU.logical_shift_right))
            link(dve.tensor_copy(fbf[:, :], fb[:, :]))
            link(dve.tensor_copy(pbf[:, :], pb[:, :]))
            link(dve.tensor_scalar(s.blockmask[:, :], fbf[:, :], pbf[:, 0:1], None, ALU.is_equal))
            dve.wait_ge(wT_ready, 2 * DC)
            for c in range(DC):
                dve.tensor_copy(s.WT[:, c, :].rearrange("p (o q) -> p o q", o=DC), pT[c][:, :, :])
            dve.wait_ge(wsd_ready, 1)
            dve.tensor_copy(s.wsd[:, :, :], pw[:, :, :])

        @block.tensor
        def _(pe):
            pe.wait_ge(w_loaded, 16 * (1 + 2 * DC))
            pe.wait_ge(ident_ready, 1)
            for c in range(DC):
                for o in range(DC):
                    pe.transpose(pT[c][:, o, :], w_sb[:, o, c * P:(c + 1) * P], s.ident[:, :]).then_inc(wT_ready, 1)
            for c in range(DC):
                for o in range(DC):
                    last = pe.matmul(pw[:, c, :], w_sb[:, o, c * P:(c + 1) * P], a_sb[:, o, :], start=(o == 0), stop=(o == DC - 1))
            last.then_inc(wsd_ready, 1)


def node_scores(s):
    nc = s.nc
    ctx, sb, ps, sem = scope(s)
    with ctx:
        TURNS = NT // G
        EC = ET // NT
        EB = 2 * ED
        HC2 = EC // 2
        PAIRS = HC2 // 2
        MID = G // 2 + 1
        xt = sb("xt", [P, G, D], F32)
        stats = sb("stats", [P, G, 6], F32)
        mv = sb("mv", [P, G, 2], F32)
        std = sb("a_std", [P, G], F32)
        rstd = sb("rstd", [P, G], F32)
        xn = sb("xn", [P, G, D], F32)
        xnT = sb("xnT", [P, 2, DC, P], F32)
        spare = sb("a_spare", [P, 1], F32)
        eps = sb("a_eps", [P, 1], F32)
        score = sb("score", [P, 2, NT], F32)
        rest = sb("rest", [P, 2, NT], F32)
        piece = sb("piece", [P, 2, NT], F32)
        attr = sb("a_attr", [P, G, EC * ED], F32)
        attrT = sb("a_attrT", [P, 2, PAIRS, P], F32)
        a_row = sb("a_a_row", [P, ED], F32)
        prod = sb("a_prod", [P, HC2, ED], F32)
        a_e = sb("a_a_e", [EB, 2], F32)
        ea = sb("a_ea", [P, ET], F32)
        pT = [ps(f"a_pT{j}", [P, DC, P]) for j in range(2)]
        pS = ps("a_pS", [P, 2 * NT])
        pEA = ps("a_pEA", [P, ET // 2])
        pE = [ps(f"a_pE{j}", [P, PAIRS, P]) for j in range(2)]
        x_in = [sem(f"a_x_in{q}") for q in range(G)]
        attr_in = [sem(f"a_attr_in{q}") for q in range(G)]
        x_used, xn_out, xnT_done, xnT_copied, score_done, mv_ready, std_ready, eps_set, link_sem = map(
            sem, ["a_x_used", "a_xn_out", "a_xnT_done", "a_xnT_copied", "a_score_done", "a_mv", "a_std_ready", "a_eps_set", "a_link"])
        a_in, a_zero, attrT_done, attrT_copied, ea_done, ea_ready, ea_out = map(
            sem, ["a_a_in", "a_a_zero", "a_attrT_done", "a_attrT_copied", "a_ea_done", "a_ea_ready", "a_ea_out"])
        prod_ready, dot_done = map(sem, ["a_prod_ready", "a_dot_done"])
        x_t = tiled(s.x)
        xn_g = s.xn.rearrange("(i q p) d -> i p q d", q=G, p=P)
        attr_c = s.edge_attr.rearrange("(p c) d -> p (c d)", p=P)
        block = ctx.enter_context(nc.Block())

        @block.sync
        def _(sp):
            sp.wait_ge(a_zero, 1)
            for k in range(2):
                sp.dma_start(a_e[k * ED:(k + 1) * ED, k:k + 1], s.A[0, 2 * D:2 * D + ED].rearrange("(p a) -> p a", a=1),
                             allow_slow_non_contiguous=True).then_inc(a_in, 16)
            sp.dma_start(a_row[:, :], s.A[0:1, 2 * D:2 * D + ED].broadcast_to([P, ED])).then_inc(a_in, 16)
            with sp.Fori(0, TURNS) as i:
                for q in range(G):
                    k = i * G + q
                    sp.wait_ge(x_used, k + 1)
                    sp.dma_start(xt[:, q, :], x_t[ds(k, 1), :, :].rearrange("a p d -> p (a d)")).then_inc(x_in[q], 16)
            sp.wait_ge(ea_ready, 1)
            sp.dma_start(s.ea.rearrange("(p c) -> p c", p=P), ea[:, :]).then_inc(ea_out, 16)
            sp.wait_ge(ea_out, 16)

        @block.gpsimd
        def _(pool):
            pool.memset(a_e[:, :], 0.0).then_inc(a_zero, 1)
            with pool.Fori(0, TURNS) as i:
                for q in range(G):
                    k = i * G + q
                    pool.wait_ge(attrT_done, k + 1)
                    pool.wait_ge(dot_done, k + 1)
                    pool.dma_start(attr[:, q, :], attr_c[:, ds(k * (EC * ED), EC * ED)]).then_inc(attr_in[q], 16)

        @block.vector
        def _(dve):
            link = Link(dve, link_sem)
            dve.sem_inc(x_used, G)
            dve.memset(eps[:, :], LN_EPS).then_inc(eps_set, 1)

            def statistics(i):
                for q in range(G):
                    dve.wait_ge(x_in[q], 16 * i + 16)
                    last = dve.bn_stats(stats[:, q, :], xt[:, q, :])
                link(last)
                dve.memset(spare[:, :], 0.0)
                for q in range(G):
                    last = dve.bn_aggr(mv[:, q, :], stats[:, q, :])
                last.then_inc(mv_ready, 1)

            def norm(i):
                dve.wait_ge(std_ready, i + 1)
                link(dve.reciprocal(rstd[:, :], std[:, :]))
                dve.wait_ge(xn_out, 16 * i + 16)
                for q in range(G):
                    dve.wait_ge(xnT_done, i * G + q + 1)
                    dve.tensor_scalar(xn[:, q, :], xt[:, q, :], mv[:, q, 0:1], rstd[:, q:q + 1], ALU.subtract, ALU.mult).then_inc(x_used, 1)
                dve.wait_ge(x_used, (i + 2) * G)

            def dots(i, tiles):
                for q in tiles:
                    k = i * G + q
                    dve.wait_ge(attr_in[q], 16 * i + 16)
                    dve.wait_ge(dot_done, k + G)
                    dve.tensor_tensor(prod[:, :, :], attr[:, q, HC2 * ED:].rearrange("p (c d) -> p c d", d=ED),
                                      a_row[:, :].rearrange("p (a d) -> p a d", a=1).broadcast_to([P, HC2, ED]), ALU.mult).then_inc(prod_ready, 1)
                    dve.wait_ge(prod_ready, k + 1)
                    dve.tensor_reduce(ea[:, ds(k * EC + HC2, HC2)], prod[:, :, :], AX_X, ALU.add).then_inc(dot_done, 1)

            dve.sem_inc(dot_done, G)
            dve.wait_ge(a_in, 48)
            statistics(0)
            with dve.Fori(0, TURNS - 1) as i:
                link.loop(i, 2)
                norm(i)
                dots(i, range(MID))
                statistics(i + 1)
                dots(i, range(MID, G))
            link.end_loop(TURNS - 1)
            norm(TURNS - 1)
            dots(TURNS - 1, range(G))
            dve.wait_ge(ea_done, NT + G)
            dve.wait_ge(dot_done, NT + G)
            dve.tensor_copy(ea[:, :].rearrange("p (t c) -> p t c", c=EC)[:, :, 0:HC2], pEA[:, :].rearrange("p (t c) -> p t c", c=HC2)).then_inc(ea_ready, 1)
            dve.wait_ge(score_done, NT + G)
            link(dve.tensor_copy(score[:, :, :], pS[:, :].rearrange("p (t k) -> p k t", k=2)))
            for m in range(3):
                frm = score if m == 0 else rest
                link(dve.tensor_copy(s.score_bits[:, :, m, :], frm[:, :, :]))
                link(dve.tensor_copy(piece[:, :, :], s.score_bits[:, :, m, :]))
                link(dve.tensor_tensor(rest[:, :, :], frm[:, :, :], piece[:, :, :], ALU.subtract))

        @block.scalar
        def _(act):
            act.wait_ge(eps_set, 1)
            act.sem_inc(xnT_copied, G)
            act.sem_inc(attrT_copied, G)
            prime(act, s, xn_out)

            def root(i):
                act.wait_ge(mv_ready, i + 1)
                act.activation(std[:, :], mv[:, :, 1], ACT.Sqrt, bias=eps[:, 0:1]).then_inc(std_ready, 1)

            def turn(i, root_of_next):
                for q in range(G):
                    k = i * G + q
                    if q == MID:
                        act.wait_ge(x_used, (i + 2) * G)
                        act.dma_start(xn_g[ds(i, 1)].rearrange("a p q d -> p (a q) d"), xn[:, :, :]).then_inc(xn_out, 16)
                        if root_of_next:
                            root(i + 1)
                    act.wait_ge(attrT_done, k + 1 + G)
                    act.wait_ge(ea_done, k + G + 1 - before(q, 2))
                    act.activation(attrT[:, q % 2], pE[q % 2][:, :, :], ACT.Identity).then_inc(attrT_copied, 1)
                    act.wait_ge(xnT_done, k + 1 + G)
                    act.wait_ge(score_done, k + G + 1 - before(q, 2))
                    act.activation(xnT[:, q % 2, :, :], pT[q % 2][:, :, :], ACT.Identity).then_inc(xnT_copied, 1)

            root(0)
            with act.Fori(0, TURNS - 1) as i:
                turn(i, True)
            turn(TURNS - 1, False)
            act.wait_ge(xn_out, 16 * (TURNS + 1))

        @block.tensor
        def _(pe):
            pe.sem_inc(xnT_done, G)
            pe.sem_inc(attrT_done, G)
            pe.sem_inc(score_done, G)
            pe.sem_inc(ea_done, G)
            pe.wait_ge(a_in, 48)
            with pe.Fori(0, TURNS) as i:
                def turn_in(q):
                    k = i * G + q
                    pe.wait_ge(attr_in[q], 16 * i + 16)
                    pe.wait_ge(attrT_copied, k + G + 1 - before(q, 2))
                    for m in range(PAIRS):
                        last = pe.transpose(pE[q % 2][:, m, :], attr[:, q, m * EB:(m + 1) * EB], s.ident[:, :])
                    last.then_inc(attrT_done, 1)
                    pe.wait_ge(x_used, k + 1 + G)
                    pe.wait_ge(xnT_copied, k + G + 1 - before(q, 2))
                    for c in range(DC):
                        last = pe.transpose(pT[q % 2][:, c, :], xn[:, q, c * P:(c + 1) * P], s.ident[:, :])
                    last.then_inc(xnT_done, 1)

                def products(q):
                    k = i * G + q
                    pe.wait_ge(attrT_copied, k + 1 + G)
                    for m in range(PAIRS):
                        last = pe.matmul(pEA[:, ds(k * HC2 + m * 2, 2)], attrT[:, q % 2, m, :], a_e[:, :], start=True, stop=True)
                    last.then_inc(ea_done, 1)
                    pe.wait_ge(xnT_copied, k + G + 1)
                    for c in range(DC):
                        last = pe.matmul(pS[:, ds(k * 2, 2)], xnT[:, q % 2, c, :], s.wsd[:, c, :], start=(c == 0), stop=(c == DC - 1))
                    last.then_inc(score_done, 1)
                turn_in(0)
                for q in range(1, G):
                    turn_in(q)
                    products(q - 1)
                products(G - 1)


def edge_digits(s):
    nc = s.nc
    ctx, sb, ps, sem = scope(s)
    with ctx:
        rows = sb("d_rows", [RP, 2, RG, P], I32)
        digit = sb("d_digit", [RP, 2, 2, RG, P], I32)
        high_f = sb("d_high_f", [RP, 2, RG, P], F32)
        low_b = sb("d_low_b", [RP, 2, RG, P], BF16)
        src_f = sb("d_src_f", [RP, RG, P], F32)
        HALF = 4
        pT = [[ps(f"d_pT{k}{h}", [P, HALF, RP]) for h in range(2)] for k in range(3)]
        rows_in, link_sem, low_ready, low_out, f_ready, T_done, base_in = map(
            sem, ["d_rows_in", "d_link", "d_low", "d_low_out", "d_f_ready", "d_T", "d_base_in"])
        block = ctx.enter_context(nc.Block())
        by_row = lambda a: a.rearrange("(g p e) -> p g e", p=RP, e=P)

        @block.sync
        def _(sp):
            sp.dma_start(rows[:, 0, :, :], by_row(s.src)).then_inc(rows_in, 16)
            sp.dma_start(rows[:, 1, :, :], by_row(s.dst)).then_inc(rows_in, 16)
            sp.dma_start(s.base[:, :], s.dst.rearrange("(a t e) -> a t e", a=1, e=P)[:, :, 0], allow_slow_non_contiguous=True).then_inc(base_in, 16)
            sp.wait_ge(low_ready, 1)
            for k in range(2):
                sp.dma_start(by_row(s.lows[0, k, :]), low_b[:, k, :, :]).then_inc(low_out, 16)
            sp.wait_ge(low_out, 32)
            sp.wait_ge(base_in, 16)

        @block.vector
        def _(dve):
            link = Link(dve, link_sem)
            dve.wait_ge(rows_in, 32)
            link(dve.tensor_scalar(digit[:, 0], rows[:, :], 7, None, ALU.logical_shift_right))
            link(dve.tensor_scalar(digit[:, 1], rows[:, :], P - 1, None, ALU.bitwise_and))
            dve.tensor_copy(low_b[:, :], digit[:, 1]).then_inc(low_ready, 1)
            dve.tensor_copy(high_f[:, :], digit[:, 0]).then_inc(f_ready, 1)
            dve.tensor_copy(src_f[:, :], rows[:, 0]).then_inc(f_ready, 1)
            dve.tensor_copy(s.dst_f[:, :], rows[:, 1]).then_inc(f_ready, 1)
            dve.wait_ge(T_done, 1)
            for k in range(3):
                for h in range(2):
                    n = min(HALF, RG - HALF * h)
                    to = (s.high[:, k, :] if k < 2 else s.srcT[:, :])[:, HALF * h * RP:(HALF * h + n) * RP]
                    dve.tensor_copy(to.rearrange("p (g r) -> p g r", g=n), pT[k][h][:, 0:n, :])

        @block.tensor
        def _(pe):
            pe.wait_ge(f_ready, 3)
            for k in range(3):
                for g in range(RG):
                    of = high_f[:, k, g, :] if k < 2 else src_f[:, g, :]
                    last = pe.transpose(pT[k][g // HALF][:, g % HALF, :], of, s.ident[0:RP, 0:RP])
            last.then_inc(T_done, 1)


def table_lookup(s):
    nc = s.nc
    ctx, sb, ps, sem = scope(s)
    with ctx:
        low = sb("t_low", [P, 2, 2, TC * P], BF16)
        onehot = sb("t_onehot", [P, 2, 2, TC * P], BF16)
        ramp = sb("t_ramp", [P, NT], BF16)
        far = sb("t_far", [P, 2, TC * P], BF16)
        neg_p = sb("t_neg_p", [P, 1], F32)
        one = sb("t_one", [P, 1], F32)
        off = sb("t_off", [P, 2, 2, TC, NT], BF16)
        picked = sb("t_picked", [P, 2, 2, TC, NT], F32)
        pR = [[ps(f"t_pR{j}{k}", [P, TC, NT]) for k in range(2)] for j in range(2)]
        low_in = [sem(f"t_low_in{j}") for j in range(2)]
        low_used, low_far, far_ready, hot_ready, rows_done, bias_set = map(sem, ["t_low_used", "t_low_far", "t_far_ready", "t_hot_ready", "t_rows", "t_bias_set"])
        off_ready, picked_ready, summed, ramp_ready = map(sem, ["t_off", "t_picked", "t_summed", "t_ramp_s"])
        block = ctx.enter_context(nc.Block())
        TURNS = ET // TC // 2

        @block.sync
        def _(sp):
            with sp.Fori(0, TURNS) as i:
                for j in range(2):
                    k = 2 * i + j
                    sp.wait_ge(low_used, k + 1)
                    sp.wait_ge(low_far, k + 1)
                    sp.dma_start(low[:, j, :, :], s.lows[:, :, ds(k * (TC * P), TC * P)].broadcast_to([P, 2, TC * P])).then_inc(low_in[j], 16)

        @block.gpsimd
        def _(pool):
            pool.tensor_copy(ramp[:, :], s.iota_f[:, 0:NT]).then_inc(ramp_ready, 1)
            pool.wait_ge(ramp_ready, 1)
            with pool.Fori(0, TURNS) as i:
                for j in range(2):
                    k = 2 * i + j
                    pool.wait_ge(picked_ready, 2 * k + 2)
                    for q in range(2):
                        pool.tensor_tensor(
                            off[:, j, q], ramp[:, :].rearrange("p (a n) -> p a n", a=1).broadcast_to([P, TC, NT]),
                            s.high[:, q, ds(k * TC, TC)].rearrange("p (t a) -> p t a", a=1).broadcast_to([P, TC, NT]),
                            ALU.subtract).then_inc(off_ready, 1)

        @block.vector
        def _(dve):
            dve.sem_inc(low_used, 2)
            dve.sem_inc(picked_ready, 4)
            dve.sem_inc(summed, 2)
            dve.tensor_scalar(neg_p[:, :], s.iota_p[:, :], -1.0, None, ALU.mult).then_inc(bias_set, 1)
            dve.memset(one[:, :], 1.0).then_inc(bias_set, 1)

            def build(turn, j):
                k = 2 * turn + j
                dve.wait_ge(low_in[j], 16 * turn + 16)
                dve.wait_ge(rows_done, k + 1)
                dve.tensor_scalar(onehot[:, j, 0], low[:, j, 0], s.iota_p[:, 0:1], None, ALU.is_equal).then_inc(low_used, 1)

            def pick(turn, j, build_after):
                k = 2 * turn + j
                dve.wait_ge(rows_done, k + 3)
                dve.wait_ge(summed, k + 1)
                for q in range(2):
                    dve.wait_ge(off_ready, 2 * k + q + 1)
                    dve.scalar_tensor_tensor(picked[:, j, q], off[:, j, q], 0.0, pR[j][q][:, :, :], ALU.is_equal, ALU.mult).then_inc(picked_ready, 1)
                if build_after:
                    build(turn + 1, j)
                dve.wait_ge(picked_ready, 2 * k + 6)
                dve.tensor_reduce(s.edge_score[:, :, ds(k * TC, TC)], picked[:, j], AX_X, ALU.add).then_inc(summed, 1)

            for j in range(2):
                build(0, j)
            with dve.Fori(0, TURNS - 1) as i:
                for j in range(2):
                    pick(i, j, True)
            for j in range(2):
                pick(TURNS - 1, j, False)

        @block.scalar
        def _(act):
            act.sem_inc(low_far, 2)
            act.wait_ge(bias_set, 2)
            with act.Fori(0, TURNS) as i:
                for j in range(2):
                    k = 2 * i + j
                    act.wait_ge(low_in[j], 16 * i + 16)
                    act.activation(far[:, j], low[:, j, 1], ACT.Abs, bias=neg_p[:, 0:1]).then_inc(low_far, 1)
                    act.wait_ge(low_far, k + 3)
                    act.wait_ge(rows_done, k + 1)
                    act.activation(onehot[:, j, 1], far[:, j], ACT.Relu, scale=-1.0, bias=one[:, 0:1]).then_inc(hot_ready, 1)

        @block.tensor
        def _(pe):
            pe.sem_inc(rows_done, 2)
            with pe.Fori(0, TURNS) as i:
                for j in range(2):
                    k = 2 * i + j
                    pe.wait_ge(low_used, k + 3)
                    pe.wait_ge(hot_ready, k + 1)
                    pe.wait_ge(picked_ready, 2 * k + 2)
                    for q in range(2):
                        for t in range(TC):
                            for m in range(3):
                                last = pe.matmul(pR[j][q][:, t, :], onehot[:, j, q, t * P:(t + 1) * P], s.score_bits[:, q, m, :],
                                                 start=(m == 0), stop=(m == 2))
                    last.then_inc(rows_done, 1)


def edge_softmax(s):
    nc = s.nc
    ctx, sb, ps, sem = scope(s)
    with ctx:
        row = lambda name: sb("s_" + name, [RP, RG, P], F32)
        g, sd, first, last, keep, fwd, top, total, e, em, ex = map(
            row, ["g", "sd", "first", "last", "keep", "fwd", "top", "total", "e", "em", "ex"])
        notfirst, tmp, in_first, in_last, rel, ea = map(row, ["notfirst", "tmp", "in_first", "in_last", "rel", "ea"])
        ends = sb("s_ends", [RP, RG, 2], F32)
        keys = sb("s_keys", [RP, RG, 2], F32)
        wide = sb("s_wide", [RP, RG, 2], F32)
        K2 = 2 * ET
        one = lambda name: sb("s1_" + name, [1, K2], F32)
        key1, val1, first1, last1, keep1, fwd1, tot1, reset1 = map(one, ["key", "val", "first", "last", "keep", "fwd", "tot", "reset"])
        span = sb("s_span", [1, ET], F32)
        span1 = sb("s_span1", [1, 1], F32)
        span_i = sb("s_span_i", [1, 1], I32)
        HALF = 4
        pT = [[ps(f"s_pT{k}{h}", [RP, HALF, P]) for h in range(2)] for k in range(2)]
        pB = [[ps(f"s_pB{k}{h}", [P, HALF, RP]) for h in range(2)] for k in range(2)]
        link_sem, ea_in, T_done, B_done, keys_ready, ends_ready, back_ready, exp_in, exp_done, out_ready, zeroed = map(
            sem, ["s_link", "s_ea_in", "s_T", "s_B", "s_keys_ready", "s_ends_ready", "s_back_ready", "s_exp_in", "s_exp", "s_out", "s_zeroed"])
        stored = [sem(f"s_stored{n}") for n in range(5)]
        line_in = [sem(f"s_line_in{n}") for n in range(3)]
        wide_in = [sem(f"s_wide_in{n}") for n in range(2)]
        block = ctx.enter_context(nc.Block())
        flat = lambda t: t[:, :, :].rearrange("p g e -> p (g e)")
        to_rows = lambda n: s.bounce[n].rearrange("(g p) k -> p g k", p=RP)
        to_line = lambda n: s.bounce[n].rearrange("(a t) k -> a (t k)", a=1)

        @block.gpsimd
        def _(pool):
            pool.memset(s.agg[:, :, :], 0.0)

        @block.sync
        def _(sp):
            sp.dma_start(ea[:, :, :], s.ea.rearrange("(g p e) -> p g e", p=RP, e=P)).then_inc(ea_in, 16)
            sp.wait_ge(keys_ready, 1)
            sp.dma_start(to_rows(0), keys[:, :, :]).then_inc(stored[0], 16)
            sp.wait_ge(stored[0], 16)
            sp.dma_start(key1[:, :], to_line(0)).then_inc(line_in[0], 16)
            for n in range(2):
                sp.wait_ge(ends_ready, n + 1)
                sp.dma_start(to_rows(1 + n), ends[:, :, :]).then_inc(stored[1 + n], 16)
                sp.wait_ge(stored[1 + n], 16)
                sp.dma_start(val1[:, :], to_line(1 + n)).then_inc(line_in[1 + n], 16)
                sp.wait_ge(back_ready, n + 1)
                sp.dma_start(to_line(3 + n), tot1[:, :]).then_inc(stored[3 + n], 16)
                sp.wait_ge(stored[3 + n], 16)
                sp.dma_start(wide[:, :, :], to_rows(3 + n)).then_inc(wide_in[n], 16)

        @block.vector
        def _(dve):
            link = Link(dve, link_sem)
            dst = s.dst_f
            bc = lambda col: col.broadcast_to([RP, RG, P])
            link(dve.tensor_copy(keys[:, :, 0:1], dst[:, :, 0:1]))
            dve.tensor_copy(keys[:, :, 1:2], dst[:, :, P - 1:P]).then_inc(keys_ready, 1)
            link(dve.memset(first[:, :, 0:1], 1.0))
            link(dve.memset(last[:, :, P - 1:P], 1.0))
            link(dve.tensor_tensor(first[:, :, 1:P], dst[:, :, 1:P], dst[:, :, 0:P - 1], ALU.not_equal))
            link(dve.tensor_copy(last[:, :, 0:P - 1], first[:, :, 1:P]))
            link(dve.tensor_scalar(keep[:, :, :], last[:, :, :], -1.0, 1.0, ALU.mult, ALU.add))
            link(dve.tensor_scalar(notfirst[:, :, :], first[:, :, :], -1.0, 1.0, ALU.mult, ALU.add))
            link(dve.tensor_scalar(first[:, :, :], first[:, :, :], -BIG, None, ALU.mult))
            link(dve.tensor_tensor(in_first[:, :, :], dst[:, :, :], bc(dst[:, :, 0:1]), ALU.is_equal))
            link(dve.tensor_tensor(in_last[:, :, :], dst[:, :, :], bc(dst[:, :, P - 1:P]), ALU.is_equal))
            link(dve.tensor_tensor(rel[:, :, :], dst[:, :, :], bc(dst[:, :, 0:1]), ALU.subtract))
            dve.wait_ge(T_done, 1)
            dve.wait_ge(ea_in, 16)
            for h in range(2):
                n = min(HALF, RG - HALF * h)
                gs = slice(HALF * h, HALF * h + n)
                link(dve.tensor_tensor(g[:, gs, :], pT[0][h][:, 0:n, :], ea[:, gs, :], ALU.add))
                link(dve.tensor_copy(sd[:, gs, :], pT[1][h][:, 0:n, :]))

            def runs(data, in_place_of_zero, op_reset, op, to):
                link(dve.tensor_tensor_scan(flat(fwd), in_place_of_zero, flat(data), 0.0, op_reset, op))
                link(dve.tensor_tensor(fwd[:, :, :], fwd[:, :, :], last[:, :, :], ALU.mult))
                link(dve.tensor_tensor_scan(flat(to)[:, ::-1], flat(keep)[:, ::-1], flat(fwd)[:, ::-1], 0.0, ALU.mult, ALU.add))
                link(dve.tensor_copy(ends[:, :, 0:1], to[:, :, 0:1]))
                dve.tensor_copy(ends[:, :, 1:2], to[:, :, P - 1:P]).then_inc(ends_ready, 1)

            def runs_over_rows(reset, op_reset, op):
                link(dve.tensor_tensor_scan(fwd1[:, :], reset, val1[:, :], 0.0, op_reset, op))
                link(dve.tensor_tensor(fwd1[:, :], fwd1[:, :], last1[:, :], ALU.mult))
                dve.tensor_tensor_scan(tot1[:, ::-1], keep1[:, ::-1], fwd1[:, ::-1], 0.0, ALU.mult, ALU.add).then_inc(back_ready, 1)

            runs(g, flat(first), ALU.add, ALU.max, top)
            dve.wait_ge(line_in[0], 16)
            link(dve.memset(first1[:, 0:1], 1.0))
            link(dve.memset(last1[:, K2 - 1:K2], 1.0))
            link(dve.tensor_tensor(first1[:, 1:K2], key1[:, 1:K2], key1[:, 0:K2 - 1], ALU.not_equal))
            link(dve.tensor_copy(last1[:, 0:K2 - 1], first1[:, 1:K2]))
            link(dve.tensor_scalar(keep1[:, :], last1[:, :], -1.0, 1.0, ALU.mult, ALU.add))
            link(dve.tensor_scalar(reset1[:, :], first1[:, :], -BIG, None, ALU.mult))
            pairs = lambda t: t[:, :].rearrange("a (t k) -> a t k", k=2)
            link(dve.tensor_tensor(span[:, :], pairs(key1)[:, :, 1], pairs(key1)[:, :, 0], ALU.subtract))
            link(dve.tensor_reduce(span1[:, :], span[:, :], AX_X, ALU.max))
            link(dve.tensor_copy(span_i[:, :], span1[:, :]))
            link(dve.tensor_scalar(span_i[:, :], span_i[:, :], 7, None, ALU.logical_shift_right))
            link(dve.tensor_scalar(s.windows[:, :], span_i[:, :], 1, None, ALU.add))
            dve.wait_ge(line_in[1], 16)
            runs_over_rows(reset1[:, :], ALU.add, ALU.max)
            dve.wait_ge(wide_in[0], 16)
            for k, part in enumerate((in_first, in_last)):
                link(dve.tensor_scalar(tmp[:, :, :], part[:, :, :], 1.0, BIG, ALU.subtract, ALU.mult))
                link(dve.tensor_tensor(tmp[:, :, :], tmp[:, :, :], bc(wide[:, :, k:k + 1]), ALU.add))
                link(dve.tensor_tensor(top[:, :, :], top[:, :, :], tmp[:, :, :], ALU.max))
            for value, to in ((g, e), (top, em)):
                link(dve.tensor_tensor(value[:, :, :], value[:, :, :], sd[:, :, :], ALU.add))
                link(dve.scalar_tensor_tensor(flat(to), flat(value), SLOPE, flat(value), ALU.mult, ALU.max))
            dve.tensor_tensor(e[:, :, :], e[:, :, :], em[:, :, :], ALU.subtract).then_inc(exp_in, 1)
            dve.wait_ge(exp_done, 1)
            runs(ex, flat(notfirst), ALU.mult, ALU.add, total)
            dve.wait_ge(line_in[2], 16)
            link(dve.tensor_tensor(pairs(val1)[:, :, 1], pairs(val1)[:, :, 1], pairs(first1)[:, :, 1], ALU.mult))
            link(dve.tensor_scalar(first1[:, :], first1[:, :], -1.0, 1.0, ALU.mult, ALU.add))
            runs_over_rows(first1[:, :], ALU.mult, ALU.add)
            dve.wait_ge(wide_in[1], 16)
            for k, part in enumerate((in_first, in_last)):
                link(dve.tensor_tensor(tmp[:, :, :], part[:, :, :], bc(wide[:, :, k:k + 1]), ALU.mult))
                link(dve.tensor_tensor(total[:, :, :], total[:, :, :], tmp[:, :, :], ALU.max))
            link(dve.reciprocal(tmp[:, :, :], total[:, :, :]))
            dve.tensor_tensor(ex[:, :, :], ex[:, :, :], tmp[:, :, :], ALU.mult).then_inc(out_ready, 1)
            dve.wait_ge(B_done, 1)
            for k, to in enumerate((s.alphaT, s.relT)):
                for h in range(2):
                    n = min(HALF, RG - HALF * h)
                    dve.tensor_copy(to[:, HALF * h * RP:(HALF * h + n) * RP].rearrange("p (g r) -> p g r", g=n), pB[k][h][:, 0:n, :])

        @block.scalar
        def _(act):
            act.wait_ge(exp_in, 1)
            act.activation(flat(ex), flat(e), ACT.Exp).then_inc(exp_done, 1)

        @block.tensor
        def _(pe):
            for k in range(2):
                for gg in range(RG):
                    done = pe.transpose(pT[k][gg // HALF][:, gg % HALF, :], s.edge_score[:, k, gg * RP:(gg + 1) * RP], s.ident[:, :])
            done.then_inc(T_done, 1)
            pe.wait_ge(out_ready, 1)
            for k, of in enumerate((ex, rel)):
                for gg in range(RG):
                    done = pe.transpose(pB[k][gg // HALF][:, gg % HALF, :], of[:, gg, :], s.ident[0:RP, 0:RP])
            done.then_inc(B_done, 1)


def aggregate(s):
    nc = s.nc
    ctx, sb, ps, sem = scope(s)
    with ctx:
        assert ET // GU == NT
        BANKS = 6
        SLOTS = 8
        index = sb("g_index", [P, GU], I32)
        spare = sb("g_spare", [P, 3], F32)
        rows = sb("g_rows", [P, GU, D], F32)
        place = sb("g_place", [P, GU, P], F32)
        ramp = sb("g_ramp", [P, P], F32)
        base = sb("g_base", [1, ET], I32)
        pA = [ps(f"g_pA{b}", [P, DC, P]) for b in range(BANKS)]
        hx = sb("g_hx", [P, D], F32)
        hsum = sb("g_hsum", [P, HEADS], F32)
        dev = sb("g_dev", [P, D], F32)
        sq = sb("g_sq", [P, D], F32)
        hvar = sb("g_hvar", [P, HEADS], F32)
        hstd = sb("g_hstd", [P, HEADS], F32)
        hinv = sb("g_hinv", [P, HEADS], F32)
        nh = sb("g_nh", [P, DC, P + 1], F32)
        zrow = sb("g_zrow", [1, P + 1], F32)
        gram = sb("g_gram", [P, DC, P + 1], F32)
        ones = sb("g_ones", [P, P], F32)
        diag = sb("g_diag", [P, DC, P], F32)
        cols = sb("g_cols", [P, 2, DC], F32)
        mix_rows = sb("g_mix_rows", [P, 2, D], F32)
        kx = sb("g_kx", [P, DC, P], F32)
        kcol = sb("g_kcol", [P, DC, 1], F32)
        pG = [ps(f"g_pG{c}", [P, 512]) for c in range(DC)]
        hx_in, hx_used, hsum_ready, dev_ready, sq_ready, hvar_ready, hstd_ready, heps_ready, hinv_ready, nh_ready = map(
            sem, ["g_hx_in", "g_hx_used", "g_hsum_ready", "g_dev_ready", "g_sq_ready", "g_hvar_ready", "g_hstd_ready", "g_heps_ready", "g_hinv_ready", "g_nh_ready"])
        gram_used, zeroed, gram_all, mix_in, diag_ready, bc_done = map(
            sem, ["g_gram_used", "g_zeroed", "g_gram_all", "g_mix_in", "g_diag_ready", "g_bc_done"])
        kv_link = sem("g_kv_link")
        row_in = [sem(f"g_row_in{q}") for q in range(GU)]
        index_ready, placed, summed, added, link_sem, setup, taken = map(sem, ["g_index_ready", "g_placed", "g_summed", "g_added", "g_link", "g_setup", "g_taken"])
        ZR = N_TURNS * XB // P // ZERO_DMAS
        zero = sb("g_zero", [P, ZR * D], F32)
        zero_set, zero_out = sem("g_zero_set"), sem("g_zero_out")
        block = ctx.enter_context(nc.Block())
        TURNS = ET // GU

        @block.sync
        def _(sp):
            flat = lambda w: w.rearrange("h a c -> (h a c)")
            for k, w in enumerate((s.kw, s.kb)):
                for c in range(DC):
                    sp.dma_start(cols[:, k, c:c + 1], flat(w)[c * P:(c + 1) * P].rearrange("(p a) -> p a", a=1),
                                 allow_slow_non_contiguous=True).then_inc(mix_in, 16)
            for k, w in enumerate((s.vw, s.vb)):
                sp.dma_start(mix_rows[:, k, :], w.rearrange("h a c -> a (h c)").broadcast_to([P, D])).then_inc(mix_in, 16)
            windows = sp.value_load(s.windows[0:1, 0:1], min_val=1, max_val=NT)
            with sp.Fori(0, windows) as w:
                with sp.Fori(0, TURNS) as i:
                    sp.wait_ge(hx_used, w * TURNS + i + 1)
                    sp.dma_start(hx[:, :], tiled(s.xn)[ds(i, 1), :, :].rearrange("a p d -> p (a d)")).then_inc(hx_in, 16)
            sp.wait_ge(zero_set, 1)
            to = s.results.rearrange("(z p r) d -> z p (r d)", z=ZERO_DMAS, p=P)
            for z in range(ZERO_DMAS):
                sp.dma_start(to[z], zero[:, :]).then_inc(zero_out, 16)
            sp.wait_ge(zero_out, 16 * ZERO_DMAS)

        @block.scalar
        def _(act):
            windows = act.value_load(s.windows[0:1, 0:1], min_val=1, max_val=NT)
            with act.Fori(0, windows) as w:
                with act.Fori(0, TURNS) as i:
                    turn = w * TURNS + i
                    for h in range(GU // SLOTS):
                        act.wait_ge(summed, turn * GU + SLOTS * (h + 1))
                        act.wait_ge(taken, turn * 2 + h + 1)
                        act.activation(index[:, h * SLOTS:(h + 1) * SLOTS], s.srcT[:, ds(i * GU + h * SLOTS, SLOTS)], ACT.Copy).then_inc(index_ready, 1)
                    act.wait_ge(dev_ready, turn + 1)
                    act.activation(sq[:, :], dev[:, :], ACT.Square).then_inc(sq_ready, 1)
                    act.wait_ge(hvar_ready, turn + 1)
                    act.activation(hstd[:, :], hvar[:, :], ACT.Sqrt, scale=1.0 / (HC - 1)).then_inc(hstd_ready, 1)

        @block.gpsimd
        def _(pool):
            pool.sem_inc(taken, 2)
            pool.memset(spare[:, :], 0.0).then_inc(setup, 1)
            pool.wait_ge(setup, 1)
            windows = pool.value_load(s.windows[0:1, 0:1], min_val=1, max_val=NT)
            with pool.Fori(0, windows) as w:
                with pool.Fori(0, TURNS) as i:
                    turn = w * TURNS + i
                    for q in range(GU):
                        if q % SLOTS == 0:
                            pool.wait_ge(index_ready, turn * (GU // SLOTS) + q // SLOTS + 1)
                            pool.tensor_tensor(spare[:, 1 + q // SLOTS:2 + q // SLOTS], spare[:, 0:1], spare[:, 0:1], ALU.mult).then_inc(taken, 1)
                        pool.indirect_dma_start(rows[:, q, :], None, s.xn, bass.IndirectOffsetOnAxis(ap=index[:, q:q + 1], axis=0)).then_inc(row_in[q], 16)

        @block.vector
        def _(dve):
            link = Link(dve, link_sem)
            dve.sem_inc(added, GU)
            windows = dve.value_load(s.windows[0:1, 0:1], min_val=1, max_val=NT)
            dve.sem_inc(hx_used, 1)
            dve.memset(zrow[:, :], 0.0).then_inc(zeroed, 1)
            dve.memset(zero[:, :], 0.0).then_inc(zero_set, 1)
            dve.memset(nh[:, :, P:P + 1], 1.0).then_inc(zeroed, 1)
            dve.memset(ones[:, :], 1.0).then_inc(zeroed, 1)

            def head_sums(turn):
                dve.wait_ge(hx_in, 16 * turn + 16)
                dve.tensor_reduce(hsum[:, :], heads(hx), AX_X, ALU.add).then_inc(hsum_ready, 1)

            def head_deviates(turn):
                dve.wait_ge(hsum_ready, turn + 1)
                dve.scalar_tensor_tensor(heads(dev), wide(hsum), -1.0 / HC, heads(hx), ALU.mult, ALU.add).then_inc(dev_ready, 1)

            def head_variances(turn):
                dve.wait_ge(dev_ready, turn + 1)
                dve.sem_inc(hx_used, 1)
                dve.wait_ge(sq_ready, turn + 1)
                dve.tensor_reduce(hvar[:, :], heads(sq), AX_X, ALU.add).then_inc(hvar_ready, 1)

            def head_eps(turn):
                dve.wait_ge(hstd_ready, turn + 1)
                dve.tensor_scalar(hstd[:, :], hstd[:, :], HEAD_EPS, None, ALU.add).then_inc(heps_ready, 1)

            def head_inverses(turn):
                dve.wait_ge(heps_ready, turn + 1)
                dve.reciprocal(hinv[:, :], hstd[:, :]).then_inc(hinv_ready, 1)

            def head_norms(turn):
                dve.wait_ge(hinv_ready, turn + 1)
                dve.wait_ge(gram_used, turn + 1)
                dve.tensor_tensor(nh[:, :, 0:P].rearrange("p c (h e) -> p c h e", h=HEADS // DC), dev[:, :].rearrange("p (c h e) -> p c h e", c=DC, e=HC),
                                  hinv[:, :].rearrange("p (c h a) -> p c h a", c=DC, a=1).broadcast_to([P, DC, HEADS // DC, HC]), ALU.mult).then_inc(nh_ready, 1)
            heads = lambda a: a[:, :].rearrange("p (h c) -> p h c", h=HEADS)
            wide = lambda a: a[:, :].rearrange("p (h a) -> p h a", a=1).broadcast_to([P, HEADS, HC])
            STEPS = {1: head_sums, 2: head_deviates, 6: head_variances, 10: head_eps, 11: head_inverses, 12: head_norms}
            link(dve.tensor_copy(ramp[:, :], s.iota_f[:, :]))
            link(dve.tensor_copy(base[:, :], s.base[:, :]))
            with dve.Fori(0, windows) as w:
                link.loop(w, 2)
                with dve.Fori(0, TURNS) as i:
                    turn = w * TURNS + i
                    _, starts = nc.values_load_multi_w_load_instructions(
                        base[0:1, ds(i * GU, GU)], engines=[DVE], min_val=0, max_val=NP,
                        skip_runtime_bounds_check_because="destinations are nodes, and later windows are held at NP")
                    for q in range(GU):
                        col = i * GU + q
                        dve.tensor_scalar(place[:, q, :], ramp[:, :], s.relT[:, ds(col, 1)], s.alphaT[:, ds(col, 1)],
                                          ALU.is_equal, ALU.mult).then_inc(placed, 1)
                    for q in range(GU):
                        dve.wait_ge(summed, turn * GU + q + 1 + GU)
                        dve.wait_ge(added, turn * GU + q + GU)
                        window = s.agg[:, :, ds(starts[q], P)]
                        dve.tensor_tensor(window, window, pA[q % BANKS][:, :, :], ALU.add).then_inc(added, 1)
                        if q in STEPS:
                            STEPS[q](turn)
                    dve.wait_ge(nh_ready, turn + 1)
                dve.wait_ge(added, (w + 1) * ET + GU)
                link(dve.tensor_scalar(ramp[:, :], ramp[:, :], float(P), None, ALU.add))
                link(dve.tensor_scalar(base[:, :], base[:, :], float(P), float(NP), ALU.add, ALU.min))
            link = Link(dve, kv_link)
            dve.wait_ge(gram_all, 1)
            for c in range(DC):
                link(dve.tensor_copy(gram[:, c, :], pG[c][:, 0:P + 1]))
            for c in range(DC):
                dve.tensor_scalar(diag[:, c, :], s.ident[:, :], gram[:, c, P:P + 1], None, ALU.mult).then_inc(diag_ready, 1)
            dve.wait_ge(bc_done, 1)
            dve.wait_ge(mix_in, 16 * (2 * DC + 2))
            for c in range(DC):
                vcols = slice(c * P, (c + 1) * P)
                link(dve.tensor_scalar(kx[:, c, :], gram[:, c, 0:P], cols[:, 0, c:c + 1], None, ALU.mult))
                link(dve.scalar_tensor_tensor(kx[:, c, :], pA[0][:, c, :], cols[:, 1, c:c + 1], kx[:, c, :], ALU.mult, ALU.add))
                link(dve.tensor_tensor(kx[:, c, :], kx[:, c, :], mix_rows[:, 0, vcols], ALU.mult))
                link(dve.tensor_scalar(kcol[:, c, :], gram[:, c, P:P + 1], cols[:, 0, c:c + 1], None, ALU.mult))
                link(dve.scalar_tensor_tensor(kcol[:, c, :], cols[:, 1, c:c + 1], float(N), kcol[:, c, :], ALU.mult, ALU.add))
                link(dve.scalar_tensor_tensor(kx[:, c, :], mix_rows[:, 1, vcols], kcol[:, c, 0:1], kx[:, c, :], ALU.mult, ALU.add))
                link(dve.scalar_tensor_tensor(s.KV[:, c, :], kx[:, c, :], 1.0 / N, s.blockmask[:, :], ALU.mult, ALU.mult))
                link(dve.tensor_tensor(s.KV[:, c, :], s.KV[:, c, :], s.ident[:, :], ALU.add))

        @block.tensor
        def _(pe):
            pe.sem_inc(summed, GU)
            pe.sem_inc(gram_used, 1)
            windows = pe.value_load(s.windows[0:1, 0:1], min_val=1, max_val=NT)
            pe.wait_ge(zeroed, 3)
            with pe.Fori(0, windows) as w:
                for c in range(DC):
                    pe.matmul(pG[c][:, 0:P + 1], zrow[:, 0:P], zrow[:, :], start=True, stop=False)
                with pe.Fori(0, TURNS) as i:
                    turn = w * TURNS + i
                    for q in range(GU):
                        pe.wait_ge(row_in[q], 16 * turn + 16)
                        pe.wait_ge(placed, turn * GU + q + 1)
                        pe.wait_ge(added, turn * GU + q + 1 + GU - before(q, BANKS, GU))
                        for c in range(DC):
                            last = pe.matmul(pA[q % BANKS][:, c, :], rows[:, q, c * P:(c + 1) * P], place[:, q, :], start=True, stop=True)
                        last.then_inc(summed, 1)
                    pe.wait_ge(nh_ready, turn + 1)
                    for c in range(DC):
                        last = pe.matmul(pG[c][:, 0:P + 1], nh[:, c, 0:P], nh[:, c, :], start=False, stop=False)
                    last.then_inc(gram_used, 1)
            for c in range(DC):
                last = pe.matmul(pG[c][:, 0:P + 1], zrow[:, 0:P], zrow[:, :], start=False, stop=True)
            last.then_inc(gram_all, 1)
            pe.wait_ge(diag_ready, DC)
            for c in range(DC):
                last = pe.matmul(pA[0][:, c, :], ones[:, :], diag[:, c, :], start=True, stop=True)
            last.then_inc(bc_done, 1)


def node_update(s):
    nc = s.nc
    ctx, sb, ps, sem = scope(s)
    with ctx:
        TURNS = NT // G
        xt = sb("u_xt", [P, G, D], F32)
        xn = sb("u_xn", [P, G, D], F32)
        aggs = sb("u_aggs", [P, 2, DC, P], F32)
        xnT = sb("u_xnT", [P, 2, DC, P], F32)
        x1 = sb("u_x1", [P, G, D], F32)
        x1b = sb("u_x1b", [P, G, D], F32)
        beta = sb("u_beta", [P, D], F32)
        h = sb("u_h", [P, G, D], F32)
        h_rows = sb("u_h_rows", [P, G, D], F32)
        hT = sb("u_hT", [P, 2, DC, P], F32)
        stats = sb("u_stats", [P, G, 6], F32)
        mv = sb("u_mv", [P, G, 2], F32)
        std = sb("u_std", [P, G], F32)
        rstd = sb("u_rstd", [P, G], F32)
        eps = sb("u_eps", [P, 1], F32)
        spare = sb("u_spare", [P, 1], F32)
        gate = sb("u_gate", [P, DC, NX], F32)
        gate_b = sb("u_gate_b", [P, NX], F32)
        logit = sb("u_logit", [P, G, NX], F32)
        best = sb("u_best", [P, G, 8], F32)
        which = sb("u_which", [P, G, 8], mybir.dt.uint32)
        pT = [ps(f"u_pT{j}", [P, DC, P]) for j in range(2)]
        pX = [ps(f"u_pX{j}", [P, D]) for j in range(2)]
        pH = [ps(f"u_pH{j}", [P, DC, P]) for j in range(2)]
        pL = ps("u_pL", [P, G, NX])
        pP = ps("u_pP", [P, G, NX])
        which_f = sb("u_which_f", [P, G, 2], F32)
        hot = sb("u_hot", [P, 2, G, NX], F32)
        both = sb("u_both", [P, G, NX], BF16)
        seen = sb("u_seen", [P, NX], F32)
        seen_b = sb("u_seen_b", [P, NX], BF16)
        new = sb("u_new", [P, NX], F32)
        picked = sb("u_picked", [P, 2, G, NX], F32)
        slot_f = sb("u_slot_f", [P, 2, G], F32)
        index = sb("u_index", [P, 2, G], I32)
        rank = sb("u_rank", [P, 2, NT], F32)
        expert = sb("u_expert", [P, 2, NT], F32)
        begin = sb("u_begin", [P, 2 * NT, NX], F32)
        node_i = sb("u_node_i", [P, NT], I32)
        node_f = sb("u_node_f", [P, NT], F32)
        exp_i = sb("u_exp_i", [P, NX], I32)
        exp_f = sb("u_exp_f", [P, NX], F32)
        valid = sb("u_valid", [P, NT], F32)
        no_expert = sb("u_no_expert", [P, NT], F32)
        away = sb("u_away", [P, 2, NT], F32)
        earlier = sb("u_earlier", [P, P], BF16)
        ones = sb("u_ones", [P, P], BF16)
        delta = sb("u_delta", [P, NT], F32)
        ex = sb("u_ex", [P, NT], F32)
        den = sb("u_den", [P, NT], F32)
        turns_i = sb("u_turns_i", [P, NX], I32)
        turns_f = sb("u_turns_f", [P, NX], F32)
        keep1 = sb("u_keep1", [P, NX], F32)
        ends = sb("u_ends", [P, NX], F32)
        scatter_spare = sb("u_scatter_spare", [P, 3], F32)
        ramps, setup, ranks_ready, both_ready, placed, slots_ready, taken, scattered, rows_free, delta_ready, exp_ready, counted, h_copied = map(
            sem, ["u_ramps", "u_setup", "u_ranks_ready", "u_both", "u_placed", "u_slots", "u_taken", "u_scattered", "u_rows_free", "u_delta_s", "u_exp", "u_counted", "u_h_copied"])
        in_x = [sem(f"u_in_x{q}") for q in range(G)]
        in_xn = [sem(f"u_in_xn{q}") for q in range(G)]
        eps_set, gate_in, x1_ready, xnT_done, xnT_copied, aggs_ready, x_done, mv_ready, std_ready, h_ready = map(
            sem, ["u_eps_set", "u_gate_in", "u_x1_ready", "u_xnT_done", "u_xnT_copied", "u_aggs_ready", "u_x_done", "u_mv_ready", "u_std_ready", "u_h_ready"])
        hT_done, hT_copied, logit_done, logit_read, link_sem, top_ready, x1b_ready, x1b_out, h_out = map(
            sem, ["u_hT_done", "u_hT_copied", "u_logit_done", "u_logit_read", "u_link", "u_top", "u_x1b_ready", "u_x1b_out", "u_h_out"])
        x_t, xn_t = tiled(s.x), tiled(s.xn)
        turn_of = lambda a, i: a.rearrange("(i q p) d -> i p q d", q=G, p=P)[ds(i, 1)].rearrange("a p q d -> p (a q) d")
        block = ctx.enter_context(nc.Block())
        tile = lambda a, k: a[ds(k, 1), :, :].rearrange("a p d -> p (a d)")

        @block.sync
        def _(sp):
            sp.dma_start(gate[:, :, :], s.gate_w.rearrange("(c p) e -> p c e", p=P)).then_inc(gate_in, 16)
            sp.dma_start(gate_b[:, :], s.gate_b.rearrange("(a e) -> a e", a=1).broadcast_to([P, NX])).then_inc(gate_in, 16)
            sp.dma_start(beta[:, :], s.beta.rearrange("(a d) -> a d", a=1).broadcast_to([P, D])).then_inc(gate_in, 16)
            with sp.Fori(0, TURNS) as i:
                for q in range(G):
                    k = i * G + q
                    sp.wait_ge(xnT_done, k + 1)
                    sp.dma_start(xn[:, q, :], tile(xn_t, k)).then_inc(in_xn[q], 16)
                    sp.wait_ge(x1_ready, k + 1)
                    sp.dma_start(xt[:, q, :], tile(x_t, k)).then_inc(in_x[q], 16)

        @block.gpsimd
        def _(pool):
            pool.iota(node_i[:, :], [[P, NT]], base=0, channel_multiplier=1).then_inc(ramps, 1)
            pool.iota(exp_i[:, :], [[1, NX]], base=0, channel_multiplier=0).then_inc(ramps, 1)
            pool.memset(scatter_spare[:, :], 0.0).then_inc(setup, 1)
            pool.wait_ge(setup, 1)
            pool.wait_ge(gate_in, 48)
            pool.sem_inc(rows_free, 1)
            with pool.Fori(0, TURNS) as i:
                for q in range(G):
                    pool.wait_ge(x1_ready, i * G + q + 1 + G)
                    pool.wait_ge(x1b_out, 16 * i + 16)
                    pool.tensor_tensor(x1b[:, q, :], x1[:, q, :], beta[:, :], ALU.add).then_inc(x1b_ready, 1)
                pool.wait_ge(slots_ready, i + 1)
                pool.wait_ge(h_copied, i + 2)
                pool.tensor_tensor(scatter_spare[:, 1:2], scatter_spare[:, 0:1], scatter_spare[:, 0:1], ALU.mult).then_inc(taken, 1)
                for q in range(G):
                    for k in range(2):
                        pool.indirect_dma_start(s.sorted, bass.IndirectOffsetOnAxis(ap=index[:, k, q:q + 1], axis=0), h_rows[:, q, :], None).then_inc(scattered, 16)
                pool.wait_ge(scattered, i * (2 * G * 16) + 2 * G * 16)
                pool.tensor_tensor(scatter_spare[:, 2:3], scatter_spare[:, 0:1], scatter_spare[:, 0:1], ALU.mult).then_inc(rows_free, 1)

        @block.vector
        def _(dve):
            link = Link(dve, link_sem)
            dve.sem_inc(x1_ready, G)
            dve.sem_inc(x1b_ready, G)
            dve.sem_inc(logit_read, 1)
            dve.memset(eps[:, :], LN_EPS).then_inc(eps_set, 1)
            dve.wait_ge(ramps, 2)
            link(dve.tensor_copy(node_f[:, :], node_i[:, :]))
            link(dve.tensor_copy(exp_f[:, :], exp_i[:, :]))
            link(dve.tensor_scalar(valid[:, :], node_f[:, :], float(N), None, ALU.is_lt))
            link(dve.tensor_scalar(no_expert[:, :], valid[:, :], -float(NX), float(NX), ALU.mult, ALU.add))
            for k in range(2):
                link(dve.tensor_scalar(away[:, k, :], node_f[:, :], float(AWAY + k * P - (NP - P)), None, ALU.add))
                link(dve.scalar_tensor_tensor(away[:, k, :], no_expert[:, :], 1.0 / NX, away[:, k, :], ALU.mult, ALU.mult))
            link(dve.tensor_scalar(earlier[:, :], s.iota_f[:, :], s.iota_p[:, 0:1], None, ALU.is_gt))
            link(dve.memset(ones[:, :], 1.0))
            link(dve.memset(seen[:, :], 0.0))
            dve.memset(seen_b[:, :], 0.0).then_inc(ranks_ready, 1)
            dve.wait_ge(gate_in, 48)
            over_e = lambda a: a.rearrange("p (g a) -> p g a", a=1).broadcast_to([P, G, NX])
            node_cols = lambda a, i: a[:, ds(i * G, G)]
            with dve.Fori(0, TURNS) as i:
                link.loop(i, 13)
                def stats_of(q):
                    dve.wait_ge(x1_ready, i * G + q + 1 + G)
                    return dve.bn_stats(stats[:, q, :], x1[:, q, :])
                dve.wait_ge(x1b_ready, (i + 1) * G)
                for q in range(G):
                    dve.wait_ge(in_x[q], 16 * i + 16)
                    dve.wait_ge(x_done, i * G + q + 1 + G)
                    dve.tensor_tensor(x1[:, q, :], pX[q % 2][:, :], xt[:, q, :], ALU.add).then_inc(x1_ready, 1)
                    if q:
                        stats_of(q - 1)
                link(stats_of(G - 1))
                dve.memset(spare[:, :], 0.0)
                for q in range(G):
                    last = dve.bn_aggr(mv[:, q, :], stats[:, q, :])
                last.then_inc(mv_ready, 1)
                dve.wait_ge(std_ready, i + 1)
                link(dve.reciprocal(rstd[:, :], std[:, :]))
                dve.wait_ge(h_copied, i + 1)
                dve.wait_ge(hT_done, (i + 1) * G)
                for q in range(G):
                    dve.tensor_scalar(h[:, q, :], x1[:, q, :], mv[:, q, 0:1], rstd[:, q:q + 1], ALU.subtract, ALU.mult).then_inc(h_ready, 1)
                dve.wait_ge(logit_done, (i + 2) * G)
                dve.tensor_tensor(logit[:, :, :], pL[:, :, :], gate_b[:, :].rearrange("p (a e) -> p a e", a=1).broadcast_to([P, G, NX]), ALU.add).then_inc(logit_read, 1)
                dve.wait_ge(logit_read, i + 2)
                dve.memset(spare[:, :], 0.0)
                for q in range(G):
                    last = dve.max(best[:, q, :], logit[:, q, :])
                link(last)
                dve.memset(spare[:, :], 0.0)
                for q in range(G):
                    last = dve.max_index(which[:, q, :], best[:, q, :], logit[:, q, :])
                link(last)
                dve.tensor_copy(s.best[:, ds(i * G, G), :], best[:, :, 0:2])
                dve.tensor_copy(which_f[:, :, :], which[:, :, 0:2]).then_inc(top_ready, 1)
                dve.wait_ge(top_ready, i + 1)
                link(dve.tensor_tensor(which_f[:, :, :], which_f[:, :, :], node_cols(no_expert, i).rearrange("p (g a) -> p g a", a=1).broadcast_to([P, G, 2]), ALU.add))
                for k in range(2):
                    last = dve.tensor_tensor(hot[:, k], exp_f[:, :].rearrange("p (a e) -> p a e", a=1).broadcast_to([P, G, NX]), over_e(which_f[:, :, k]), ALU.is_equal)
                link(last)
                dve.tensor_tensor(both[:, :, :], hot[:, 0], hot[:, 1], ALU.add).then_inc(both_ready, 1)
                dve.wait_ge(both_ready, i + 1)
                link(dve.tensor_reduce(new[:, :], both[:, :, :].rearrange("p g e -> p e g"), AX_X, ALU.add))
                link(dve.tensor_tensor(seen[:, :], seen[:, :], new[:, :], ALU.add))
                dve.wait_ge(placed, i + 1)
                dve.tensor_copy(seen_b[:, :], seen[:, :])
                for k in range(2):
                    last = dve.tensor_tensor(picked[:, k], pP[:, :, :], hot[:, k], ALU.mult)
                last.then_inc(ranks_ready, 1)
                dve.wait_ge(ranks_ready, i + 2)
                link(dve.tensor_reduce(slot_f[:, :, :], picked[:, :], AX_X, ALU.add))
                dve.tensor_copy(rank[:, :, ds(i * G, G)], slot_f[:, :, :])
                link(dve.tensor_copy(expert[:, :, ds(i * G, G)], which_f[:, :, :].rearrange("p g k -> p k g")))
                link(dve.scalar_tensor_tensor(slot_f[:, :, :], which_f[:, :, :].rearrange("p g k -> p k g"), float(XL), slot_f[:, :, :], ALU.mult, ALU.add))
                over_k = lambda a: a.rearrange("p (a g) -> p a g", a=1).broadcast_to([P, 2, G])
                link(dve.tensor_tensor(slot_f[:, :, :], slot_f[:, :, :], over_k(node_cols(valid, i)), ALU.mult))
                link(dve.tensor_tensor(slot_f[:, :, :], slot_f[:, :, :], away[:, :, ds(i * G, G)], ALU.add))
                dve.wait_ge(rows_free, i + 1)
                dve.tensor_copy(index[:, :, :], slot_f[:, :, :]).then_inc(slots_ready, 1)
                dve.wait_ge(slots_ready, i + 1)
            link.end_loop(TURNS)
            dve.tensor_tensor(delta[:, :], s.best[:, :, 1], s.best[:, :, 0], ALU.subtract).then_inc(delta_ready, 1)
            dve.wait_ge(counted, 1)
            counts = pP[:, 0, :]
            link(dve.tensor_copy(s.count[:, :], counts[0:1, :]))
            link(dve.tensor_scalar(turns_f[:, :], counts, float(XB - 1), float(XB), ALU.add, ALU.max))
            link(dve.tensor_copy(turns_i[:, :], turns_f[:, :]))
            link(dve.tensor_scalar(turns_i[:, :], turns_i[:, :], XB.bit_length() - 1, None, ALU.logical_shift_right))
            link(dve.tensor_copy(s.turns[:, :], turns_i[0:1, :]))
            link(dve.tensor_copy(turns_f[:, :], turns_i[:, :]))
            link(dve.memset(keep1[:, :], 1.0))
            link(dve.tensor_tensor_scan(ends[:, :], keep1[:, :], turns_f[:, :], 0.0, ALU.mult, ALU.add))
            link(dve.tensor_copy(s.total[:, :], ends[0:1, NX - 1:NX]))
            link(dve.tensor_tensor(ends[:, :], ends[:, :], turns_f[:, :], ALU.subtract))
            link(dve.tensor_copy(s.before[:, :], ends[0:1, :]))
            link(dve.tensor_scalar(ends[:, :], ends[:, :], float(XB), None, ALU.mult))
            wide_e = lambda a: a.rearrange("p (t e) -> p t e", t=1).broadcast_to([P, 2 * NT, NX])
            link(dve.tensor_tensor(begin[:, :, :], wide_e(exp_f[:, :]), expert[:, :, :].rearrange("p k t -> p (k t)").rearrange("p (t a) -> p t a", a=1).broadcast_to([P, 2 * NT, NX]), ALU.is_equal))
            link(dve.tensor_tensor(begin[:, :, :], begin[:, :, :], wide_e(ends[:, :]), ALU.mult))
            link(dve.tensor_reduce(expert[:, :, :].rearrange("p k t -> p (k t)"), begin[:, :, :], AX_X, ALU.add))
            link(dve.tensor_tensor(rank[:, :, :], rank[:, :, :], expert[:, :, :], ALU.add))
            link(dve.tensor_copy(s.result_row[:, :, :], rank[:, :, :]))
            dve.wait_ge(exp_ready, 1)
            link(dve.tensor_scalar(den[:, :], ex[:, :], 1.0, None, ALU.add))
            link(dve.reciprocal(s.weight[:, :, 0], den[:, :]))
            link(dve.tensor_tensor(s.weight[:, :, 1], s.weight[:, :, 0], ex[:, :], ALU.mult))

        @block.scalar
        def _(act):
            act.wait_ge(eps_set, 1)
            act.sem_inc(xnT_copied, G)
            act.sem_inc(hT_copied, G)
            act.sem_inc(h_copied, 1)
            prime(act, s, x1b_out)
            prime(act, s, h_out)
            with act.Fori(0, TURNS) as i:
                for q in range(G):
                    k = i * G + q
                    act.wait_ge(x_done, k + G + 1 - before(q, 2))
                    act.activation(aggs[:, q % 2, :, :], s.agg[:, :, ds(k * P, P)], ACT.Identity).then_inc(aggs_ready, 1)
                    act.wait_ge(xnT_done, k + 1 + G)
                    act.activation(xnT[:, q % 2, :, :], pT[q % 2][:, :, :], ACT.Identity).then_inc(xnT_copied, 1)
                act.wait_ge(mv_ready, i + 1)
                act.activation(std[:, :], mv[:, :, 1], ACT.Sqrt, bias=eps[:, 0:1]).then_inc(std_ready, 1)
                for q in range(G):
                    k = i * G + q
                    act.wait_ge(hT_done, k + 1 + G)
                    act.wait_ge(logit_done, k + G + 1 - before(q, 2))
                    act.activation(hT[:, q % 2, :, :], pH[q % 2][:, :, :], ACT.Identity).then_inc(hT_copied, 1)
                act.wait_ge(h_out, 16 * i + 16)
                act.wait_ge(rows_free, i + 1)
                act.activation(h_rows[:, :, :], h[:, :, :], ACT.Identity).then_inc(h_copied, 1)
                act.wait_ge(h_copied, i + 2)
                act.dma_start(turn_of(s.h, i), h_rows[:, :, :]).then_inc(h_out, 16)
                act.wait_ge(x1b_ready, (i + 2) * G)
                act.dma_start(turn_of(s.x1, i), x1b[:, :, :]).then_inc(x1b_out, 16)
            act.wait_ge(x1b_out, 16 * (TURNS + 1))
            act.wait_ge(h_out, 16 * (TURNS + 1))
            act.wait_ge(delta_ready, 1)
            act.activation(ex[:, :], delta[:, :], ACT.Exp).then_inc(exp_ready, 1)

        @block.tensor
        def _(pe):
            pe.sem_inc(xnT_done, G)
            pe.sem_inc(x_done, G)
            pe.sem_inc(hT_done, G)
            pe.sem_inc(logit_done, G)
            pe.wait_ge(gate_in, 48)
            with pe.Fori(0, TURNS) as i:
                def turn_xn(q):
                    k = i * G + q
                    pe.wait_ge(in_xn[q], 16 * i + 16)
                    pe.wait_ge(xnT_copied, k + G + 1 - before(q, 2))
                    for c in range(DC):
                        last = pe.transpose(pT[q % 2][:, c, :], xn[:, q, c * P:(c + 1) * P], s.ident[:, :])
                    last.then_inc(xnT_done, 1)

                def sum_x(q):
                    k = i * G + q
                    pe.wait_ge(x1_ready, k + G + 1 - before(q, 2))
                    pe.wait_ge(aggs_ready, k + 1)
                    for c in range(DC):
                        pe.matmul(pX[q % 2][:, :], aggs[:, q % 2, c, :], s.WT[:, c, :], start=(c == 0), stop=False)
                    pe.wait_ge(xnT_copied, k + 1 + G)
                    for c in range(DC):
                        last = pe.matmul(pX[q % 2][:, c * P:(c + 1) * P], xnT[:, q % 2, c, :], s.KV[:, c, :], start=False, stop=(c == DC - 1))
                    last.then_inc(x_done, 1)

                def turn_h(q):
                    k = i * G + q
                    pe.wait_ge(h_ready, k + 1)
                    pe.wait_ge(hT_copied, k + G + 1 - before(q, 2))
                    for c in range(DC):
                        last = pe.transpose(pH[q % 2][:, c, :], h[:, q, c * P:(c + 1) * P], s.ident[:, :])
                    last.then_inc(hT_done, 1)

                def logits(q):
                    k = i * G + q
                    pe.wait_ge(hT_copied, k + 1 + G)
                    if q == 0:
                        pe.wait_ge(logit_read, i + 1)
                    for c in range(DC):
                        last = pe.matmul(pL[:, q, :], hT[:, q % 2, c, :], gate[:, c, :], start=(c == 0), stop=(c == DC - 1))
                    last.then_inc(logit_done, 1)

                for turn, use in ((turn_xn, sum_x), (turn_h, logits)):
                    turn(0)
                    for q in range(1, G):
                        turn(q)
                        use(q - 1)
                    use(G - 1)
                pe.wait_ge(ranks_ready, i + 1)
                pe.wait_ge(both_ready, i + 1)
                pe.matmul(pP[:, :, :], ones[:, :], seen_b[:, :].rearrange("p (a e) -> p a e", a=1).broadcast_to([P, G, NX]), start=True, stop=False)
                last = pe.matmul(pP[:, :, :], earlier[:, :], both[:, :, :], start=False, stop=False)
                for q in range(G - 1):
                    last = pe.matmul(pP[:, q + 1:G, :], ones[:, :], both[:, q:q + 1, :].broadcast_to([P, G - 1 - q, NX]), start=False, stop=(q == G - 2))
                last.then_inc(placed, 1)
            pe.wait_ge(ranks_ready, TURNS + 1)
            pe.matmul(pP[:, 0, :], ones[:, :], seen_b[:, :], start=True, stop=True).then_inc(counted, 1)


def experts(s):
    nc = s.nc
    ctx, sb, ps, sem = scope(s)
    with ctx:
        B = XB // P
        w1 = sb("x_w1", [P, 2, DC, FF], F32)
        w2 = sb("x_w2", [P, 2, FC, D], F32)
        b1 = sb("x_b1", [P, 2, FC], F32)
        b2 = sb("x_b2", [P, 2, D], F32)
        zero = sb("x_zero", [P, B * D], F32)
        spare = sb("x_spare", [P, 1], F32)
        taken = sem("x_taken")
        rows = sb("x_rows", [P, B, D], F32)
        xT = sb("x_xT", [P, DC, XB], F32)
        hid = sb("x_hid", [P, FC, XB], F32)
        res = sb("x_res", [P, B, D], F32)
        done = sb("x_done", [1, 1], F32)
        end = sb("x_end", [1, 1], F32)
        pT = [ps(f"x_pT{b}", [P, DC, P]) for b in range(B)]
        pH = [ps(f"x_pH{f}", [P, XB]) for f in range(FC)]
        pY = [ps(f"x_pY{b}", [P, D]) for b in range(B)]
        w_in = [sem(f"x_w_in{r}") for r in range(2)]
        row_in = [sem(f"x_row_in{b}") for b in range(B)]
        res_out = [sem(f"x_res_out{b}") for b in range(B)]
        w_used, rows_T, xT_ready, hid_done, hid_ready, y_done, res_ready, setup, tail_out = map(
            sem, ["x_w_used", "x_rows_T", "x_xT_ready", "x_hid_done", "x_hid_ready", "x_y_done", "x_res_ready", "x_setup", "x_tail_out"])
        block = ctx.enter_context(nc.Block())

        def turns(engine, body, first=None, after=None, peeled=0):
            def two(pair):
                for r in range(2):
                    e = 2 * pair + r
                    if first is not None:
                        first(pair, r, e)
                    count = engine.value_load(s.turns[0:1, ds(e, 1)], min_val=1, max_val=-(-N // XB))
                    start = engine.value_load(s.before[0:1, ds(e, 1)], min_val=0, max_val=N_TURNS - 1)
                    with engine.Fori(0, count) as b:
                        turn = nc.s_assert_within(start + b, 0, N_TURNS - 1, skip_runtime_bounds_check_because="all experts' turns are at most N_TURNS")
                        body(e, r, b, turn)
                    if after is not None:
                        after(r, e, start + count)

            with engine.Fori(0, NX // 2 - peeled) as pair:
                two(pair)
            for pair in range(NX // 2 - peeled, NX // 2):
                two(pair)

        @block.sync
        def _(sp):
            def load(r, e):
                sp.dma_start(w1[:, r], s.w1[ds(e, 1), :, :].rearrange("a (c p) f -> p (a c) f", p=P)).then_inc(w_in[r], 16)
                sp.dma_start(w2[:, r], s.w2[ds(e, 1), :, :].rearrange("a (c p) f -> p (a c) f", p=P)).then_inc(w_in[r], 16)
                sp.dma_start(b1[:, r], s.b1[ds(e, 1), :].rearrange("a (c p) -> p (a c)", p=P), allow_slow_non_contiguous=True).then_inc(w_in[r], 16)
                sp.dma_start(b2[:, r], s.b2[ds(e, 1), :].broadcast_to([P, D])).then_inc(w_in[r], 16)

            def load_next(pair, r, e):
                if isinstance(e, int) and e + 1 == NX:
                    return
                sp.wait_ge(w_used, e + 1)
                load(1 - r, e + 1)

            def body(e, r, b, n):
                for q in range(B):
                    sp.wait_ge(res_ready, n * B + q + 1 + B)
                    sp.dma_start(s.results[ds((n * B + q) * P, P), :], res[:, q, :]).then_inc(res_out[q], 16)
            sp.wait_ge(setup, 1)
            load(0, 0)
            for q in range(B):
                prime(sp, s, res_out[q])
            turns(sp, body, load_next, peeled=1)

        @block.scalar
        def _(act):
            def first(pair, r, e):
                act.wait_ge(w_in[r], 64 * pair + 64)

            def transposed(n):
                for q in range(B):
                    act.wait_ge(rows_T, n * B + q + 1 + B)
                    act.activation(xT[:, :, q * P:(q + 1) * P], pT[q][:, :, :], ACT.Identity).then_inc(xT_ready, 1)

            def body(e, r, b, n):
                for f in range(FC):
                    act.wait_ge(hid_done, n * FC + f + 1)
                    act.activation(hid[:, f, :], pH[f][:, :], ACT.Relu, bias=b1[:, r, f:f + 1]).then_inc(hid_ready, 1)
                transposed(n + 1)
            transposed(0)
            turns(act, body, first)

        @block.gpsimd
        def _(pool):
            pool.memset(zero[:, :], 0.0).then_inc(setup, 1)
            pool.wait_ge(setup, 1)

            def first(pair, r, e):
                rows_of_expert = pool.value_load(s.count[0:1, ds(e, 1)], min_val=0, max_val=N)
                pool.dma_start(s.sorted[ds(rows_of_expert + e * XL, XB), :].rearrange("(p r) d -> p (r d)", p=P), zero[:, :]).then_inc(tail_out, 16)
                pool.wait_ge(tail_out, 16 * e + 16)

            def body(e, r, b, n):
                for q in range(B):
                    pool.wait_ge(rows_T, n * B + q + 1)
                    pool.dma_start(rows[:, q, :], s.sorted[ds(e * XL + (b * B + q) * P, P), :]).then_inc(row_in[q], 16)
            turns(pool, body, first)
            total = pool.value_load(s.total[0:1, 0:1], min_val=NX, max_val=N_TURNS)
            pool.wait_ge(rows_T, total * B + B)
            pool.tensor_tensor(spare[:, :], zero[:, 0:1], zero[:, 0:1], ALU.mult).then_inc(taken, 1)
            pool.wait_ge(taken, 1)
            for q in range(B):
                pool.dma_start(rows[:, q, :], s.sorted[q * P:(q + 1) * P, :]).then_inc(row_in[q], 16)

        @block.tensor
        def _(pe):
            pe.sem_inc(rows_T, B)

            def first(pair, r, e):
                pe.wait_ge(w_in[r], 64 * pair + 64)

            def transpose(n):
                for q in range(B):
                    pe.wait_ge(row_in[q], 16 * n + 16)
                    for c in range(DC):
                        last = pe.transpose(pT[q][:, c, :], rows[:, q, c * P:(c + 1) * P], s.ident[:, :])
                    last.then_inc(rows_T, 1)

            def body(e, r, b, n):
                pe.wait_ge(xT_ready, n * B + B)
                for f in range(FC):
                    for c in range(DC):
                        last = pe.matmul(pH[f][:, :], w1[:, r, c, f * P:(f + 1) * P], xT[:, c, :], start=(c == 0), stop=(c == DC - 1))
                    last.then_inc(hid_done, 1)
                transpose(n + 1)
                for q in range(B):
                    pe.wait_ge(res_ready, n * B + q + 1)
                    for f in range(FC):
                        if q == 0:
                            pe.wait_ge(hid_ready, n * FC + f + 1)
                        last = pe.matmul(pY[q][:, :], hid[:, f, q * P:(q + 1) * P], w2[:, r, f, :], start=(f == 0), stop=(f == FC - 1))
                    last.then_inc(y_done, 1)
            transpose(0)
            turns(pe, body, first)

        @block.vector
        def _(dve):
            dve.sem_inc(res_ready, B)
            dve.sem_inc(w_used, 1)

            def first(pair, r, e):
                dve.wait_ge(w_in[r], 64 * pair + 64)

            def body(e, r, b, n):
                for q in range(B):
                    dve.wait_ge(y_done, n * B + q + 1)
                    dve.wait_ge(res_out[q], 16 * n + 16)
                    dve.tensor_tensor(res[:, q, :], pY[q][:, :], b2[:, r, :], ALU.add).then_inc(res_ready, 1)
            def after(r, e, n):
                dve.wait_ge(res_ready, n * B + B)
                dve.wait_ge(w_used, e + 1)
                dve.memset(done[:, :], 0.0).then_inc(w_used, 1)
            turns(dve, body, first, after)
            total = dve.value_load(s.total[0:1, 0:1], min_val=NX, max_val=N_TURNS)
            for q in range(B):
                dve.wait_ge(res_out[q], total * 16 + 16)
            dve.memset(end[:, :], 0.0)


def final_norm(s):
    nc = s.nc
    ctx, sb, ps, sem = scope(s)
    with ctx:
        TURNS = NT // G
        PARTS = (range(0, 4), range(4, G))
        x1 = sb("f_x1", [P, G, D], F32)
        h = sb("f_h", [P, G, D], F32)
        res = sb("f_res", [P, G, 2, D], F32)
        index = sb("f_index", [P, 2, G], I32)
        y = sb("f_y", [P, G, D], F32)
        o = sb("f_o", [P, G, D], F32)
        scale = sb("f_gamma", [P, D], F32)
        stats = sb("f_stats", [P, G, 6], F32)
        mv = sb("f_mv", [P, G, 2], F32)
        std = sb("f_std", [P, G], F32)
        rstd = sb("f_rstd", [P, G], F32)
        eps = sb("f_eps", [P, 1], F32)
        spare = sb("f_spare", [P, 3], F32)
        spare2 = sb("f_spare2", [P, 1], F32)
        row_in = [[sem(f"f_row_in{q}{k}") for k in range(2)] for q in range(G)]
        h_in = [sem(f"f_h_in{part}") for part in range(2)]
        x1_in, out_out, gamma_in, eps_set, index_ready, first_ready, y_ready, mv_ready, std_ready, scaled, o_ready, link_sem, taken, setup = map(
            sem, ["f_x1_in", "f_out", "f_gamma_in", "f_eps_set", "f_index_ready", "f_first", "f_y", "f_mv", "f_std_s", "f_scaled", "f_o_ready", "f_link", "f_taken", "f_setup"])
        turn_of = lambda a, i: a.rearrange("(i q p) d -> i p q d", q=G, p=P)[ds(i, 1)].rearrange("a p q d -> p (a q) d")
        h_t = tiled(s.h).rearrange("t p d -> p t d")
        block = ctx.enter_context(nc.Block())

        @block.sync
        def _(sp):
            sp.dma_start(scale[:, :], s.gamma.rearrange("(a d) -> a d", a=1).broadcast_to([P, D])).then_inc(gamma_in, 16)
            prime(sp, s, out_out)
            with sp.Fori(0, TURNS) as i:
                sp.wait_ge(o_ready, (i + 1) * G)
                sp.dma_start(x1[:, :, :], turn_of(s.x1, i)).then_inc(x1_in, 16)
                sp.wait_ge(o_ready, (i + 2) * G)
                sp.dma_start(turn_of(s.out, i), o[:, :, :]).then_inc(out_out, 16)
            sp.wait_ge(out_out, 16 * (TURNS + 1))

        @block.scalar
        def _(act):
            def fetch(i, part):
                tiles = PARTS[part]
                act.wait_ge(y_ready, i * G + tiles[-1] + 1)
                act.wait_ge(taken, i * 2 + part + 1)
                cols = slice(tiles[0], tiles[-1] + 1)
                act.activation(index[:, :, cols], s.result_row[:, :, ds(i * G + tiles[0], len(tiles))], ACT.Copy).then_inc(index_ready, 1)
                act.dma_start(h[:, cols, :], h_t[:, ds(i * G + tiles[0], len(tiles)), :]).then_inc(h_in[part], 16)

            def root(i):
                act.wait_ge(mv_ready, i + 1)
                act.activation(std[:, :], mv[:, :, 1], ACT.Sqrt, bias=eps[:, 0:1]).then_inc(std_ready, 1)

            act.wait_ge(eps_set, 1)
            fetch(0, 0)
            with act.Fori(0, TURNS - 1) as i:
                fetch(i, 1)
                fetch(i + 1, 0)
                root(i)
            fetch(TURNS - 1, 1)
            root(TURNS - 1)

        @block.gpsimd
        def _(pool):
            pool.sem_inc(taken, 2)
            pool.memset(spare[:, :], 0.0).then_inc(setup, 1)
            pool.wait_ge(setup, 1)
            with pool.Fori(0, TURNS) as i:
                for part, tiles in enumerate(PARTS):
                    pool.wait_ge(index_ready, i * 2 + part + 1)
                    pool.tensor_tensor(spare[:, 1 + part:2 + part], spare[:, 0:1], spare[:, 0:1], ALU.mult).then_inc(taken, 1)
                    for q in tiles:
                        for e in range(2):
                            pool.indirect_dma_start(res[:, q, e, :], None, s.results, bass.IndirectOffsetOnAxis(ap=index[:, e, q:q + 1], axis=0)).then_inc(row_in[q][e], 16)

        @block.vector
        def _(dve):
            link = Link(dve, link_sem)
            dve.sem_inc(y_ready, G)
            dve.sem_inc(o_ready, G)
            dve.memset(eps[:, :], LN_EPS).then_inc(eps_set, 1)
            dve.wait_ge(gamma_in, 16)
            with dve.Fori(0, TURNS) as i:
                link.loop(i, 2)
                w = lambda q, e: s.weight[:, ds(i * G + q, 1), e:e + 1].rearrange("p a e -> p (a e)")

                def second(q):
                    dve.wait_ge(row_in[q][1], 16 * i + 16)
                    dve.wait_ge(first_ready, i * G + q + 1)
                    dve.scalar_tensor_tensor(y[:, q, :], res[:, q, 1, :], w(q, 1), y[:, q, :], ALU.mult, ALU.add).then_inc(y_ready, 1)

                def stats_of(q):
                    dve.wait_ge(y_ready, i * G + q + 1 + G)
                    return dve.bn_stats(stats[:, q, :], y[:, q, :])
                for q in range(G):
                    dve.wait_ge(h_in[0 if q in PARTS[0] else 1], 16 * i + 16)
                    dve.wait_ge(row_in[q][0], 16 * i + 16)
                    dve.scalar_tensor_tensor(y[:, q, :], res[:, q, 0, :], w(q, 0), h[:, q, :], ALU.mult, ALU.add).then_inc(first_ready, 1)
                    if q:
                        stats_of(q - 1)
                    second(q)
                link(stats_of(G - 1))
                dve.memset(spare2[:, :], 0.0)
                for q in range(G):
                    last = dve.bn_aggr(mv[:, q, :], stats[:, q, :])
                last.then_inc(mv_ready, 1)
                dve.wait_ge(std_ready, i + 1)
                link(dve.reciprocal(rstd[:, :], std[:, :]))
                for q in range(G):
                    dve.scalar_tensor_tensor(y[:, q, :], y[:, q, :], mv[:, q, 0:1], scale[:, :], ALU.subtract, ALU.mult).then_inc(scaled, 1)
                dve.wait_ge(x1_in, 16 * i + 16)
                dve.wait_ge(out_out, 16 * i + 16)
                for q in range(G):
                    dve.wait_ge(scaled, i * G + q + 1)
                    dve.scalar_tensor_tensor(o[:, q, :], y[:, q, :], rstd[:, q:q + 1], x1[:, q, :], ALU.mult, ALU.add).then_inc(o_ready, 1)
                dve.wait_ge(o_ready, (i + 2) * G)


def laid_out(x, src, dst, edge_attr_64, L0_gnn_W, L0_gnn_A, L0_mix_kln_weight, L0_mix_kln_bias, L0_mix_vln_weight,
             L0_mix_vln_bias, L0_ffn_gate_w, L0_ffn_gate_b, L0_ffn_w1, L0_ffn_b1, L0_ffn_w2, L0_ffn_b2, L0_ffn_gamma, L0_ffn_beta):
    import numpy as np

    def padded(a, rows, fill=0):
        a = np.asarray(a)
        return np.concatenate([a, np.full((rows - a.shape[0],) + a.shape[1:], fill, a.dtype)])

    named = dict(
        x=padded(x, NP), src=padded(src, EP), dst=padded(dst, EP, N), edge_attr=padded(edge_attr_64, EP), W=L0_gnn_W, A=L0_gnn_A,
        kw=L0_mix_kln_weight, kb=L0_mix_kln_bias, vw=L0_mix_vln_weight, vb=L0_mix_vln_bias,
        gate_w=L0_ffn_gate_w, gate_b=L0_ffn_gate_b, w1=L0_ffn_w1, b1=L0_ffn_b1, w2=L0_ffn_w2, b2=L0_ffn_b2,
        gamma=L0_ffn_gamma, beta=L0_ffn_beta)
    return {f"in_{k}": np.ascontiguousarray(v) for k, v in named.items()}


def kernel(**inputs):
    import numpy as np
    import concourse.bacc as bacc
    from concourse.bass_utils import run_bass_kernel_spmd

    nc = bacc.Bacc("TRN2", target_bir_lowering=False, num_devices=1)
    arrays = laid_out(**inputs)
    args = [nc.dram_tensor(name, a.shape, mybir.dt.from_np(a.dtype), kind="ExternalInput").ap() for name, a in arrays.items()]
    args.append(nc.dram_tensor("out_rows", (NP, D), F32, kind="ExternalOutput").ap())
    build(nc, *args)
    r = run_bass_kernel_spmd(nc, [arrays], core_ids=[0])
    return np.asarray(r.results[0]["out_rows"])[:N]
```

```python
from contextlib import ExitStack

import concourse.bass as bass
from concourse import mybir

F32 = mybir.dt.float32
BF16 = mybir.dt.bfloat16
I32 = mybir.dt.int32
ALU = mybir.AluOpType
ACT = mybir.ActivationFunctionType
AX_X = mybir.AxisListType.X
DVE = mybir.EngineType.DVE
ds = bass.ds

P = 128
N, D, E, ED = 6250, 256, 100000, 64
HEADS, HC = 8, 32
NX, FF = 16, 512
DC, FC = D // P, FF // P
NT = 49
NP = NT * P
G = 7
ET = 784
EP = ET * P
RG = 7
RP = ET // RG
TC = 8
GU = 16
XB = 256
N_TURNS = (2 * N + NX * (XB - 1)) // XB + 1
ZERO_DMAS = 13
XL = -(-(N + XB) // P) * P
AWAY = NX * XL
LN_EPS = 1e-5
HEAD_EPS = 1e-5
SLOPE = 0.2
BIG = 1e30


class Link:

    def __init__(self, engine, semaphore, start=0):
        self.engine, self.semaphore, self.start = engine, semaphore, start
        self.count, self.turn, self.per = 0, None, 0

    def loop(self, turn, per):
        self.start += self.count
        self.turn, self.per, self.count = turn, per, 0

    def end_loop(self, turns):
        assert self.count == self.per, (self.count, self.per)
        self.start += turns * self.per
        self.turn, self.count = None, 0

    def __call__(self, ins):
        self.count += 1
        ins.then_inc(self.semaphore, 1)
        at = self.start + self.count
        if self.turn is not None:
            at = self.turn * self.per + at
        self.engine.wait_ge(self.semaphore, at)


def before(q, slots, per=G):
    if q >= slots:
        return slots
    return per - max(u for u in range(per) if u % slots == q % slots) + q


def prime(engine, s, semaphore):
    cell = s.prime[0:1, s.primed:s.primed + 1]
    s.primed += 1
    engine.dma_start(cell, s.gate_b[0:1].rearrange("(a b) -> a b", a=1)).then_inc(semaphore, 16)


def tiled(ap):
    return ap.rearrange("(t p) d -> t p d", p=P)


class Store:
    pass


def build(nc, x, src, dst, edge_attr, W, A, kw, kb, vw, vb, gate_w, gate_b, w1, b1, w2, b2, gamma, beta, out):
    s = Store()
    s.nc = nc
    s.x, s.src, s.dst, s.edge_attr, s.W, s.A = x, src, dst, edge_attr, W, A
    s.kw, s.kb, s.vw, s.vb = kw, kb, vw, vb
    s.gate_w, s.gate_b, s.w1, s.b1, s.w2, s.b2, s.gamma, s.beta, s.out = gate_w, gate_b, w1, b1, w2, b2, gamma, beta, out
    s.xn = nc.dram_tensor("xn_rows", (NP, D), F32, kind="Internal").ap()
    s.x1 = nc.dram_tensor("x1_rows", (NP, D), F32, kind="Internal").ap()
    s.lows = nc.dram_tensor("low_digits", (1, 2, EP), BF16, kind="Internal").ap()
    s.ea = nc.dram_tensor("edge_logits", (EP,), F32, kind="Internal").ap()
    s.src_by = nc.dram_tensor("sources_by_destination", (EP, 1), I32, kind="Internal").ap()
    s.dst_by = nc.dram_tensor("destinations_sorted", (EP, 1), I32, kind="Internal").ap()
    s.ea_by = nc.dram_tensor("edge_logits_by_destination", (EP, 1), F32, kind="Internal").ap()
    s.h = nc.dram_tensor("h_rows", (NP, D), F32, kind="Internal").ap()
    s.sorted = nc.dram_tensor("rows_by_expert", (AWAY + 2 * P, D), F32, kind="Internal").ap()
    s.results = nc.dram_tensor("results", (N_TURNS * XB, D), F32, kind="Internal").ap()
    s.bounce = nc.dram_tensor("row_ends", (8, ET, 2), F32, kind="Internal").ap()
    with ExitStack() as ctx:
        sb = lambda name, shape, dt: ctx.enter_context(nc.sbuf_tensor(name, shape, dt))
        s.semaphores = []
        s.prime, s.primed = sb("prime", [1, 16], F32), 0
        s.ident = sb("ident", [P, P], F32)
        s.iota_f = sb("iota_f", [P, P], F32)
        s.iota_p = sb("iota_p", [P, 1], F32)
        s.WT = sb("WT", [P, DC, D], F32)
        s.wsd = sb("wsd", [P, DC, 2], F32)
        s.KV = sb("KV", [P, DC, P], F32)
        s.blockmask = sb("blockmask", [P, P], F32)
        s.agg = sb("agg", [P, DC, NP + P], F32)
        with ExitStack() as edge_ctx:
            eb = lambda name, shape, dt: edge_ctx.enter_context(nc.sbuf_tensor(name, shape, dt))
            s.score_bits = eb("score_bits", [P, 2, 3, NT], BF16)
            s.high = eb("high", [P, 2, ET], BF16)
            s.edge_score = eb("edge_score", [P, 2, ET], F32)
            s.srcT = eb("srcT", [P, ET], I32)
            s.relT = eb("relT", [P, ET], F32)
            s.alphaT = eb("alphaT", [P, ET], F32)
            s.base = eb("base", [1, ET], I32)
            s.windows = eb("windows", [1, 1], I32)
            s.dst_f = eb("dst_f", [RP, RG, P], F32)
            s.unsorted = eb("unsorted", [1, 1], I32)
            constants(s)
            node_scores(s)
            sort_edges(s)
            edge_digits(s)
            table_lookup(s)
            edge_softmax(s)
            aggregate(s)
        nc.clear_and_free_semaphores(s.semaphores)
        nc.all_engine_barrier()
        s.semaphores = []
        s.best = sb("best", [P, NT, 2], F32)
        s.weight = sb("weight", [P, NT, 2], F32)
        s.result_row = sb("result_row", [P, 2, NT], I32)
        s.count = sb("count", [1, NX], I32)
        s.turns = sb("turns", [1, NX], I32)
        s.before = sb("before", [1, NX], I32)
        s.total = sb("total", [1, 1], I32)
        s.rank = sb("rank", [P, 2, NT], F32)
        s.expert = sb("expert", [P, 2, NT], F32)
        s.exp_f = sb("exp_f", [P, NX], F32)
        s.begins = sb("begins", [P, NX], F32)
        s.w1_sb = sb("w1_sb", [P, 2, DC, FF], F32)
        s.w2_sb = sb("w2_sb", [P, 2, FC, D], F32)
        s.b1_sb = sb("b1_sb", [P, 2, FC], F32)
        s.b2_sb = sb("b2_sb", [P, 2, D], F32)
        s.w_in = [nc.alloc_semaphore(f"w_in{r}") for r in range(2)]
        s.semaphores += s.w_in
        node_update(s)
        experts(s)
        final_norm(s)
        nc.clear_and_free_semaphores(s.semaphores)


def scope(s):
    ctx = ExitStack()
    sb = lambda name, shape, dt: ctx.enter_context(s.nc.sbuf_tensor(name, shape, dt))
    ps = lambda name, shape, dt=F32: ctx.enter_context(s.nc.psum_tensor(name, shape, dt))

    def sem(name):
        s.semaphores.append(s.nc.alloc_semaphore(name))
        return s.semaphores[-1]
    return ctx, sb, ps, sem


def constants(s):
    nc = s.nc
    ctx, sb, ps, sem = scope(s)
    with ctx:
        w_sb = sb("w_sb", [P, DC, D], F32)
        a_sb = sb("a_sb", [P, DC, 2], F32)
        fi = sb("fi", [P, P], I32)
        pi = sb("pi", [P, 1], I32)
        fb = sb("fb", [P, P], I32)
        pb = sb("pb", [P, 1], I32)
        fbf = sb("fbf", [P, P], F32)
        pbf = sb("pbf", [P, 1], F32)
        pT = [ps(f"pT{c}", [P, DC, P]) for c in range(DC)]
        pw = ps("pw", [P, DC, 2])
        here = sb("c_here", [RP, RG, P], I32)
        after = sb("c_after", [RP, RG, P], I32)
        here_f = sb("c_here_f", [RP, RG, P], F32)
        after_f = sb("c_after_f", [RP, RG, P], F32)
        falls = sb("c_falls", [RP, 1], F32)
        falls1 = sb("c_falls1", [1, 1], F32)
        p_falls = ps("c_p_falls", [1, RP])
        dst_in, falls_ready, falls_T, copied = map(sem, ["c_dst_in", "c_falls_ready", "c_falls_T", "c_copied"])
        w_loaded, ramps, const_link, ident_ready, wT_ready, wsd_ready = map(
            sem, ["c_w_loaded", "c_ramps", "c_link", "c_ident", "c_wT", "c_wsd"])
        block = ctx.enter_context(nc.Block())

        @block.sync
        def _(sp):
            by_row = lambda a: a.rearrange("(g p e) -> p g e", p=RP, e=P)
            sp.dma_start(here[:, :, :], by_row(s.dst[0:EP])).then_inc(dst_in, 16)
            sp.dma_start(after[:, :, :], by_row(s.dst[1:EP + 1])).then_inc(dst_in, 16)
            sp.dma_start(w_sb[:, :, :], s.W.rearrange("(c p) i -> p c i", p=P)).then_inc(w_loaded, 16)
            for k in range(2):
                for c in range(DC):
                    sp.dma_start(a_sb[:, c, k:k + 1], s.A[0, k * D + c * P:k * D + (c + 1) * P].rearrange("(p a) -> p a", a=1),
                                 allow_slow_non_contiguous=True).then_inc(w_loaded, 16)
            lines = lambda a: a.rearrange("(p e) -> p e", p=P)
            sp.dma_start(s.src_by.rearrange("(p e) a -> p (e a)", p=P), lines(s.src)).then_inc(copied, 16)
            sp.dma_start(s.dst_by.rearrange("(p e) a -> p (e a)", p=P), lines(s.dst[0:EP])).then_inc(copied, 16)
            sp.wait_ge(copied, 32)

        @block.gpsimd
        def _(pool):
            pool.iota(fi[:, :], [[1, P]], base=0, channel_multiplier=0).then_inc(ramps, 1)
            pool.iota(pi[:, :], [[0, 1]], base=0, channel_multiplier=1).then_inc(ramps, 1)

        @block.vector
        def _(dve):
            link = Link(dve, const_link)
            dve.wait_ge(ramps, 2)
            dve.tensor_copy(s.iota_f[:, :], fi[:, :])
            link(dve.tensor_copy(s.iota_p[:, :], pi[:, :]))
            dve.tensor_scalar(s.ident[:, :], s.iota_f[:, :], s.iota_p[:, 0:1], None, ALU.is_equal).then_inc(ident_ready, 1)
            shift = HC.bit_length() - 1
            link(dve.tensor_scalar(fb[:, :], fi[:, :], shift, None, ALU.logical_shift_right))
            link(dve.tensor_scalar(pb[:, :], pi[:, :], shift, None, ALU.logical_shift_right))
            link(dve.tensor_copy(fbf[:, :], fb[:, :]))
            link(dve.tensor_copy(pbf[:, :], pb[:, :]))
            link(dve.tensor_scalar(s.blockmask[:, :], fbf[:, :], pbf[:, 0:1], None, ALU.is_equal))
            dve.wait_ge(wT_ready, 2 * DC)
            for c in range(DC):
                dve.tensor_copy(s.WT[:, c, :].rearrange("p (o q) -> p o q", o=DC), pT[c][:, :, :])
            dve.wait_ge(wsd_ready, 1)
            dve.tensor_copy(s.wsd[:, :, :], pw[:, :, :])
            dve.wait_ge(dst_in, 32)
            link(dve.tensor_copy(here_f[:, :, :], here[:, :, :]))
            link(dve.tensor_copy(after_f[:, :, :], after[:, :, :]))
            link(dve.tensor_tensor(here_f[:, :, :], here_f[:, :, :], after_f[:, :, :], ALU.is_gt))
            dve.tensor_reduce(falls[:, :], here_f[:, :, :].rearrange("p g e -> p (g e)"), AX_X, ALU.max).then_inc(falls_ready, 1)
            dve.wait_ge(falls_T, 1)
            link(dve.tensor_reduce(falls1[:, :], p_falls[:, :], AX_X, ALU.max))
            dve.tensor_copy(s.unsorted[:, :], falls1[:, :])

        @block.tensor
        def _(pe):
            pe.wait_ge(w_loaded, 16 * (1 + 2 * DC))
            pe.wait_ge(ident_ready, 1)
            for c in range(DC):
                for o in range(DC):
                    pe.transpose(pT[c][:, o, :], w_sb[:, o, c * P:(c + 1) * P], s.ident[:, :]).then_inc(wT_ready, 1)
            for c in range(DC):
                for o in range(DC):
                    last = pe.matmul(pw[:, c, :], w_sb[:, o, c * P:(c + 1) * P], a_sb[:, o, :], start=(o == 0), stop=(o == DC - 1))
            last.then_inc(wsd_ready, 1)
            pe.wait_ge(falls_ready, 1)
            pe.transpose(p_falls[:, :], falls[:, :], s.ident[0:RP, 0:RP]).then_inc(falls_T, 1)


def node_scores(s):
    nc = s.nc
    ctx, sb, ps, sem = scope(s)
    with ctx:
        TURNS = NT // G
        EC = ET // NT
        EB = 2 * ED
        PC, VC = 4, 6
        RC = EC - PC
        PAIRS = PC // 2
        MID = G // 2 + 1
        xt = sb("xt", [P, G, D], F32)
        stats = sb("stats", [P, G, 6], F32)
        mv = sb("mv", [P, G, 2], F32)
        std = sb("a_std", [P, G], F32)
        rstd = sb("rstd", [P, G], F32)
        xn = sb("xn", [P, G, D], F32)
        xnT = sb("xnT", [P, 2, DC, P], F32)
        spare = sb("a_spare", [P, 1], F32)
        eps = sb("a_eps", [P, 1], F32)
        score = sb("score", [P, 2, NT], F32)
        rest = sb("rest", [P, 2, NT], F32)
        piece = sb("piece", [P, 2, NT], F32)
        attr = sb("a_attr", [P, G, EC * ED], F32)
        attrT = sb("a_attrT", [P, 2, PAIRS, P], F32)
        a_row = sb("a_a_row", [P, ED], F32)
        prod = sb("a_prod", [P, 2, RC, ED], F32)
        a_e = sb("a_a_e", [EB, 2], F32)
        ea = sb("a_ea", [P, ET], F32)
        pT = [ps(f"a_pT{j}", [P, DC, P]) for j in range(2)]
        pS = ps("a_pS", [P, 2 * NT])
        pEA = ps("a_pEA", [P, NT * PC])
        pE = [ps(f"a_pE{j}", [P, PAIRS, P]) for j in range(2)]
        x_in = [sem(f"a_x_in{q}") for q in range(G)]
        attr_in = [sem(f"a_attr_in{q}") for q in range(G)]
        x_used, xn_out, xnT_done, xnT_copied, score_done, mv_ready, std_ready, eps_set, link_sem = map(
            sem, ["a_x_used", "a_xn_out", "a_xnT_done", "a_xnT_copied", "a_score_done", "a_mv", "a_std_ready", "a_eps_set", "a_link"])
        a_in, a_zero, attrT_done, attrT_copied, ea_done, ea_ready, ea_out = map(
            sem, ["a_a_in", "a_a_zero", "a_attrT_done", "a_attrT_copied", "a_ea_done", "a_ea_ready", "a_ea_out"])
        prod_ready, pool_prod, dot_done = map(sem, ["a_prod_ready", "a_pool_prod", "a_dot_done"])
        x_t = tiled(s.x)
        xn_g = s.xn.rearrange("(i q p) d -> i p q d", q=G, p=P)
        attr_c = s.edge_attr.rearrange("(p c) d -> p (c d)", p=P)
        columns = lambda q, start, end: attr[:, q, start * ED:end * ED].rearrange("p (c d) -> p c d", d=ED)
        a_rows = lambda n: a_row[:, :].rearrange("p (a d) -> p a d", a=1).broadcast_to([P, n, ED])
        block = ctx.enter_context(nc.Block())

        @block.sync
        def _(sp):
            sp.wait_ge(a_zero, 1)
            for k in range(2):
                sp.dma_start(a_e[k * ED:(k + 1) * ED, k:k + 1], s.A[0, 2 * D:2 * D + ED].rearrange("(p a) -> p a", a=1),
                             allow_slow_non_contiguous=True).then_inc(a_in, 16)
            sp.dma_start(a_row[:, :], s.A[0:1, 2 * D:2 * D + ED].broadcast_to([P, ED])).then_inc(a_in, 16)
            with sp.Fori(0, TURNS) as i:
                for q in range(G):
                    k = i * G + q
                    sp.wait_ge(x_used, k + 1)
                    sp.dma_start(xt[:, q, :], x_t[ds(k, 1), :, :].rearrange("a p d -> p (a d)")).then_inc(x_in[q], 16)
                for q in range(G):
                    k = i * G + q
                    sp.wait_ge(attrT_done, k + 1)
                    sp.wait_ge(dot_done, k + 1)
                    sp.dma_start(attr[:, q, :], attr_c[:, ds(k * (EC * ED), EC * ED)]).then_inc(attr_in[q], 16)
            sp.wait_ge(ea_ready, 1)
            sp.dma_start(s.ea.rearrange("(p c) -> p c", p=P), ea[:, :]).then_inc(ea_out, 16)
            sp.dma_start(s.ea_by.rearrange("(p c) a -> p (c a)", p=P), ea[:, :]).then_inc(ea_out, 16)
            sp.wait_ge(ea_out, 32)

        @block.gpsimd
        def _(pool):
            pool.memset(a_e[:, :], 0.0).then_inc(a_zero, 1)
            pool.wait_ge(a_in, 48)
            with pool.Fori(0, TURNS) as i:
                for q in range(G):
                    k = i * G + q
                    pool.wait_ge(attr_in[q], 16 * i + 16)
                    pool.wait_ge(dot_done, k + G + 1 - before(q, 2))
                    pool.tensor_tensor(prod[:, q % 2, VC:, :], columns(q, PC + VC, EC), a_rows(EC - PC - VC), ALU.mult).then_inc(pool_prod, 1)

        @block.vector
        def _(dve):
            link = Link(dve, link_sem)
            dve.sem_inc(x_used, G)
            dve.memset(eps[:, :], LN_EPS).then_inc(eps_set, 1)

            def statistics(i):
                for q in range(G):
                    dve.wait_ge(x_in[q], 16 * i + 16)
                    last = dve.bn_stats(stats[:, q, :], xt[:, q, :])
                link(last)
                dve.memset(spare[:, :], 0.0)
                for q in range(G):
                    last = dve.bn_aggr(mv[:, q, :], stats[:, q, :])
                last.then_inc(mv_ready, 1)

            def norm(i):
                dve.wait_ge(std_ready, i + 1)
                link(dve.reciprocal(rstd[:, :], std[:, :]))
                dve.wait_ge(xn_out, 16 * i + 16)
                for q in range(G):
                    dve.wait_ge(xnT_done, i * G + q + 1)
                    dve.tensor_scalar(xn[:, q, :], xt[:, q, :], mv[:, q, 0:1], rstd[:, q:q + 1], ALU.subtract, ALU.mult).then_inc(x_used, 1)
                dve.wait_ge(x_used, (i + 2) * G)

            def dots(i, tiles):
                def sums(q):
                    k = i * G + q
                    dve.wait_ge(prod_ready, k + 1)
                    dve.wait_ge(pool_prod, k + 1)
                    dve.tensor_reduce(ea[:, ds(k * EC + PC, RC)], prod[:, q % 2], AX_X, ALU.add).then_inc(dot_done, 1)
                for q in tiles:
                    dve.wait_ge(attr_in[q], 16 * i + 16)
                    dve.wait_ge(dot_done, i * G + q + G + 1 - before(q, 2))
                    dve.tensor_tensor(prod[:, q % 2, 0:VC, :], columns(q, PC, PC + VC), a_rows(VC), ALU.mult).then_inc(prod_ready, 1)
                    if q:
                        sums(q - 1)
                if q == G - 1:
                    sums(q)

            dve.sem_inc(dot_done, G)
            dve.wait_ge(a_in, 48)
            statistics(0)
            with dve.Fori(0, TURNS - 1) as i:
                link.loop(i, 2)
                norm(i)
                dots(i, range(MID))
                statistics(i + 1)
                dots(i, range(MID, G))
            link.end_loop(TURNS - 1)
            norm(TURNS - 1)
            dots(TURNS - 1, range(G))
            dve.wait_ge(ea_done, NT + G)
            dve.wait_ge(dot_done, NT + G)
            dve.tensor_copy(ea[:, :].rearrange("p (t c) -> p t c", c=EC)[:, :, 0:PC], pEA[:, :].rearrange("p (t c) -> p t c", c=PC)).then_inc(ea_ready, 1)
            dve.wait_ge(score_done, NT + G)
            link(dve.tensor_copy(score[:, :, :], pS[:, :].rearrange("p (t k) -> p k t", k=2)))
            for m in range(3):
                frm = score if m == 0 else rest
                link(dve.tensor_copy(s.score_bits[:, :, m, :], frm[:, :, :]))
                link(dve.tensor_copy(piece[:, :, :], s.score_bits[:, :, m, :]))
                link(dve.tensor_tensor(rest[:, :, :], frm[:, :, :], piece[:, :, :], ALU.subtract))

        @block.scalar
        def _(act):
            act.wait_ge(eps_set, 1)
            act.sem_inc(xnT_copied, G)
            act.sem_inc(attrT_copied, G)
            prime(act, s, xn_out)

            def root(i):
                act.wait_ge(mv_ready, i + 1)
                act.activation(std[:, :], mv[:, :, 1], ACT.Sqrt, bias=eps[:, 0:1]).then_inc(std_ready, 1)

            def turn(i, root_of_next):
                for q in range(G):
                    k = i * G + q
                    if q == MID:
                        act.wait_ge(x_used, (i + 2) * G)
                        act.dma_start(xn_g[ds(i, 1)].rearrange("a p q d -> p (a q) d"), xn[:, :, :]).then_inc(xn_out, 16)
                        if root_of_next:
                            root(i + 1)
                    act.wait_ge(attrT_done, k + 1 + G)
                    act.wait_ge(ea_done, k + G + 1 - before(q, 2))
                    act.activation(attrT[:, q % 2], pE[q % 2][:, :, :], ACT.Identity).then_inc(attrT_copied, 1)
                    act.wait_ge(xnT_done, k + 1 + G)
                    act.wait_ge(score_done, k + G + 1 - before(q, 2))
                    act.activation(xnT[:, q % 2, :, :], pT[q % 2][:, :, :], ACT.Identity).then_inc(xnT_copied, 1)

            root(0)
            with act.Fori(0, TURNS - 1) as i:
                turn(i, True)
            turn(TURNS - 1, False)
            act.wait_ge(xn_out, 16 * (TURNS + 1))

        @block.tensor
        def _(pe):
            pe.sem_inc(xnT_done, G)
            pe.sem_inc(attrT_done, G)
            pe.sem_inc(score_done, G)
            pe.sem_inc(ea_done, G)
            pe.wait_ge(a_in, 48)
            with pe.Fori(0, TURNS) as i:
                def turn_in(q):
                    k = i * G + q
                    pe.wait_ge(attr_in[q], 16 * i + 16)
                    pe.wait_ge(attrT_copied, k + G + 1 - before(q, 2))
                    for m in range(PAIRS):
                        last = pe.transpose(pE[q % 2][:, m, :], attr[:, q, m * EB:(m + 1) * EB], s.ident[:, :])
                    last.then_inc(attrT_done, 1)
                    pe.wait_ge(x_used, k + 1 + G)
                    pe.wait_ge(xnT_copied, k + G + 1 - before(q, 2))
                    for c in range(DC):
                        last = pe.transpose(pT[q % 2][:, c, :], xn[:, q, c * P:(c + 1) * P], s.ident[:, :])
                    last.then_inc(xnT_done, 1)

                def products(q):
                    k = i * G + q
                    pe.wait_ge(attrT_copied, k + 1 + G)
                    for m in range(PAIRS):
                        last = pe.matmul(pEA[:, ds(k * PC + m * 2, 2)], attrT[:, q % 2, m, :], a_e[:, :], start=True, stop=True)
                    last.then_inc(ea_done, 1)
                    pe.wait_ge(xnT_copied, k + G + 1)
                    for c in range(DC):
                        last = pe.matmul(pS[:, ds(k * 2, 2)], xnT[:, q % 2, c, :], s.wsd[:, c, :], start=(c == 0), stop=(c == DC - 1))
                    last.then_inc(score_done, 1)
                turn_in(0)
                for q in range(1, G):
                    turn_in(q)
                    products(q - 1)
                products(G - 1)


def sort_edges(s):
    nc = s.nc
    ctx, sb, ps, sem = scope(s)
    with ctx:
        C = EP // NT
        col = lambda name, dt=F32: sb("o_" + name, [P, ET], dt)
        dst_f, number, rank = map(col, ["dst_f", "number", "rank"])
        src_i, dst_i, number_i, rank_i = (col(n, I32) for n in ("src_i", "dst_i", "number_i", "rank_i"))
        ea = col("ea")
        ramp_i = sb("o_ramp_i", [P, C], I32)
        ramp = sb("o_ramp", [P, C], F32)
        chunk_i = sb("o_chunk_i", [P, C], I32)
        chunk = sb("o_chunk", [P, C], F32)
        before_it = sb("o_before_it", [P, C], F32)
        counts = sb("o_counts", [P, C], F32)
        count = sb("o_count", [P, 1], F32)
        cell = [sb(f"o_cell{k}", [P, 1], dt) for k, dt in enumerate((I32, I32, F32, I32))]
        spare = sb("o_spare", [P, 3], F32)
        cols_in, chunk_in, chunk_used, ramps, link_sem, chunk_link, ranked, scattered, setup, cells_ready, taken, ended = map(
            sem, ["o_cols_in", "o_chunk_in", "o_chunk_used", "o_ramps", "o_link", "o_chunk_link", "o_ranked", "o_scattered", "o_setup",
                  "o_cells_ready", "o_taken", "o_ended"])
        block = ctx.enter_context(nc.Block())
        flag = lambda engine: engine.value_load(s.unsorted[0:1, 0:1], min_val=0, max_val=1)

        @block.sync
        def _(sp):
            with sp.If(flag(sp) > 0):
                for to, of in ((src_i, s.src), (dst_i, s.dst[0:EP]), (ea, s.ea)):
                    sp.dma_start(to[:, :], of.rearrange("(t p) -> p t", p=P), allow_slow_non_contiguous=True).then_inc(cols_in, 16)
                with sp.Fori(0, NT) as c:
                    sp.wait_ge(chunk_used, c + 1)
                    sp.dma_start(chunk_i[:, :], s.dst[0:EP].rearrange("(a e) -> a e", a=1)[:, ds(c * C, C)].broadcast_to([P, C])).then_inc(chunk_in, 16)

        @block.gpsimd
        def _(pool):
            with pool.If(flag(pool) > 0):
                pool.iota(number_i[:, :], [[P, ET]], base=0, channel_multiplier=1).then_inc(ramps, 1)
                pool.iota(ramp_i[:, :], [[1, C]], base=0, channel_multiplier=0).then_inc(ramps, 1)
                pool.memset(spare[:, :], 0.0).then_inc(setup, 1)
                pool.wait_ge(setup, 1)
                pool.wait_ge(cols_in, 48)
                pool.wait_ge(ranked, 1)
                with pool.Fori(0, ET) as t:
                    for to, of in zip(cell, (src_i, dst_i, ea, rank_i)):
                        pool.tensor_copy(to[:, :], of[:, ds(t, 1)]).then_inc(cells_ready, 1)
                    pool.wait_ge(cells_ready, t * 4 + 4)
                    pool.tensor_tensor(spare[:, 1:2], spare[:, 0:1], spare[:, 0:1], ALU.mult).then_inc(taken, 1)
                    for to, of in zip((s.src_by, s.dst_by, s.ea_by), cell):
                        pool.indirect_dma_start(to, bass.IndirectOffsetOnAxis(ap=cell[3][:, 0:1], axis=0), of[:, :], None).then_inc(scattered, 16)
                    pool.wait_ge(scattered, t * 48 + 48)
                    pool.tensor_tensor(spare[:, 2:3], spare[:, 0:1], spare[:, 0:1], ALU.mult).then_inc(ended, 1)

        @block.vector
        def _(dve):
            with dve.If(flag(dve) > 0):
                dve.sem_inc(chunk_used, 1)
                dve.wait_ge(ramps, 2)
                dve.wait_ge(cols_in, 48)
                link = Link(dve, chunk_link)
                link(dve.tensor_copy(dst_f[:, :], dst_i[:, :]))
                link(dve.tensor_copy(number[:, :], number_i[:, :]))
                link(dve.tensor_copy(ramp[:, :], ramp_i[:, :]))
                link(dve.memset(rank[:, :], 0.0))
                inner = Link(dve, link_sem)
                with dve.Fori(0, NT) as c:
                    link.loop(c, 2)
                    dve.wait_ge(chunk_in, 16 * c + 16)
                    dve.tensor_copy(chunk[:, :], chunk_i[:, :]).then_inc(chunk_used, 1)
                    dve.wait_ge(chunk_used, c + 2)
                    dve.memset(count[:, :], 0.0)
                    with dve.Fori(0, ET) as t:
                        inner.loop(c * ET + t, 5)
                        its = lambda a: a[:, ds(t, 1)]
                        inner(dve.tensor_scalar(before_it[:, :], ramp[:, :], its(number), None, ALU.is_lt))
                        inner(dve.scalar_tensor_tensor(before_it[:, :], chunk[:, :], its(dst_f), before_it[:, :], ALU.is_equal, ALU.mult))
                        inner(dve.scalar_tensor_tensor(counts[:, :], chunk[:, :], its(dst_f), before_it[:, :], ALU.is_lt, ALU.add))
                        inner(dve.tensor_reduce(count[:, :], counts[:, :], AX_X, ALU.add))
                        inner(dve.tensor_tensor(its(rank), its(rank), count[:, :], ALU.add))
                    link(dve.tensor_scalar(number[:, :], number[:, :], -float(C), None, ALU.add))
                    link(dve.memset(count[:, :], 0.0))
                dve.tensor_copy(rank_i[:, :], rank[:, :]).then_inc(ranked, 1)


def edge_digits(s):
    nc = s.nc
    ctx, sb, ps, sem = scope(s)
    with ctx:
        rows = sb("d_rows", [RP, 2, RG, P], I32)
        digit = sb("d_digit", [RP, 2, 2, RG, P], I32)
        high_f = sb("d_high_f", [RP, 2, RG, P], F32)
        low_b = sb("d_low_b", [RP, 2, RG, P], BF16)
        src_f = sb("d_src_f", [RP, RG, P], F32)
        HALF = 4
        pT = [[ps(f"d_pT{k}{h}", [P, HALF, RP]) for h in range(2)] for k in range(3)]
        rows_in, link_sem, low_ready, low_out, f_ready, T_done, base_in = map(
            sem, ["d_rows_in", "d_link", "d_low", "d_low_out", "d_f_ready", "d_T", "d_base_in"])
        block = ctx.enter_context(nc.Block())
        by_row = lambda a: a.rearrange("(g p e) -> p g e", p=RP, e=P)

        @block.sync
        def _(sp):
            in_rows = lambda a: a.rearrange("(g p e) a -> p g (e a)", p=RP, e=P)
            sp.dma_start(rows[:, 0, :, :], in_rows(s.src_by)).then_inc(rows_in, 16)
            sp.dma_start(rows[:, 1, :, :], in_rows(s.dst_by)).then_inc(rows_in, 16)
            sp.dma_start(s.base[:, :], s.dst_by.rearrange("(t e) a -> a t e", e=P)[:, :, 0], allow_slow_non_contiguous=True).then_inc(base_in, 16)
            sp.wait_ge(low_ready, 1)
            for k in range(2):
                sp.dma_start(by_row(s.lows[0, k, :]), low_b[:, k, :, :]).then_inc(low_out, 16)
            sp.wait_ge(low_out, 32)
            sp.wait_ge(base_in, 16)

        @block.vector
        def _(dve):
            link = Link(dve, link_sem)
            dve.wait_ge(rows_in, 32)
            link(dve.tensor_scalar(digit[:, 0], rows[:, :], 7, None, ALU.logical_shift_right))
            link(dve.tensor_scalar(digit[:, 1], rows[:, :], P - 1, None, ALU.bitwise_and))
            dve.tensor_copy(low_b[:, :], digit[:, 1]).then_inc(low_ready, 1)
            dve.tensor_copy(high_f[:, :], digit[:, 0]).then_inc(f_ready, 1)
            dve.tensor_copy(src_f[:, :], rows[:, 0]).then_inc(f_ready, 1)
            dve.tensor_copy(s.dst_f[:, :], rows[:, 1]).then_inc(f_ready, 1)
            dve.wait_ge(T_done, 1)
            for k in range(3):
                for h in range(2):
                    n = min(HALF, RG - HALF * h)
                    to = (s.high[:, k, :] if k < 2 else s.srcT[:, :])[:, HALF * h * RP:(HALF * h + n) * RP]
                    dve.tensor_copy(to.rearrange("p (g r) -> p g r", g=n), pT[k][h][:, 0:n, :])

        @block.tensor
        def _(pe):
            pe.wait_ge(f_ready, 3)
            for k in range(3):
                for g in range(RG):
                    of = high_f[:, k, g, :] if k < 2 else src_f[:, g, :]
                    last = pe.transpose(pT[k][g // HALF][:, g % HALF, :], of, s.ident[0:RP, 0:RP])
            last.then_inc(T_done, 1)


def table_lookup(s):
    nc = s.nc
    ctx, sb, ps, sem = scope(s)
    with ctx:
        R = 4
        CHUNKS = ET // TC
        TURNS, REST = CHUNKS // R, CHUNKS % R
        assert REST == 2
        low = sb("t_low", [P, R, 2, TC * P], BF16)
        onehot = sb("t_onehot", [P, R, 2, TC * P], BF16)
        ramp = sb("t_ramp", [P, NT], BF16)
        far = sb("t_far", [P, 2, TC * P], BF16)
        neg_p = sb("t_neg_p", [P, 1], F32)
        one = sb("t_one", [P, 1], F32)
        off = sb("t_off", [P, 2, 2, TC, NT], BF16)
        picked = sb("t_picked", [P, 2, 2, TC, NT], F32)
        pR = [[ps(f"t_pR{j}{k}", [P, TC, NT]) for k in range(2)] for j in range(R)]
        low_in = [sem(f"t_low_in{j}") for j in range(R)]
        low_used, low_far, hot_ready, rows_done, bias_set = map(sem, ["t_low_used", "t_low_far", "t_hot_ready", "t_rows", "t_bias_set"])
        off_ready, picked_ready, summed, ramp_ready = map(sem, ["t_off", "t_picked", "t_summed", "t_ramp_s"])
        block = ctx.enter_context(nc.Block())

        def chunks(engine, step):
            with engine.Fori(0, TURNS) as i:
                for j in range(R):
                    step(i, j)
            for j in range(REST):
                step(TURNS, j)

        @block.sync
        def _(sp):
            def load(i, j):
                k = R * i + j
                sp.wait_ge(low_used, k + 1)
                sp.wait_ge(low_far, k + 1)
                sp.dma_start(low[:, j, :, :], s.lows[:, :, ds(k * (TC * P), TC * P)].broadcast_to([P, 2, TC * P])).then_inc(low_in[j], 16)
            chunks(sp, load)

        @block.gpsimd
        def _(pool):
            pool.tensor_copy(ramp[:, :], s.iota_f[:, 0:NT]).then_inc(ramp_ready, 1)
            pool.wait_ge(ramp_ready, 1)

            def distances(i, j):
                k = R * i + j
                pool.wait_ge(picked_ready, 2 * k + 2)
                for q in range(2):
                    pool.tensor_tensor(
                        off[:, j % 2, q], ramp[:, :].rearrange("p (a n) -> p a n", a=1).broadcast_to([P, TC, NT]),
                        s.high[:, q, ds(k * TC, TC)].rearrange("p (t a) -> p t a", a=1).broadcast_to([P, TC, NT]),
                        ALU.subtract).then_inc(off_ready, 1)
            chunks(pool, distances)

        @block.vector
        def _(dve):
            dve.sem_inc(low_used, R)
            dve.sem_inc(picked_ready, 4)
            dve.sem_inc(summed, 2)
            dve.tensor_scalar(neg_p[:, :], s.iota_p[:, :], -1.0, None, ALU.mult).then_inc(bias_set, 1)
            dve.memset(one[:, :], 1.0).then_inc(bias_set, 1)

            def build(i, j):
                dve.wait_ge(low_in[j], 16 * i + 16)
                dve.wait_ge(rows_done, R * i + j + 1)
                dve.tensor_scalar(onehot[:, j, 0], low[:, j, 0], s.iota_p[:, 0:1], None, ALU.is_equal).then_inc(low_used, 1)

            def pick(i, j):
                k = R * i + j
                dve.wait_ge(rows_done, k + 1 + R)
                dve.wait_ge(summed, k + 1)
                for q in range(2):
                    dve.wait_ge(off_ready, 2 * k + q + 1)
                    dve.scalar_tensor_tensor(picked[:, j % 2, q], off[:, j % 2, q], 0.0, pR[j][q][:, :, :], ALU.is_equal, ALU.mult).then_inc(picked_ready, 1)
                if i is not TURNS:
                    build(i + (j + 2) // R, (j + 2) % R)
                dve.wait_ge(picked_ready, 2 * k + 6)
                dve.tensor_reduce(s.edge_score[:, :, ds(k * TC, TC)], picked[:, j % 2], AX_X, ALU.add).then_inc(summed, 1)

            for j in range(2):
                build(0, j)
            chunks(dve, pick)

        @block.scalar
        def _(act):
            act.sem_inc(low_far, R)
            act.wait_ge(bias_set, 2)

            def build(i, j):
                k = R * i + j
                act.wait_ge(low_in[j], 16 * i + 16)
                act.activation(far[:, j % 2], low[:, j, 1], ACT.Abs, bias=neg_p[:, 0:1]).then_inc(low_far, 1)
                act.wait_ge(low_far, k + 1 + R)
                act.wait_ge(rows_done, k + 1)
                act.activation(onehot[:, j, 1], far[:, j % 2], ACT.Relu, scale=-1.0, bias=one[:, 0:1]).then_inc(hot_ready, 1)
            chunks(act, build)

        @block.tensor
        def _(pe):
            pe.sem_inc(rows_done, R)

            def rows(i, j):
                k = R * i + j
                pe.wait_ge(low_used, k + 1 + R)
                pe.wait_ge(hot_ready, k + 1)
                pe.wait_ge(picked_ready, 2 * k + 2)
                for q in range(2):
                    for t in range(TC):
                        for m in range(3):
                            last = pe.matmul(pR[j][q][:, t, :], onehot[:, j, q, t * P:(t + 1) * P], s.score_bits[:, q, m, :],
                                             start=(m == 0), stop=(m == 2))
                last.then_inc(rows_done, 1)
            chunks(pe, rows)


def edge_softmax(s):
    nc = s.nc
    ctx, sb, ps, sem = scope(s)
    with ctx:
        row = lambda name: sb("s_" + name, [RP, RG, P], F32)
        g, sd, first, last, keep, fwd, top, total, e, em, ex = map(
            row, ["g", "sd", "first", "last", "keep", "fwd", "top", "total", "e", "em", "ex"])
        notfirst, tmp, in_first, in_last, rel, ea = map(row, ["notfirst", "tmp", "in_first", "in_last", "rel", "ea"])
        ends = sb("s_ends", [RP, RG, 2], F32)
        keys = sb("s_keys", [RP, RG, 2], F32)
        wide = sb("s_wide", [RP, RG, 2], F32)
        K2 = 2 * ET
        one = lambda name: sb("s1_" + name, [1, K2], F32)
        key1, val1, first1, last1, keep1, fwd1, tot1, reset1 = map(one, ["key", "val", "first", "last", "keep", "fwd", "tot", "reset"])
        span = sb("s_span", [1, ET], F32)
        span1 = sb("s_span1", [1, 1], F32)
        span_i = sb("s_span_i", [1, 1], I32)
        HALF = 4
        pT = [[ps(f"s_pT{k}{h}", [RP, HALF, P]) for h in range(2)] for k in range(2)]
        pB = [[ps(f"s_pB{k}{h}", [P, HALF, RP]) for h in range(2)] for k in range(2)]
        link_sem, ea_in, T_done, B_done, keys_ready, ends_ready, back_ready, exp_in, exp_done, out_ready, zeroed = map(
            sem, ["s_link", "s_ea_in", "s_T", "s_B", "s_keys_ready", "s_ends_ready", "s_back_ready", "s_exp_in", "s_exp", "s_out", "s_zeroed"])
        stored = [sem(f"s_stored{n}") for n in range(5)]
        line_in = [sem(f"s_line_in{n}") for n in range(3)]
        wide_in = [sem(f"s_wide_in{n}") for n in range(2)]
        block = ctx.enter_context(nc.Block())
        flat = lambda t: t[:, :, :].rearrange("p g e -> p (g e)")
        to_rows = lambda n: s.bounce[n].rearrange("(g p) k -> p g k", p=RP)
        to_line = lambda n: s.bounce[n].rearrange("(a t) k -> a (t k)", a=1)

        @block.gpsimd
        def _(pool):
            pool.memset(s.agg[:, :, :], 0.0)

        @block.sync
        def _(sp):
            sp.dma_start(ea[:, :, :], s.ea_by.rearrange("(g p e) a -> p g (e a)", p=RP, e=P)).then_inc(ea_in, 16)
            sp.wait_ge(keys_ready, 1)
            sp.dma_start(to_rows(0), keys[:, :, :]).then_inc(stored[0], 16)
            sp.wait_ge(stored[0], 16)
            sp.dma_start(key1[:, :], to_line(0)).then_inc(line_in[0], 16)
            for n in range(2):
                sp.wait_ge(ends_ready, n + 1)
                sp.dma_start(to_rows(1 + n), ends[:, :, :]).then_inc(stored[1 + n], 16)
                sp.wait_ge(stored[1 + n], 16)
                sp.dma_start(val1[:, :], to_line(1 + n)).then_inc(line_in[1 + n], 16)
                sp.wait_ge(back_ready, n + 1)
                sp.dma_start(to_line(3 + n), tot1[:, :]).then_inc(stored[3 + n], 16)
                sp.wait_ge(stored[3 + n], 16)
                sp.dma_start(wide[:, :, :], to_rows(3 + n)).then_inc(wide_in[n], 16)

        @block.vector
        def _(dve):
            link = Link(dve, link_sem)
            dst = s.dst_f
            bc = lambda col: col.broadcast_to([RP, RG, P])
            link(dve.tensor_copy(keys[:, :, 0:1], dst[:, :, 0:1]))
            dve.tensor_copy(keys[:, :, 1:2], dst[:, :, P - 1:P]).then_inc(keys_ready, 1)
            link(dve.memset(first[:, :, 0:1], 1.0))
            link(dve.memset(last[:, :, P - 1:P], 1.0))
            link(dve.tensor_tensor(first[:, :, 1:P], dst[:, :, 1:P], dst[:, :, 0:P - 1], ALU.not_equal))
            link(dve.tensor_copy(last[:, :, 0:P - 1], first[:, :, 1:P]))
            link(dve.tensor_scalar(keep[:, :, :], last[:, :, :], -1.0, 1.0, ALU.mult, ALU.add))
            link(dve.tensor_scalar(notfirst[:, :, :], first[:, :, :], -1.0, 1.0, ALU.mult, ALU.add))
            link(dve.tensor_scalar(first[:, :, :], first[:, :, :], -BIG, None, ALU.mult))
            link(dve.tensor_tensor(in_first[:, :, :], dst[:, :, :], bc(dst[:, :, 0:1]), ALU.is_equal))
            link(dve.tensor_tensor(in_last[:, :, :], dst[:, :, :], bc(dst[:, :, P - 1:P]), ALU.is_equal))
            link(dve.tensor_tensor(rel[:, :, :], dst[:, :, :], bc(dst[:, :, 0:1]), ALU.subtract))
            dve.wait_ge(T_done, 1)
            dve.wait_ge(ea_in, 16)
            for h in range(2):
                n = min(HALF, RG - HALF * h)
                gs = slice(HALF * h, HALF * h + n)
                link(dve.tensor_tensor(g[:, gs, :], pT[0][h][:, 0:n, :], ea[:, gs, :], ALU.add))
                link(dve.tensor_copy(sd[:, gs, :], pT[1][h][:, 0:n, :]))

            def runs(data, in_place_of_zero, op_reset, op, to):
                link(dve.tensor_tensor_scan(flat(fwd), in_place_of_zero, flat(data), 0.0, op_reset, op))
                link(dve.tensor_tensor(fwd[:, :, :], fwd[:, :, :], last[:, :, :], ALU.mult))
                link(dve.tensor_tensor_scan(flat(to)[:, ::-1], flat(keep)[:, ::-1], flat(fwd)[:, ::-1], 0.0, ALU.mult, ALU.add))
                link(dve.tensor_copy(ends[:, :, 0:1], to[:, :, 0:1]))
                dve.tensor_copy(ends[:, :, 1:2], to[:, :, P - 1:P]).then_inc(ends_ready, 1)

            def runs_over_rows(reset, op_reset, op):
                link(dve.tensor_tensor_scan(fwd1[:, :], reset, val1[:, :], 0.0, op_reset, op))
                link(dve.tensor_tensor(fwd1[:, :], fwd1[:, :], last1[:, :], ALU.mult))
                dve.tensor_tensor_scan(tot1[:, ::-1], keep1[:, ::-1], fwd1[:, ::-1], 0.0, ALU.mult, ALU.add).then_inc(back_ready, 1)

            runs(g, flat(first), ALU.add, ALU.max, top)
            dve.wait_ge(line_in[0], 16)
            link(dve.memset(first1[:, 0:1], 1.0))
            link(dve.memset(last1[:, K2 - 1:K2], 1.0))
            link(dve.tensor_tensor(first1[:, 1:K2], key1[:, 1:K2], key1[:, 0:K2 - 1], ALU.not_equal))
            link(dve.tensor_copy(last1[:, 0:K2 - 1], first1[:, 1:K2]))
            link(dve.tensor_scalar(keep1[:, :], last1[:, :], -1.0, 1.0, ALU.mult, ALU.add))
            link(dve.tensor_scalar(reset1[:, :], first1[:, :], -BIG, None, ALU.mult))
            pairs = lambda t: t[:, :].rearrange("a (t k) -> a t k", k=2)
            link(dve.tensor_tensor(span[:, :], pairs(key1)[:, :, 1], pairs(key1)[:, :, 0], ALU.subtract))
            link(dve.tensor_reduce(span1[:, :], span[:, :], AX_X, ALU.max))
            link(dve.tensor_copy(span_i[:, :], span1[:, :]))
            link(dve.tensor_scalar(span_i[:, :], span_i[:, :], 7, None, ALU.logical_shift_right))
            link(dve.tensor_scalar(s.windows[:, :], span_i[:, :], 1, None, ALU.add))
            dve.wait_ge(line_in[1], 16)
            runs_over_rows(reset1[:, :], ALU.add, ALU.max)
            dve.wait_ge(wide_in[0], 16)
            for k, part in enumerate((in_first, in_last)):
                link(dve.tensor_scalar(tmp[:, :, :], part[:, :, :], 1.0, BIG, ALU.subtract, ALU.mult))
                link(dve.tensor_tensor(tmp[:, :, :], tmp[:, :, :], bc(wide[:, :, k:k + 1]), ALU.add))
                link(dve.tensor_tensor(top[:, :, :], top[:, :, :], tmp[:, :, :], ALU.max))
            for value, to in ((g, e), (top, em)):
                link(dve.tensor_tensor(value[:, :, :], value[:, :, :], sd[:, :, :], ALU.add))
                link(dve.scalar_tensor_tensor(flat(to), flat(value), SLOPE, flat(value), ALU.mult, ALU.max))
            dve.tensor_tensor(e[:, :, :], e[:, :, :], em[:, :, :], ALU.subtract).then_inc(exp_in, 1)
            dve.wait_ge(exp_done, 1)
            runs(ex, flat(notfirst), ALU.mult, ALU.add, total)
            dve.wait_ge(line_in[2], 16)
            link(dve.tensor_tensor(pairs(val1)[:, :, 1], pairs(val1)[:, :, 1], pairs(first1)[:, :, 1], ALU.mult))
            link(dve.tensor_scalar(first1[:, :], first1[:, :], -1.0, 1.0, ALU.mult, ALU.add))
            runs_over_rows(first1[:, :], ALU.mult, ALU.add)
            dve.wait_ge(wide_in[1], 16)
            for k, part in enumerate((in_first, in_last)):
                link(dve.tensor_tensor(tmp[:, :, :], part[:, :, :], bc(wide[:, :, k:k + 1]), ALU.mult))
                link(dve.tensor_tensor(total[:, :, :], total[:, :, :], tmp[:, :, :], ALU.max))
            link(dve.reciprocal(tmp[:, :, :], total[:, :, :]))
            dve.tensor_tensor(ex[:, :, :], ex[:, :, :], tmp[:, :, :], ALU.mult).then_inc(out_ready, 1)
            dve.wait_ge(B_done, 1)
            for k, to in enumerate((s.alphaT, s.relT)):
                for h in range(2):
                    n = min(HALF, RG - HALF * h)
                    dve.tensor_copy(to[:, HALF * h * RP:(HALF * h + n) * RP].rearrange("p (g r) -> p g r", g=n), pB[k][h][:, 0:n, :])

        @block.scalar
        def _(act):
            act.wait_ge(exp_in, 1)
            act.activation(flat(ex), flat(e), ACT.Exp).then_inc(exp_done, 1)

        @block.tensor
        def _(pe):
            for k in range(2):
                for gg in range(RG):
                    done = pe.transpose(pT[k][gg // HALF][:, gg % HALF, :], s.edge_score[:, k, gg * RP:(gg + 1) * RP], s.ident[:, :])
            done.then_inc(T_done, 1)
            pe.wait_ge(out_ready, 1)
            for k, of in enumerate((ex, rel)):
                for gg in range(RG):
                    done = pe.transpose(pB[k][gg // HALF][:, gg % HALF, :], of[:, gg, :], s.ident[0:RP, 0:RP])
            done.then_inc(B_done, 1)


def aggregate(s):
    nc = s.nc
    ctx, sb, ps, sem = scope(s)
    with ctx:
        assert ET // GU == NT
        BANKS = 6
        SLOTS = 8
        index = sb("g_index", [P, GU], I32)
        spare = sb("g_spare", [P, 3], F32)
        rows = sb("g_rows", [P, GU, D], F32)
        place = sb("g_place", [P, GU, P], F32)
        ramp = sb("g_ramp", [P, P], F32)
        base = sb("g_base", [1, ET], I32)
        pA = [ps(f"g_pA{b}", [P, DC, P]) for b in range(BANKS)]
        hx = sb("g_hx", [P, D], F32)
        hsum = sb("g_hsum", [P, HEADS], F32)
        dev = sb("g_dev", [P, D], F32)
        sq = sb("g_sq", [P, D], F32)
        hvar = sb("g_hvar", [P, HEADS], F32)
        hstd = sb("g_hstd", [P, HEADS], F32)
        hinv = sb("g_hinv", [P, HEADS], F32)
        nh = sb("g_nh", [P, DC, P + 1], F32)
        zrow = sb("g_zrow", [1, P + 1], F32)
        gram = sb("g_gram", [P, DC, P + 1], F32)
        ones = sb("g_ones", [P, P], F32)
        diag = sb("g_diag", [P, DC, P], F32)
        cols = sb("g_cols", [P, 2, DC], F32)
        mix_rows = sb("g_mix_rows", [P, 2, D], F32)
        kx = sb("g_kx", [P, DC, P], F32)
        kcol = sb("g_kcol", [P, DC, 1], F32)
        pG = [ps(f"g_pG{c}", [P, 512]) for c in range(DC)]
        hx_in, hx_used, hsum_ready, dev_ready, sq_ready, hvar_ready, hstd_ready, heps_ready, hinv_ready, nh_ready = map(
            sem, ["g_hx_in", "g_hx_used", "g_hsum_ready", "g_dev_ready", "g_sq_ready", "g_hvar_ready", "g_hstd_ready", "g_heps_ready", "g_hinv_ready", "g_nh_ready"])
        gram_used, zeroed, gram_all, mix_in, diag_ready, bc_done = map(
            sem, ["g_gram_used", "g_zeroed", "g_gram_all", "g_mix_in", "g_diag_ready", "g_bc_done"])
        kv_link = sem("g_kv_link")
        row_in = [sem(f"g_row_in{q}") for q in range(GU)]
        index_ready, placed, summed, added, link_sem, setup, taken = map(sem, ["g_index_ready", "g_placed", "g_summed", "g_added", "g_link", "g_setup", "g_taken"])
        ZR = N_TURNS * XB // P // ZERO_DMAS
        zero = sb("g_zero", [P, ZR * D], F32)
        zero_set, zero_out = sem("g_zero_set"), sem("g_zero_out")
        block = ctx.enter_context(nc.Block())
        TURNS = ET // GU

        @block.sync
        def _(sp):
            flat = lambda w: w.rearrange("h a c -> (h a c)")
            for k, w in enumerate((s.kw, s.kb)):
                for c in range(DC):
                    sp.dma_start(cols[:, k, c:c + 1], flat(w)[c * P:(c + 1) * P].rearrange("(p a) -> p a", a=1),
                                 allow_slow_non_contiguous=True).then_inc(mix_in, 16)
            for k, w in enumerate((s.vw, s.vb)):
                sp.dma_start(mix_rows[:, k, :], w.rearrange("h a c -> a (h c)").broadcast_to([P, D])).then_inc(mix_in, 16)
            windows = sp.value_load(s.windows[0:1, 0:1], min_val=1, max_val=NT)
            with sp.Fori(0, windows) as w:
                with sp.Fori(0, TURNS) as i:
                    sp.wait_ge(hx_used, w * TURNS + i + 1)
                    sp.dma_start(hx[:, :], tiled(s.xn)[ds(i, 1), :, :].rearrange("a p d -> p (a d)")).then_inc(hx_in, 16)
            sp.wait_ge(zero_set, 1)
            to = s.results.rearrange("(z p r) d -> z p (r d)", z=ZERO_DMAS, p=P)
            for z in range(ZERO_DMAS):
                sp.dma_start(to[z], zero[:, :]).then_inc(zero_out, 16)
            sp.wait_ge(zero_out, 16 * ZERO_DMAS)

        @block.scalar
        def _(act):
            windows = act.value_load(s.windows[0:1, 0:1], min_val=1, max_val=NT)
            with act.Fori(0, windows) as w:
                with act.Fori(0, TURNS) as i:
                    turn = w * TURNS + i
                    for h in range(GU // SLOTS):
                        act.wait_ge(summed, turn * GU + SLOTS * (h + 1))
                        act.wait_ge(taken, turn * 2 + h + 1)
                        act.activation(index[:, h * SLOTS:(h + 1) * SLOTS], s.srcT[:, ds(i * GU + h * SLOTS, SLOTS)], ACT.Copy).then_inc(index_ready, 1)
                    act.wait_ge(dev_ready, turn + 1)
                    act.activation(sq[:, :], dev[:, :], ACT.Square).then_inc(sq_ready, 1)
                    act.wait_ge(hvar_ready, turn + 1)
                    act.activation(hstd[:, :], hvar[:, :], ACT.Sqrt, scale=1.0 / (HC - 1)).then_inc(hstd_ready, 1)

        @block.gpsimd
        def _(pool):
            pool.sem_inc(taken, 2)
            pool.memset(spare[:, :], 0.0).then_inc(setup, 1)
            pool.wait_ge(setup, 1)
            windows = pool.value_load(s.windows[0:1, 0:1], min_val=1, max_val=NT)
            with pool.Fori(0, windows) as w:
                with pool.Fori(0, TURNS) as i:
                    turn = w * TURNS + i
                    for q in range(GU):
                        if q % SLOTS == 0:
                            pool.wait_ge(index_ready, turn * (GU // SLOTS) + q // SLOTS + 1)
                            pool.tensor_tensor(spare[:, 1 + q // SLOTS:2 + q // SLOTS], spare[:, 0:1], spare[:, 0:1], ALU.mult).then_inc(taken, 1)
                        pool.indirect_dma_start(rows[:, q, :], None, s.xn, bass.IndirectOffsetOnAxis(ap=index[:, q:q + 1], axis=0)).then_inc(row_in[q], 16)

        @block.vector
        def _(dve):
            link = Link(dve, link_sem)
            dve.sem_inc(added, GU)
            windows = dve.value_load(s.windows[0:1, 0:1], min_val=1, max_val=NT)
            dve.sem_inc(hx_used, 1)
            dve.memset(zrow[:, :], 0.0).then_inc(zeroed, 1)
            dve.memset(zero[:, :], 0.0).then_inc(zero_set, 1)
            dve.memset(nh[:, :, P:P + 1], 1.0).then_inc(zeroed, 1)
            dve.memset(ones[:, :], 1.0).then_inc(zeroed, 1)

            def head_sums(turn):
                dve.wait_ge(hx_in, 16 * turn + 16)
                dve.tensor_reduce(hsum[:, :], heads(hx), AX_X, ALU.add).then_inc(hsum_ready, 1)

            def head_deviates(turn):
                dve.wait_ge(hsum_ready, turn + 1)
                dve.scalar_tensor_tensor(heads(dev), wide(hsum), -1.0 / HC, heads(hx), ALU.mult, ALU.add).then_inc(dev_ready, 1)

            def head_variances(turn):
                dve.wait_ge(dev_ready, turn + 1)
                dve.sem_inc(hx_used, 1)
                dve.wait_ge(sq_ready, turn + 1)
                dve.tensor_reduce(hvar[:, :], heads(sq), AX_X, ALU.add).then_inc(hvar_ready, 1)

            def head_eps(turn):
                dve.wait_ge(hstd_ready, turn + 1)
                dve.tensor_scalar(hstd[:, :], hstd[:, :], HEAD_EPS, None, ALU.add).then_inc(heps_ready, 1)

            def head_inverses(turn):
                dve.wait_ge(heps_ready, turn + 1)
                dve.reciprocal(hinv[:, :], hstd[:, :]).then_inc(hinv_ready, 1)

            def head_norms(turn):
                dve.wait_ge(hinv_ready, turn + 1)
                dve.wait_ge(gram_used, turn + 1)
                dve.tensor_tensor(nh[:, :, 0:P].rearrange("p c (h e) -> p c h e", h=HEADS // DC), dev[:, :].rearrange("p (c h e) -> p c h e", c=DC, e=HC),
                                  hinv[:, :].rearrange("p (c h a) -> p c h a", c=DC, a=1).broadcast_to([P, DC, HEADS // DC, HC]), ALU.mult).then_inc(nh_ready, 1)
            heads = lambda a: a[:, :].rearrange("p (h c) -> p h c", h=HEADS)
            wide = lambda a: a[:, :].rearrange("p (h a) -> p h a", a=1).broadcast_to([P, HEADS, HC])
            STEPS = {1: head_sums, 2: head_deviates, 6: head_variances, 10: head_eps, 11: head_inverses, 12: head_norms}
            link(dve.tensor_copy(ramp[:, :], s.iota_f[:, :]))
            link(dve.tensor_copy(base[:, :], s.base[:, :]))
            with dve.Fori(0, windows) as w:
                link.loop(w, 2)
                with dve.Fori(0, TURNS) as i:
                    turn = w * TURNS + i
                    _, starts = nc.values_load_multi_w_load_instructions(
                        base[0:1, ds(i * GU, GU)], engines=[DVE], min_val=0, max_val=NP,
                        skip_runtime_bounds_check_because="destinations are nodes, and later windows are held at NP")
                    for q in range(GU):
                        col = i * GU + q
                        dve.tensor_scalar(place[:, q, :], ramp[:, :], s.relT[:, ds(col, 1)], s.alphaT[:, ds(col, 1)],
                                          ALU.is_equal, ALU.mult).then_inc(placed, 1)
                    for q in range(GU):
                        dve.wait_ge(summed, turn * GU + q + 1 + GU)
                        dve.wait_ge(added, turn * GU + q + GU)
                        window = s.agg[:, :, ds(starts[q], P)]
                        dve.tensor_tensor(window, window, pA[q % BANKS][:, :, :], ALU.add).then_inc(added, 1)
                        if q in STEPS:
                            STEPS[q](turn)
                    dve.wait_ge(nh_ready, turn + 1)
                dve.wait_ge(added, (w + 1) * ET + GU)
                link(dve.tensor_scalar(ramp[:, :], ramp[:, :], float(P), None, ALU.add))
                link(dve.tensor_scalar(base[:, :], base[:, :], float(P), float(NP), ALU.add, ALU.min))
            link = Link(dve, kv_link)
            dve.wait_ge(gram_all, windows)
            for c in range(DC):
                link(dve.tensor_copy(gram[:, c, :], pG[c][:, 0:P + 1]))
            for c in range(DC):
                dve.tensor_scalar(diag[:, c, :], s.ident[:, :], gram[:, c, P:P + 1], None, ALU.mult).then_inc(diag_ready, 1)
            dve.wait_ge(bc_done, 1)
            dve.wait_ge(mix_in, 16 * (2 * DC + 2))
            for c in range(DC):
                vcols = slice(c * P, (c + 1) * P)
                link(dve.tensor_scalar(kx[:, c, :], gram[:, c, 0:P], cols[:, 0, c:c + 1], None, ALU.mult))
                link(dve.scalar_tensor_tensor(kx[:, c, :], pA[0][:, c, :], cols[:, 1, c:c + 1], kx[:, c, :], ALU.mult, ALU.add))
                link(dve.tensor_tensor(kx[:, c, :], kx[:, c, :], mix_rows[:, 0, vcols], ALU.mult))
                link(dve.tensor_scalar(kcol[:, c, :], gram[:, c, P:P + 1], cols[:, 0, c:c + 1], None, ALU.mult))
                link(dve.scalar_tensor_tensor(kcol[:, c, :], cols[:, 1, c:c + 1], float(N), kcol[:, c, :], ALU.mult, ALU.add))
                link(dve.scalar_tensor_tensor(kx[:, c, :], mix_rows[:, 1, vcols], kcol[:, c, 0:1], kx[:, c, :], ALU.mult, ALU.add))
                link(dve.scalar_tensor_tensor(s.KV[:, c, :], kx[:, c, :], 1.0 / N, s.blockmask[:, :], ALU.mult, ALU.mult))
                link(dve.tensor_tensor(s.KV[:, c, :], s.KV[:, c, :], s.ident[:, :], ALU.add))

        @block.tensor
        def _(pe):
            pe.sem_inc(summed, GU)
            pe.sem_inc(gram_used, 1)
            windows = pe.value_load(s.windows[0:1, 0:1], min_val=1, max_val=NT)
            pe.wait_ge(zeroed, 3)
            with pe.Fori(0, windows) as w:
                for c in range(DC):
                    pe.matmul(pG[c][:, 0:P + 1], zrow[:, 0:P], zrow[:, :], start=True, stop=False)
                with pe.Fori(0, TURNS) as i:
                    turn = w * TURNS + i
                    for q in range(GU):
                        pe.wait_ge(row_in[q], 16 * turn + 16)
                        pe.wait_ge(placed, turn * GU + q + 1)
                        pe.wait_ge(added, turn * GU + q + 1 + GU - before(q, BANKS, GU))
                        for c in range(DC):
                            last = pe.matmul(pA[q % BANKS][:, c, :], rows[:, q, c * P:(c + 1) * P], place[:, q, :], start=True, stop=True)
                        last.then_inc(summed, 1)
                    pe.wait_ge(nh_ready, turn + 1)
                    for c in range(DC):
                        last = pe.matmul(pG[c][:, 0:P + 1], nh[:, c, 0:P], nh[:, c, :], start=False, stop=False)
                    last.then_inc(gram_used, 1)
                for c in range(DC):
                    last = pe.matmul(pG[c][:, 0:P + 1], zrow[:, 0:P], zrow[:, :], start=False, stop=True)
                last.then_inc(gram_all, 1)
            pe.wait_ge(diag_ready, DC)
            for c in range(DC):
                last = pe.matmul(pA[0][:, c, :], ones[:, :], diag[:, c, :], start=True, stop=True)
            last.then_inc(bc_done, 1)


def load_expert(s, sp, r, e):
    sp.dma_start(s.w1_sb[:, r], s.w1[ds(e, 1), :, :].rearrange("a (c p) f -> p (a c) f", p=P)).then_inc(s.w_in[r], 16)
    sp.dma_start(s.w2_sb[:, r], s.w2[ds(e, 1), :, :].rearrange("a (c p) f -> p (a c) f", p=P)).then_inc(s.w_in[r], 16)
    sp.dma_start(s.b1_sb[:, r], s.b1[ds(e, 1), :].rearrange("a (c p) -> p (a c)", p=P), allow_slow_non_contiguous=True).then_inc(s.w_in[r], 16)
    sp.dma_start(s.b2_sb[:, r], s.b2[ds(e, 1), :].broadcast_to([P, D])).then_inc(s.w_in[r], 16)


def node_update(s):
    nc = s.nc
    ctx, sb, ps, sem = scope(s)
    with ctx:
        TURNS = NT // G
        FIRST = 2
        xt = sb("u_xt", [P, G, D], F32)
        xn = sb("u_xn", [P, G, D], F32)
        aggs = sb("u_aggs", [P, 2, DC, P], F32)
        xnT = sb("u_xnT", [P, 2, DC, P], F32)
        x1 = sb("u_x1", [P, G, D], F32)
        x1b = sb("u_x1b", [P, G, D], F32)
        beta = sb("u_beta", [P, D], F32)
        h = sb("u_h", [P, G, D], F32)
        h_rows = sb("u_h_rows", [P, G, D], F32)
        hT = sb("u_hT", [P, 2, DC, P], F32)
        stats = sb("u_stats", [P, G, 6], F32)
        mv = sb("u_mv", [P, G, 2], F32)
        std = sb("u_std", [P, G], F32)
        rstd = sb("u_rstd", [P, G], F32)
        eps = sb("u_eps", [P, 1], F32)
        spare = sb("u_spare", [P, 1], F32)
        gate = sb("u_gate", [P, DC, NX], F32)
        gate_b = sb("u_gate_b", [P, NX], F32)
        logit = sb("u_logit", [P, G, NX], F32)
        best = sb("u_best", [P, G, 8], F32)
        which = sb("u_which", [P, G, 8], mybir.dt.uint32)
        pT = [ps(f"u_pT{j}", [P, DC, P]) for j in range(2)]
        pX = [ps(f"u_pX{j}", [P, D]) for j in range(4)]
        pL = ps("u_pL", [P, G, NX])
        pP = ps("u_pP", [P, G, NX])
        which_f = sb("u_which_f", [P, G, 2], F32)
        hot = sb("u_hot", [P, 2, G, NX], F32)
        both = sb("u_both", [P, G, NX], BF16)
        seen = sb("u_seen", [P, NX], F32)
        seen_b = sb("u_seen_b", [P, NX], BF16)
        new = sb("u_new", [P, NX], F32)
        picked = sb("u_picked", [P, 2, G, NX], F32)
        slot_f = sb("u_slot_f", [P, 2, G], F32)
        index = sb("u_index", [P, 2, G], I32)
        node_i = sb("u_node_i", [P, NT], I32)
        node_f = sb("u_node_f", [P, NT], F32)
        exp_i = sb("u_exp_i", [P, NX], I32)
        valid = sb("u_valid", [P, NT], F32)
        no_expert = sb("u_no_expert", [P, NT], F32)
        away = sb("u_away", [P, 2, NT], F32)
        earlier = sb("u_earlier", [P, P], BF16)
        ones = sb("u_ones", [P, P], BF16)
        turns_i = sb("u_turns_i", [P, NX], I32)
        turns_f = sb("u_turns_f", [P, NX], F32)
        keep1 = sb("u_keep1", [P, NX], F32)
        ends = sb("u_ends", [P, NX], F32)
        zero = sb("u_zero", [P, XB // P * D], F32)
        counts_set = sem("u_counts_set")
        tails_out = [sem(f"u_tails_out{half}") for half in range(2)]
        scatter_spare = sb("u_scatter_spare", [P, 4], F32)
        ramps, setup, ranks_ready, both_ready, placed, slots_ready, taken, scattered, rows_free, counted, h_copied = map(
            sem, ["u_ramps", "u_setup", "u_ranks_ready", "u_both", "u_placed", "u_slots", "u_taken", "u_scattered", "u_rows_free", "u_counted", "u_h_copied"])
        in_x = [sem(f"u_in_x{q}") for q in range(G)]
        in_xn = [sem(f"u_in_xn{q}") for q in range(G)]
        eps_set, gate_in, x1_ready, xnT_done, xnT_copied, aggs_ready, x_done, mv_ready, std_ready, h_ready = map(
            sem, ["u_eps_set", "u_gate_in", "u_x1_ready", "u_xnT_done", "u_xnT_copied", "u_aggs_ready", "u_x_done", "u_mv_ready", "u_std_ready", "u_h_ready"])
        hT_done, hT_copied, logit_done, logit_read, link_sem, top_ready, x1b_ready, x1b_out, h_out = map(
            sem, ["u_hT_done", "u_hT_copied", "u_logit_done", "u_logit_read", "u_link", "u_top", "u_x1b_ready", "u_x1b_out", "u_h_out"])
        x_t, xn_t = tiled(s.x), tiled(s.xn)
        turn_of = lambda a, i: a.rearrange("(i q p) d -> i p q d", q=G, p=P)[ds(i, 1)].rearrange("a p q d -> p (a q) d")
        block = ctx.enter_context(nc.Block())
        tile = lambda a, k: a[ds(k, 1), :, :].rearrange("a p d -> p (a d)")

        def tails(engine, half):
            engine.wait_ge(counts_set, 1)
            with engine.Fori(half * NX // 2, (half + 1) * NX // 2) as e:
                rows_of_expert = engine.value_load(s.count[0:1, ds(e, 1)], min_val=0, max_val=N)
                engine.dma_start(s.sorted[ds(rows_of_expert + e * XL, XB), :].rearrange("(p r) d -> p (r d)", p=P), zero[:, :]).then_inc(tails_out[half], 16)
            engine.wait_ge(tails_out[half], 8 * NX)

        @block.sync
        def _(sp):
            sp.dma_start(gate[:, :, :], s.gate_w.rearrange("(c p) e -> p c e", p=P)).then_inc(gate_in, 16)
            sp.dma_start(gate_b[:, :], s.gate_b.rearrange("(a e) -> a e", a=1).broadcast_to([P, NX])).then_inc(gate_in, 16)
            sp.dma_start(beta[:, :], s.beta.rearrange("(a d) -> a d", a=1).broadcast_to([P, D])).then_inc(gate_in, 16)
            with sp.Fori(0, TURNS) as i:
                for q in range(G):
                    k = i * G + q
                    sp.wait_ge(xnT_done, k + 1)
                    sp.dma_start(xn[:, q, :], tile(xn_t, k)).then_inc(in_xn[q], 16)
                    sp.wait_ge(x1_ready, k + 1)
                    sp.dma_start(xt[:, q, :], tile(x_t, k)).then_inc(in_x[q], 16)
            load_expert(s, sp, 0, 0)
            tails(sp, 0)

        @block.gpsimd
        def _(pool):
            pool.iota(node_i[:, :], [[P, NT]], base=0, channel_multiplier=1).then_inc(ramps, 1)
            pool.iota(exp_i[:, :], [[1, NX]], base=0, channel_multiplier=0).then_inc(ramps, 1)
            pool.memset(scatter_spare[:, :], 0.0).then_inc(setup, 1)
            pool.wait_ge(setup, 1)
            pool.wait_ge(gate_in, 48)
            pool.sem_inc(rows_free, 1)
            with pool.Fori(0, TURNS) as i:
                for q in range(G):
                    pool.wait_ge(x1_ready, i * G + q + 1 + G)
                    pool.tensor_tensor(x1b[:, q, :], x1[:, q, :], beta[:, :], ALU.add).then_inc(x1b_ready, 1)
                pool.wait_ge(x1b_ready, (i + 2) * G)
                pool.tensor_tensor(scatter_spare[:, 3:4], scatter_spare[:, 0:1], scatter_spare[:, 0:1], ALU.mult).then_inc(taken, 1)
                pool.dma_start(turn_of(s.x1, i), x1b[:, :, :]).then_inc(x1b_out, 16)
                pool.wait_ge(slots_ready, i + 1)
                pool.wait_ge(h_copied, i + 2)
                pool.tensor_tensor(scatter_spare[:, 1:2], scatter_spare[:, 0:1], scatter_spare[:, 0:1], ALU.mult).then_inc(taken, 1)
                for q in range(G):
                    for k in range(2):
                        pool.indirect_dma_start(s.sorted, bass.IndirectOffsetOnAxis(ap=index[:, k, q:q + 1], axis=0), h_rows[:, q, :], None).then_inc(scattered, 16)
                pool.wait_ge(x1b_out, 16 * i + 16)
                pool.wait_ge(scattered, i * (2 * G * 16) + 2 * G * 16)
                pool.tensor_tensor(scatter_spare[:, 2:3], scatter_spare[:, 0:1], scatter_spare[:, 0:1], ALU.mult).then_inc(rows_free, 1)

        @block.vector
        def _(dve):
            link = Link(dve, link_sem)
            dve.sem_inc(x1_ready, G)
            dve.sem_inc(x1b_ready, G)
            dve.sem_inc(logit_read, 1)
            link(dve.memset(zero[:, :], 0.0))
            dve.memset(eps[:, :], LN_EPS).then_inc(eps_set, 1)
            dve.wait_ge(ramps, 2)
            link(dve.tensor_copy(node_f[:, :], node_i[:, :]))
            link(dve.tensor_copy(s.exp_f[:, :], exp_i[:, :]))
            link(dve.tensor_scalar(valid[:, :], node_f[:, :], float(N), None, ALU.is_lt))
            link(dve.tensor_scalar(no_expert[:, :], valid[:, :], -float(NX), float(NX), ALU.mult, ALU.add))
            for k in range(2):
                link(dve.tensor_scalar(away[:, k, :], node_f[:, :], float(AWAY + k * P - (NP - P)), None, ALU.add))
                link(dve.scalar_tensor_tensor(away[:, k, :], no_expert[:, :], 1.0 / NX, away[:, k, :], ALU.mult, ALU.mult))
            link(dve.tensor_scalar(earlier[:, :], s.iota_f[:, :], s.iota_p[:, 0:1], None, ALU.is_gt))
            link(dve.memset(ones[:, :], 1.0))
            link(dve.memset(seen[:, :], 0.0))
            dve.memset(seen_b[:, :], 0.0).then_inc(ranks_ready, 1)
            dve.wait_ge(gate_in, 48)
            over_e = lambda a: a.rearrange("p (g a) -> p g a", a=1).broadcast_to([P, G, NX])
            node_cols = lambda a, i: a[:, ds(i * G, G)]
            with dve.Fori(0, TURNS) as i:
                link.loop(i, 13)
                def stats_of(q):
                    dve.wait_ge(x1_ready, i * G + q + 1 + G)
                    return dve.bn_stats(stats[:, q, :], x1[:, q, :])
                dve.wait_ge(x1b_ready, (i + 1) * G)
                for q in range(G):
                    dve.wait_ge(in_x[q], 16 * i + 16)
                    dve.wait_ge(x_done, i * G + q + 1 + G)
                    dve.tensor_tensor(x1[:, q, :], pX[q % 4][:, :], xt[:, q, :], ALU.add).then_inc(x1_ready, 1)
                    if q:
                        stats_of(q - 1)
                link(stats_of(G - 1))
                dve.memset(spare[:, :], 0.0)
                for q in range(G):
                    last = dve.bn_aggr(mv[:, q, :], stats[:, q, :])
                last.then_inc(mv_ready, 1)
                dve.wait_ge(std_ready, i + 1)
                link(dve.reciprocal(rstd[:, :], std[:, :]))
                dve.wait_ge(h_copied, i + 1)
                dve.wait_ge(hT_done, (i + 1) * G)
                for q in range(G):
                    dve.tensor_scalar(h[:, q, :], x1[:, q, :], mv[:, q, 0:1], rstd[:, q:q + 1], ALU.subtract, ALU.mult).then_inc(h_ready, 1)
                dve.wait_ge(logit_done, (i + 2) * G)
                dve.tensor_tensor(logit[:, :, :], pL[:, :, :], gate_b[:, :].rearrange("p (a e) -> p a e", a=1).broadcast_to([P, G, NX]), ALU.add).then_inc(logit_read, 1)
                dve.wait_ge(logit_read, i + 2)
                dve.memset(spare[:, :], 0.0)
                for q in range(G):
                    last = dve.max(best[:, q, :], logit[:, q, :])
                link(last)
                dve.memset(spare[:, :], 0.0)
                for q in range(G):
                    last = dve.max_index(which[:, q, :], best[:, q, :], logit[:, q, :])
                link(last)
                dve.tensor_copy(s.best[:, ds(i * G, G), :], best[:, :, 0:2])
                dve.tensor_copy(which_f[:, :, :], which[:, :, 0:2]).then_inc(top_ready, 1)
                dve.wait_ge(top_ready, i + 1)
                link(dve.tensor_tensor(which_f[:, :, :], which_f[:, :, :], node_cols(no_expert, i).rearrange("p (g a) -> p g a", a=1).broadcast_to([P, G, 2]), ALU.add))
                for k in range(2):
                    last = dve.tensor_tensor(hot[:, k], s.exp_f[:, :].rearrange("p (a e) -> p a e", a=1).broadcast_to([P, G, NX]), over_e(which_f[:, :, k]), ALU.is_equal)
                link(last)
                dve.tensor_tensor(both[:, :, :], hot[:, 0], hot[:, 1], ALU.add).then_inc(both_ready, 1)
                dve.wait_ge(both_ready, i + 1)
                link(dve.tensor_reduce(new[:, :], both[:, :, :].rearrange("p g e -> p e g"), AX_X, ALU.add))
                link(dve.tensor_tensor(seen[:, :], seen[:, :], new[:, :], ALU.add))
                dve.wait_ge(placed, i + 1)
                dve.tensor_copy(seen_b[:, :], seen[:, :])
                for k in range(2):
                    last = dve.tensor_tensor(picked[:, k], pP[:, :, :], hot[:, k], ALU.mult)
                last.then_inc(ranks_ready, 1)
                dve.wait_ge(ranks_ready, i + 2)
                link(dve.tensor_reduce(slot_f[:, :, :], picked[:, :], AX_X, ALU.add))
                dve.tensor_copy(s.rank[:, :, ds(i * G, G)], slot_f[:, :, :])
                link(dve.tensor_copy(s.expert[:, :, ds(i * G, G)], which_f[:, :, :].rearrange("p g k -> p k g")))
                link(dve.scalar_tensor_tensor(slot_f[:, :, :], which_f[:, :, :].rearrange("p g k -> p k g"), float(XL), slot_f[:, :, :], ALU.mult, ALU.add))
                over_k = lambda a: a.rearrange("p (a g) -> p a g", a=1).broadcast_to([P, 2, G])
                link(dve.tensor_tensor(slot_f[:, :, :], slot_f[:, :, :], over_k(node_cols(valid, i)), ALU.mult))
                link(dve.tensor_tensor(slot_f[:, :, :], slot_f[:, :, :], away[:, :, ds(i * G, G)], ALU.add))
                dve.wait_ge(rows_free, i + 1)
                dve.tensor_copy(index[:, :, :], slot_f[:, :, :]).then_inc(slots_ready, 1)
                dve.wait_ge(slots_ready, i + 1)
            link.end_loop(TURNS)
            dve.wait_ge(counted, 1)
            counts = pP[:, 0, :]
            dve.tensor_copy(s.count[:, :], counts[0:1, :]).then_inc(counts_set, 1)
            link(dve.tensor_scalar(turns_f[:, :], counts, float(XB - 1), float(XB), ALU.add, ALU.max))
            link(dve.tensor_copy(turns_i[:, :], turns_f[:, :]))
            link(dve.tensor_scalar(turns_i[:, :], turns_i[:, :], XB.bit_length() - 1, None, ALU.logical_shift_right))
            link(dve.tensor_copy(s.turns[:, :], turns_i[0:1, :]))
            link(dve.tensor_copy(turns_f[:, :], turns_i[:, :]))
            link(dve.memset(keep1[:, :], 1.0))
            link(dve.tensor_tensor_scan(ends[:, :], keep1[:, :], turns_f[:, :], 0.0, ALU.mult, ALU.add))
            link(dve.tensor_copy(s.total[:, :], ends[0:1, NX - 1:NX]))
            link(dve.tensor_tensor(ends[:, :], ends[:, :], turns_f[:, :], ALU.subtract))
            link(dve.tensor_copy(s.before[:, :], ends[0:1, :]))
            link(dve.tensor_scalar(s.begins[:, :], ends[:, :], float(XB), None, ALU.mult))

        @block.scalar
        def _(act):
            act.wait_ge(eps_set, 1)
            act.sem_inc(xnT_copied, G)
            act.sem_inc(hT_copied, G)
            act.sem_inc(h_copied, 1)
            prime(act, s, h_out)

            def for_x(i, tiles):
                for q in tiles:
                    k = i * G + q
                    act.wait_ge(x_done, k + G + 1 - before(q, 2))
                    act.activation(aggs[:, q % 2, :, :], s.agg[:, :, ds(k * P, P)], ACT.Identity).then_inc(aggs_ready, 1)
                    act.wait_ge(xnT_done, k + 1 + G)
                    act.activation(xnT[:, q % 2, :, :], pT[q % 2][:, :, :], ACT.Identity).then_inc(xnT_copied, 1)

            def for_h(i):
                act.wait_ge(mv_ready, i + 1)
                act.activation(std[:, :], mv[:, :, 1], ACT.Sqrt, bias=eps[:, 0:1]).then_inc(std_ready, 1)
                for q in range(G):
                    k = i * G + q
                    act.wait_ge(hT_done, k + 1 + G)
                    act.wait_ge(logit_done, k + G + 1 - before(q, 2))
                    act.activation(hT[:, q % 2, :, :], pT[q % 2][:, :, :], ACT.Identity).then_inc(hT_copied, 1)

            def copy_h(i):
                act.wait_ge(h_out, 16 * i + 16)
                act.wait_ge(rows_free, i + 1)
                act.activation(h_rows[:, :, :], h[:, :, :], ACT.Identity).then_inc(h_copied, 1)
                act.wait_ge(h_copied, i + 2)
                act.dma_start(turn_of(s.h, i), h_rows[:, :, :]).then_inc(h_out, 16)

            for_x(0, range(FIRST))
            with act.Fori(0, TURNS - 1) as i:
                for_x(i, range(FIRST, G))
                for_h(i)
                for_x(i + 1, range(FIRST))
                copy_h(i)
            for_x(TURNS - 1, range(FIRST, G))
            for_h(TURNS - 1)
            copy_h(TURNS - 1)
            act.wait_ge(h_out, 16 * (TURNS + 1))
            tails(act, 1)

        @block.tensor
        def _(pe):
            pe.sem_inc(xnT_done, G)
            pe.sem_inc(x_done, G)
            pe.sem_inc(hT_done, G)
            pe.sem_inc(logit_done, G)
            pe.wait_ge(gate_in, 48)

            def turn_xn(i, q):
                k = i * G + q
                pe.wait_ge(in_xn[q], 16 * i + 16)
                pe.wait_ge(xnT_copied, k + G + 1 - before(q, 2))
                for c in range(DC):
                    last = pe.transpose(pT[q % 2][:, c, :], xn[:, q, c * P:(c + 1) * P], s.ident[:, :])
                last.then_inc(xnT_done, 1)

            def sum_x(i, q):
                k = i * G + q
                pe.wait_ge(x1_ready, k + G + 1 - before(q, 4))
                pe.wait_ge(aggs_ready, k + 1)
                for c in range(DC):
                    pe.matmul(pX[q % 4][:, :], aggs[:, q % 2, c, :], s.WT[:, c, :], start=(c == 0), stop=False)
                pe.wait_ge(xnT_copied, k + 1 + G)
                for c in range(DC):
                    last = pe.matmul(pX[q % 4][:, c * P:(c + 1) * P], xnT[:, q % 2, c, :], s.KV[:, c, :], start=False, stop=(c == DC - 1))
                last.then_inc(x_done, 1)

            def turn_h(i, q):
                k = i * G + q
                pe.wait_ge(h_ready, k + 1)
                pe.wait_ge(hT_copied, k + G + 1 - before(q, 2))
                for c in range(DC):
                    last = pe.transpose(pT[q % 2][:, c, :], h[:, q, c * P:(c + 1) * P], s.ident[:, :])
                last.then_inc(hT_done, 1)

            def logits(i, q):
                k = i * G + q
                pe.wait_ge(hT_copied, k + 1 + G)
                if q == 0:
                    pe.wait_ge(logit_read, i + 1)
                for c in range(DC):
                    last = pe.matmul(pL[:, q, :], hT[:, q % 2, c, :], gate[:, c, :], start=(c == 0), stop=(c == DC - 1))
                last.then_inc(logit_done, 1)

            def steps(i, turn, use, tiles):
                for q in tiles:
                    turn(i, q)
                    if q:
                        use(i, q - 1)
                if q == G - 1:
                    use(i, q)

            def places(i):
                pe.wait_ge(ranks_ready, i + 1)
                pe.wait_ge(both_ready, i + 1)
                pe.matmul(pP[:, :, :], ones[:, :], seen_b[:, :].rearrange("p (a e) -> p a e", a=1).broadcast_to([P, G, NX]), start=True, stop=False)
                pe.matmul(pP[:, :, :], earlier[:, :], both[:, :, :], start=False, stop=False)
                for q in range(G - 1):
                    last = pe.matmul(pP[:, q + 1:G, :], ones[:, :], both[:, q:q + 1, :].broadcast_to([P, G - 1 - q, NX]), start=False, stop=(q == G - 2))
                last.then_inc(placed, 1)

            steps(0, turn_xn, sum_x, range(FIRST))
            with pe.Fori(0, TURNS - 1) as i:
                steps(i, turn_xn, sum_x, range(FIRST, G))
                steps(i, turn_h, logits, range(G))
                steps(i + 1, turn_xn, sum_x, range(FIRST))
                places(i)
            steps(TURNS - 1, turn_xn, sum_x, range(FIRST, G))
            steps(TURNS - 1, turn_h, logits, range(G))
            places(TURNS - 1)
            pe.wait_ge(ranks_ready, TURNS + 1)
            pe.matmul(pP[:, 0, :], ones[:, :], seen_b[:, :], start=True, stop=True).then_inc(counted, 1)


def experts(s):
    nc = s.nc
    ctx, sb, ps, sem = scope(s)
    with ctx:
        B = XB // P
        w1, w2, b1, b2, w_in = s.w1_sb, s.w2_sb, s.b1_sb, s.b2_sb, s.w_in
        begin = sb("x_begin", [P, 2 * NT, NX], F32)
        delta = sb("x_delta", [P, NT], F32)
        ex = sb("x_ex", [P, NT], F32)
        den = sb("x_den", [P, NT], F32)
        link_sem, delta_ready, exp_ready = map(sem, ["x_link", "x_delta_ready", "x_exp_ready"])
        zero = sb("x_zero", [P, 1], F32)
        spare = sb("x_spare", [P, 1], F32)
        taken = sem("x_taken")
        rows = sb("x_rows", [P, B, D], F32)
        xT = sb("x_xT", [P, DC, XB], F32)
        hid = sb("x_hid", [P, FC, XB], F32)
        res = sb("x_res", [P, B, D], F32)
        done = sb("x_done", [1, 1], F32)
        end = sb("x_end", [1, 1], F32)
        pT = [ps(f"x_pT{b}", [P, DC, P]) for b in range(B)]
        pH = [ps(f"x_pH{f}", [P, XB]) for f in range(FC)]
        pY = [ps(f"x_pY{b}", [P, D]) for b in range(B)]
        row_in = [sem(f"x_row_in{b}") for b in range(B)]
        res_out = [sem(f"x_res_out{b}") for b in range(B)]
        w_used, rows_T, xT_ready, hid_done, hid_ready, y_done, res_ready, setup = map(
            sem, ["x_w_used", "x_rows_T", "x_xT_ready", "x_hid_done", "x_hid_ready", "x_y_done", "x_res_ready", "x_setup"])
        block = ctx.enter_context(nc.Block())

        def turns(engine, body, first=None, after=None, peeled=0):
            def two(pair):
                for r in range(2):
                    e = 2 * pair + r
                    if first is not None:
                        first(pair, r, e)
                    count = engine.value_load(s.turns[0:1, ds(e, 1)], min_val=1, max_val=-(-N // XB))
                    start = engine.value_load(s.before[0:1, ds(e, 1)], min_val=0, max_val=N_TURNS - 1)
                    with engine.Fori(0, count) as b:
                        turn = nc.s_assert_within(start + b, 0, N_TURNS - 1, skip_runtime_bounds_check_because="all experts' turns are at most N_TURNS")
                        body(e, r, b, turn)
                    if after is not None:
                        after(r, e, start + count)

            with engine.Fori(0, NX // 2 - peeled) as pair:
                two(pair)
            for pair in range(NX // 2 - peeled, NX // 2):
                two(pair)

        @block.sync
        def _(sp):
            def load_next(pair, r, e):
                if isinstance(e, int) and e + 1 == NX:
                    return
                sp.wait_ge(w_used, e + 1)
                load_expert(s, sp, 1 - r, e + 1)

            def body(e, r, b, n):
                for q in range(B):
                    sp.wait_ge(res_ready, n * B + q + 1 + B)
                    sp.dma_start(s.results[ds((n * B + q) * P, P), :], res[:, q, :]).then_inc(res_out[q], 16)
            for q in range(B):
                prime(sp, s, res_out[q])
            turns(sp, body, load_next, peeled=1)

        @block.scalar
        def _(act):
            def first(pair, r, e):
                act.wait_ge(w_in[r], 64 * pair + 64)

            def transposed(n):
                for q in range(B):
                    act.wait_ge(rows_T, n * B + q + 1 + B)
                    act.activation(xT[:, :, q * P:(q + 1) * P], pT[q][:, :, :], ACT.Identity).then_inc(xT_ready, 1)

            def body(e, r, b, n):
                for f in range(FC):
                    act.wait_ge(hid_done, n * FC + f + 1)
                    act.activation(hid[:, f, :], pH[f][:, :], ACT.Relu, bias=b1[:, r, f:f + 1]).then_inc(hid_ready, 1)
                transposed(n + 1)
            act.wait_ge(delta_ready, 1)
            act.activation(ex[:, :], delta[:, :], ACT.Exp).then_inc(exp_ready, 1)
            transposed(0)
            turns(act, body, first)

        @block.gpsimd
        def _(pool):
            pool.memset(zero[:, :], 0.0).then_inc(setup, 1)
            pool.wait_ge(setup, 1)

            def body(e, r, b, n):
                for q in range(B):
                    pool.wait_ge(rows_T, n * B + q + 1)
                    pool.dma_start(rows[:, q, :], s.sorted[ds(e * XL + (b * B + q) * P, P), :]).then_inc(row_in[q], 16)
            turns(pool, body)
            total = pool.value_load(s.total[0:1, 0:1], min_val=NX, max_val=N_TURNS)
            pool.wait_ge(rows_T, total * B + B)
            pool.tensor_tensor(spare[:, :], zero[:, 0:1], zero[:, 0:1], ALU.mult).then_inc(taken, 1)
            pool.wait_ge(taken, 1)
            for q in range(B):
                pool.dma_start(rows[:, q, :], s.sorted[q * P:(q + 1) * P, :]).then_inc(row_in[q], 16)

        @block.tensor
        def _(pe):
            pe.sem_inc(rows_T, B)

            def first(pair, r, e):
                pe.wait_ge(w_in[r], 64 * pair + 64)

            def transpose(n):
                for q in range(B):
                    pe.wait_ge(row_in[q], 16 * n + 16)
                    for c in range(DC):
                        last = pe.transpose(pT[q][:, c, :], rows[:, q, c * P:(c + 1) * P], s.ident[:, :])
                    last.then_inc(rows_T, 1)

            def body(e, r, b, n):
                pe.wait_ge(xT_ready, n * B + B)
                for f in range(FC):
                    for c in range(DC):
                        last = pe.matmul(pH[f][:, :], w1[:, r, c, f * P:(f + 1) * P], xT[:, c, :], start=(c == 0), stop=(c == DC - 1))
                    last.then_inc(hid_done, 1)
                transpose(n + 1)
                for q in range(B):
                    pe.wait_ge(res_ready, n * B + q + 1)
                    for f in range(FC):
                        if q == 0:
                            pe.wait_ge(hid_ready, n * FC + f + 1)
                        last = pe.matmul(pY[q][:, :], hid[:, f, q * P:(q + 1) * P], w2[:, r, f, :], start=(f == 0), stop=(f == FC - 1))
                    last.then_inc(y_done, 1)
            transpose(0)
            turns(pe, body, first)

        @block.vector
        def _(dve):
            dve.sem_inc(res_ready, B)
            dve.sem_inc(w_used, 1)
            link = Link(dve, link_sem)
            dve.tensor_tensor(delta[:, :], s.best[:, :, 1], s.best[:, :, 0], ALU.subtract).then_inc(delta_ready, 1)
            wide_e = lambda a: a.rearrange("p (t e) -> p t e", t=1).broadcast_to([P, 2 * NT, NX])
            all_k = lambda a: a[:, :, :].rearrange("p k t -> p (k t)")
            link(dve.tensor_tensor(begin[:, :, :], wide_e(s.exp_f[:, :]), all_k(s.expert).rearrange("p (t a) -> p t a", a=1).broadcast_to([P, 2 * NT, NX]), ALU.is_equal))
            link(dve.tensor_tensor(begin[:, :, :], begin[:, :, :], wide_e(s.begins[:, :]), ALU.mult))
            link(dve.tensor_reduce(all_k(s.expert), begin[:, :, :], AX_X, ALU.add))
            link(dve.tensor_tensor(s.rank[:, :, :], s.rank[:, :, :], s.expert[:, :, :], ALU.add))
            link(dve.tensor_copy(s.result_row[:, :, :], s.rank[:, :, :]))
            dve.wait_ge(exp_ready, 1)
            link(dve.tensor_scalar(den[:, :], ex[:, :], 1.0, None, ALU.add))
            link(dve.reciprocal(s.weight[:, :, 0], den[:, :]))
            link(dve.tensor_tensor(s.weight[:, :, 1], s.weight[:, :, 0], ex[:, :], ALU.mult))

            def first(pair, r, e):
                dve.wait_ge(w_in[r], 64 * pair + 64)

            def body(e, r, b, n):
                for q in range(B):
                    dve.wait_ge(y_done, n * B + q + 1)
                    dve.wait_ge(res_out[q], 16 * n + 16)
                    dve.tensor_tensor(res[:, q, :], pY[q][:, :], b2[:, r, :], ALU.add).then_inc(res_ready, 1)
            def after(r, e, n):
                dve.wait_ge(res_ready, n * B + B)
                dve.wait_ge(w_used, e + 1)
                dve.memset(done[:, :], 0.0).then_inc(w_used, 1)
            turns(dve, body, first, after)
            total = dve.value_load(s.total[0:1, 0:1], min_val=NX, max_val=N_TURNS)
            for q in range(B):
                dve.wait_ge(res_out[q], total * 16 + 16)
            dve.memset(end[:, :], 0.0)


def final_norm(s):
    nc = s.nc
    ctx, sb, ps, sem = scope(s)
    with ctx:
        TURNS = NT // G
        PARTS = (range(0, 4), range(4, G))
        x1 = sb("f_x1", [P, G, D], F32)
        h = sb("f_h", [P, G, D], F32)
        res = sb("f_res", [P, G, 2, D], F32)
        index = sb("f_index", [P, 2, G], I32)
        y = sb("f_y", [P, G, D], F32)
        o = sb("f_o", [P, G, D], F32)
        scale = sb("f_gamma", [P, D], F32)
        stats = sb("f_stats", [P, G, 6], F32)
        mv = sb("f_mv", [P, G, 2], F32)
        std = sb("f_std", [P, G], F32)
        rstd = sb("f_rstd", [P, G], F32)
        eps = sb("f_eps", [P, 1], F32)
        spare = sb("f_spare", [P, 3], F32)
        spare2 = sb("f_spare2", [P, 1], F32)
        row_in = [[sem(f"f_row_in{q}{k}") for k in range(2)] for q in range(G)]
        h_in = [sem(f"f_h_in{part}") for part in range(2)]
        x1_in, out_out, gamma_in, eps_set, index_ready, first_ready, y_ready, mv_ready, std_ready, scaled, o_ready, link_sem, taken, setup = map(
            sem, ["f_x1_in", "f_out", "f_gamma_in", "f_eps_set", "f_index_ready", "f_first", "f_y", "f_mv", "f_std_s", "f_scaled", "f_o_ready", "f_link", "f_taken", "f_setup"])
        turn_of = lambda a, i: a.rearrange("(i q p) d -> i p q d", q=G, p=P)[ds(i, 1)].rearrange("a p q d -> p (a q) d")
        h_t = tiled(s.h).rearrange("t p d -> p t d")
        block = ctx.enter_context(nc.Block())

        @block.sync
        def _(sp):
            sp.dma_start(scale[:, :], s.gamma.rearrange("(a d) -> a d", a=1).broadcast_to([P, D])).then_inc(gamma_in, 16)
            prime(sp, s, out_out)
            with sp.Fori(0, TURNS) as i:
                sp.wait_ge(o_ready, (i + 1) * G)
                sp.dma_start(x1[:, :, :], turn_of(s.x1, i)).then_inc(x1_in, 16)
                sp.wait_ge(o_ready, (i + 2) * G)
                sp.dma_start(turn_of(s.out, i), o[:, :, :]).then_inc(out_out, 16)
            sp.wait_ge(out_out, 16 * (TURNS + 1))

        @block.scalar
        def _(act):
            def fetch(i, part):
                tiles = PARTS[part]
                act.wait_ge(y_ready, i * G + tiles[-1] + 1)
                act.wait_ge(taken, i * 2 + part + 1)
                cols = slice(tiles[0], tiles[-1] + 1)
                act.activation(index[:, :, cols], s.result_row[:, :, ds(i * G + tiles[0], len(tiles))], ACT.Copy).then_inc(index_ready, 1)
                act.dma_start(h[:, cols, :], h_t[:, ds(i * G + tiles[0], len(tiles)), :]).then_inc(h_in[part], 16)

            def root(i):
                act.wait_ge(mv_ready, i + 1)
                act.activation(std[:, :], mv[:, :, 1], ACT.Sqrt, bias=eps[:, 0:1]).then_inc(std_ready, 1)

            act.wait_ge(eps_set, 1)
            fetch(0, 0)
            with act.Fori(0, TURNS - 1) as i:
                fetch(i, 1)
                fetch(i + 1, 0)
                root(i)
            fetch(TURNS - 1, 1)
            root(TURNS - 1)

        @block.gpsimd
        def _(pool):
            pool.sem_inc(taken, 2)
            pool.memset(spare[:, :], 0.0).then_inc(setup, 1)
            pool.wait_ge(setup, 1)
            with pool.Fori(0, TURNS) as i:
                for part, tiles in enumerate(PARTS):
                    pool.wait_ge(index_ready, i * 2 + part + 1)
                    pool.tensor_tensor(spare[:, 1 + part:2 + part], spare[:, 0:1], spare[:, 0:1], ALU.mult).then_inc(taken, 1)
                    for q in tiles:
                        for e in range(2):
                            pool.indirect_dma_start(res[:, q, e, :], None, s.results, bass.IndirectOffsetOnAxis(ap=index[:, e, q:q + 1], axis=0)).then_inc(row_in[q][e], 16)

        @block.vector
        def _(dve):
            link = Link(dve, link_sem)
            dve.sem_inc(y_ready, G)
            dve.sem_inc(o_ready, G)
            dve.memset(eps[:, :], LN_EPS).then_inc(eps_set, 1)
            dve.wait_ge(gamma_in, 16)
            with dve.Fori(0, TURNS) as i:
                link.loop(i, 2)
                w = lambda q, e: s.weight[:, ds(i * G + q, 1), e:e + 1].rearrange("p a e -> p (a e)")

                def second(q):
                    dve.wait_ge(row_in[q][1], 16 * i + 16)
                    dve.wait_ge(first_ready, i * G + q + 1)
                    dve.scalar_tensor_tensor(y[:, q, :], res[:, q, 1, :], w(q, 1), y[:, q, :], ALU.mult, ALU.add).then_inc(y_ready, 1)

                def stats_of(q):
                    dve.wait_ge(y_ready, i * G + q + 1 + G)
                    return dve.bn_stats(stats[:, q, :], y[:, q, :])
                for q in range(G):
                    dve.wait_ge(h_in[0 if q in PARTS[0] else 1], 16 * i + 16)
                    dve.wait_ge(row_in[q][0], 16 * i + 16)
                    dve.scalar_tensor_tensor(y[:, q, :], res[:, q, 0, :], w(q, 0), h[:, q, :], ALU.mult, ALU.add).then_inc(first_ready, 1)
                    if q:
                        stats_of(q - 1)
                    second(q)
                link(stats_of(G - 1))
                dve.memset(spare2[:, :], 0.0)
                for q in range(G):
                    last = dve.bn_aggr(mv[:, q, :], stats[:, q, :])
                last.then_inc(mv_ready, 1)
                dve.wait_ge(std_ready, i + 1)
                link(dve.reciprocal(rstd[:, :], std[:, :]))
                for q in range(G):
                    dve.scalar_tensor_tensor(y[:, q, :], y[:, q, :], mv[:, q, 0:1], scale[:, :], ALU.subtract, ALU.mult).then_inc(scaled, 1)
                dve.wait_ge(x1_in, 16 * i + 16)
                dve.wait_ge(out_out, 16 * i + 16)
                for q in range(G):
                    dve.wait_ge(scaled, i * G + q + 1)
                    dve.scalar_tensor_tensor(o[:, q, :], y[:, q, :], rstd[:, q:q + 1], x1[:, q, :], ALU.mult, ALU.add).then_inc(o_ready, 1)
                dve.wait_ge(o_ready, (i + 2) * G)


def laid_out(x, src, dst, edge_attr_64, L0_gnn_W, L0_gnn_A, L0_mix_kln_weight, L0_mix_kln_bias, L0_mix_vln_weight,
             L0_mix_vln_bias, L0_ffn_gate_w, L0_ffn_gate_b, L0_ffn_w1, L0_ffn_b1, L0_ffn_w2, L0_ffn_b2, L0_ffn_gamma, L0_ffn_beta):
    import numpy as np

    def padded(a, rows, fill=0):
        a = np.asarray(a)
        return np.concatenate([a, np.full((rows - a.shape[0],) + a.shape[1:], fill, a.dtype)])

    named = dict(
        x=padded(x, NP), src=padded(src, EP), dst=padded(dst, EP + 1, N), edge_attr=padded(edge_attr_64, EP), W=L0_gnn_W, A=L0_gnn_A,
        kw=L0_mix_kln_weight, kb=L0_mix_kln_bias, vw=L0_mix_vln_weight, vb=L0_mix_vln_bias,
        gate_w=L0_ffn_gate_w, gate_b=L0_ffn_gate_b, w1=L0_ffn_w1, b1=L0_ffn_b1, w2=L0_ffn_w2, b2=L0_ffn_b2,
        gamma=L0_ffn_gamma, beta=L0_ffn_beta)
    return {f"in_{k}": np.ascontiguousarray(v) for k, v in named.items()}


def kernel(**inputs):
    import numpy as np
    import concourse.bacc as bacc
    from concourse.bass_utils import run_bass_kernel_spmd

    nc = bacc.Bacc("TRN2", target_bir_lowering=False, num_devices=1)
    arrays = laid_out(**inputs)
    args = [nc.dram_tensor(name, a.shape, mybir.dt.from_np(a.dtype), kind="ExternalInput").ap() for name, a in arrays.items()]
    args.append(nc.dram_tensor("out_rows", (NP, D), F32, kind="ExternalOutput").ap())
    build(nc, *args)
    r = run_bass_kernel_spmd(nc, [arrays], core_ids=[0])
    return np.asarray(r.results[0]["out_rows"])[:N]
```
